# Optimizing a Trainium2 kernel written in Bass

```python
import numpy as np
import jax
import jax.numpy as jnp

def _softmax(x, axis=-1):
    return jax.nn.softmax(x, axis=axis)

def _gelu(x):
    return jax.nn.gelu(x, approximate=True)

def _silu(x):
    return jax.nn.silu(x)

def _sigmoid(x):
    return jax.nn.sigmoid(x)

def _layernorm(x, axis=-1, eps=1e-05):
    m = jnp.mean(x, axis=axis, keepdims=True)
    v = jnp.var(x, axis=axis, keepdims=True)
    return (x - m) / jnp.sqrt(v + eps)

def _scatter_add(tgt, idx, src, axis=0):
    return tgt.at[idx].add(src)

def _segment_sum(src, seg, n):
    return jax.ops.segment_sum(src, seg, n)
kernel_name = 'mk_gnn_ffn_d4_gnn_r8_067c78'

def setup_inputs(seed: int=0):
    np.random.seed(seed)
    _w = jnp.asarray

    def _rec_inputs():
        import jax
        import jax.numpy as jnp
        _gk = jax.random.key(seed)
        x = -8.776e-05 + 1 * jax.random.normal(jax.random.fold_in(_gk, 1), (1250, 512), jnp.float32)
        src = jax.random.randint(jax.random.fold_in(_gk, 2), (40000,), 0, 1250, jnp.int32)
        dst = jnp.minimum((1250 * jax.random.uniform(jax.random.fold_in(_gk, 3), (40000,)) ** 2.0).astype(jnp.int32), 9999)
        _o = jnp.argsort(dst, stable=True)
        src = src[_o]
        dst = dst[_o]
        return (x, src, dst)
    x, src, dst = _rec_inputs()

    def _L0_gnn_setup():
        import jax, jax.numpy as jnp
        import numpy as np
        N_NODES = 1250
        N_EDGES = 20000
        D_IN = 512
        D_OUT = 512
        key = jax.random.key(seed)
        k_x, k_e, k_wl, k_wr = jax.random.split(key, 4)
        x = jax.random.normal(k_x, (N_NODES, D_IN), dtype=jnp.float32)
        edge_index = jax.random.randint(k_e, (2, N_EDGES), 0, N_NODES, dtype=jnp.int64)
        scale = 1.0 / np.sqrt(D_IN)
        W_l = jax.random.normal(k_wl, (D_IN, D_OUT), dtype=jnp.float32) * scale
        W_r = jax.random.normal(k_wr, (D_IN, D_OUT), dtype=jnp.float32) * scale
        b = jnp.zeros((D_OUT,), dtype=jnp.float32)
        return {'x': x, 'edge_index': edge_index, 'W_l': W_l, 'W_r': W_r, 'b': b}
    _L0_gnn_all = _L0_gnn_setup()
    _L0_gnn_in = {k: v for k, v in _L0_gnn_all.items() if k in ('W_l', 'W_r', 'b')}
    del _L0_gnn_all

    def _L0_ffn_setup():
        import jax, jax.numpy as jnp
        import numpy as np
        S, B, D, F, E, K = (1024, 2, 512, 256, 8, 2)
        key = jax.random.key(seed)
        ks = jax.random.split(key, 12)
        s = lambda *sh: 1.0 / np.sqrt(sh[0])
        inp = {'x': jax.random.normal(ks[0], (S, B, D), dtype=jnp.float32), 'Wg': jax.random.normal(ks[1], (D, E), dtype=jnp.float32) * s(D), 'bg': jnp.zeros((E,), dtype=jnp.float32), 'W1': jax.random.normal(ks[2], (E, D, F), dtype=jnp.float32) * s(D), 'b1': jnp.zeros((E, F), dtype=jnp.float32), 'W2': jax.random.normal(ks[3], (E, F, D), dtype=jnp.float32) * s(F), 'b2': jnp.zeros((E, D), dtype=jnp.float32), 'Ws1': jax.random.normal(ks[4], (D, F), dtype=jnp.float32) * s(D), 'bs1': jnp.zeros((F,), dtype=jnp.float32), 'Ws2': jax.random.normal(ks[5], (F, D), dtype=jnp.float32) * s(F), 'bs2': jnp.zeros((D,), dtype=jnp.float32)}
        return inp
    _L0_ffn_all = _L0_ffn_setup()
    _L0_ffn_in = {k: v for k, v in _L0_ffn_all.items() if k in ('Wg', 'bg', 'W1', 'b1', 'W2', 'b2', 'Ws1', 'bs1', 'Ws2', 'bs2')}
    del _L0_ffn_all

    def _L1_gnn_setup():
        import jax, jax.numpy as jnp
        import numpy as np
        N = 6250
        DIM = 512
        E = 18750
        key = jax.random.key(seed)
        k_x, k_src, k_dst, k_w, k_b = jax.random.split(key, 5)
        x = jax.random.normal(k_x, (N, DIM), dtype=jnp.float32)
        src = jax.random.randint(k_src, (E,), 0, N)
        dst = jax.random.randint(k_dst, (E,), 0, N)
        edge_index = jnp.stack([src, dst], axis=0)
        bound = 1.0 / np.sqrt(DIM)
        W = jax.random.uniform(k_w, (DIM, DIM), minval=-bound, maxval=bound, dtype=jnp.float32)
        b = jax.random.uniform(k_b, (DIM,), minval=-bound, maxval=bound, dtype=jnp.float32)
        alpha = jnp.float32(0.5)
        return {'x': x, 'edge_index': edge_index, 'num_nodes': N, 'alpha': alpha, 'W': W, 'b': b}
    _L1_gnn_all = _L1_gnn_setup()
    _L1_gnn_in = {k: v for k, v in _L1_gnn_all.items() if k in ('alpha', 'W', 'b')}
    del _L1_gnn_all

    def _L1_ffn_setup():
        import jax, jax.numpy as jnp
        import numpy as np
        SINKHORN_ITERS = 8
        TEMPERATURE = 1.0
        EPS = 1e-10

        def sinkhorn(gates):
            t = jnp.log(jnp.clip(gates, EPS)) / TEMPERATURE

            def body(t, _):
                t = t - jax.nn.logsumexp(t, axis=-2, keepdims=True)
                t = t - jax.nn.logsumexp(t, axis=-1, keepdims=True)
                return (t, None)
            t, _ = jax.lax.scan(body, t, None, length=SINKHORN_ITERS)
            return jnp.exp(t)
        key = jax.random.key(seed)
        k1, k2, k3 = jax.random.split(key, 3)
        b, n, d, e, h = (4, 1024, 512, 8, 1)
        x = jax.random.normal(k1, (b, n, d), dtype=jnp.float32)
        gate_w = jax.random.normal(k2, (h, d, e), dtype=jnp.float32)
        experts = jax.random.normal(k3, (e, d, d), dtype=jnp.float32) / np.sqrt(d)
        return {'x': x, 'gate_w': gate_w, 'experts': experts}
    _L1_ffn_all = _L1_ffn_setup()
    _L1_ffn_in = {k: v for k, v in _L1_ffn_all.items() if k in ('gate_w', 'experts')}
    del _L1_ffn_all

    def _L2_gnn_setup():
        import jax, jax.numpy as jnp
        import numpy as np
        from math import sqrt
        N = 6250
        E = 100000
        D_EMB = 512
        DK = 64
        DV = 64
        HEADS = 8

        def _attention_message(Q, K, V, senders, receivers, n_nodes):
            scale = 1.0 / sqrt(Q.shape[-1])
            scores = jnp.einsum('ehd,ehd->eh', Q[receivers], K[senders]) * scale
            smax = jax.ops.segment_max(scores, receivers, num_segments=n_nodes)
            ex = jnp.exp(scores - smax[receivers])
            denom = jax.ops.segment_sum(ex, receivers, num_segments=n_nodes)
            att = ex / denom[receivers]
            out = jax.ops.segment_sum(att[:, :, None] * V[senders], receivers, num_segments=n_nodes)
            return (out, att)
        key = jax.random.key(seed)
        k1, k2, k3, k4 = jax.random.split(key, 4)
        x = jax.random.normal(k1, (N, D_EMB), dtype=jnp.float32)
        edge_index = jax.random.randint(k2, (2, E), 0, N, dtype=jnp.int64)
        out_qkv = (2 * DK + DV) * HEADS
        W_qkv = jax.random.normal(k3, (out_qkv, D_EMB), dtype=jnp.float32) / sqrt(D_EMB)
        b_qkv = jnp.zeros((out_qkv,), dtype=jnp.float32)
        W_ff = jax.random.normal(k4, (D_EMB, DV * HEADS), dtype=jnp.float32) / sqrt(DV * HEADS)
        b_ff = jnp.zeros((D_EMB,), dtype=jnp.float32)
        return {'x': x, 'edge_index': edge_index, 'W_qkv': W_qkv, 'b_qkv': b_qkv, 'W_ff': W_ff, 'b_ff': b_ff}
    _L2_gnn_all = _L2_gnn_setup()
    _L2_gnn_in = {k: v for k, v in _L2_gnn_all.items() if k in ('W_qkv', 'b_qkv', 'W_ff', 'b_ff')}
    del _L2_gnn_all

    def _L2_ffn_setup():
        import jax, jax.numpy as jnp
        import numpy as np
        B, S, D, F, E = (8, 512, 512, 256, 8)
        INIT_LAMBDA = 0.2
        LN_EPS = 1e-05
        LN_MERGE = 0.03
        key = jax.random.key(seed)
        ks = jax.random.split(key, 12)
        n = lambda k, shp, s=1.0: jax.random.normal(k, shp, dtype=jnp.float32) * s
        return {'hidden_states': n(ks[0], (B, S, D)), 'gfc1_w': n(ks[1], (D, D), 0.01), 'gfc1_b': jnp.zeros((D,), jnp.float32), 'gfc2_w': n(ks[2], (E, D), 0.01), 'gfc2_b': jnp.full((E,), INIT_LAMBDA, dtype=jnp.float32), 'W1': n(ks[3], (F, D), 0.02), 'b1': jnp.zeros((F,), jnp.float32), 'W2': n(ks[4], (D, F), 0.02), 'b2': jnp.zeros((D,), jnp.float32), 'ln_g': jnp.ones((D,), jnp.float32), 'ln_b': jnp.zeros((D,), jnp.float32), 'tv_W1': n(ks[5], (E, F, D), 0.02), 'tv_b1': n(ks[6], (E, F), 0.02), 'tv_W2': n(ks[7], (E, D, F), 0.02), 'tv_b2': n(ks[8], (E, D), 0.02), 'tv_ln_g': n(ks[9], (E, D), 0.02), 'tv_ln_b': n(ks[10], (E, D), 0.02)}
    _L2_ffn_all = _L2_ffn_setup()
    _L2_ffn_in = {k: v for k, v in _L2_ffn_all.items() if k in ('gfc1_w', 'gfc1_b', 'gfc2_w', 'gfc2_b', 'W1', 'b1', 'W2', 'b2', 'ln_g', 'ln_b', 'tv_W1', 'tv_b1', 'tv_W2', 'tv_b2', 'tv_ln_g', 'tv_ln_b')}
    del _L2_ffn_all

    def _L3_gnn_setup():
        import jax, jax.numpy as jnp
        import numpy as np
        N = 6250
        IN_CH = 512
        OUT_CH = 512
        DEG = 32
        E = N * DEG
        key = jax.random.key(seed)
        kx, kwc, kwn, kb, ke = jax.random.split(key, 5)
        x = jax.random.normal(kx, (N, IN_CH), dtype=jnp.float32)
        bound = 1.0 / np.sqrt(IN_CH)
        wc = jax.random.uniform(kwc, (IN_CH, OUT_CH), minval=-bound, maxval=bound, dtype=jnp.float32)
        wn = jax.random.uniform(kwn, (IN_CH, OUT_CH), minval=-bound, maxval=bound, dtype=jnp.float32)
        bias = jax.random.uniform(kb, (OUT_CH,), minval=-bound, maxval=bound, dtype=jnp.float32)
        src = jnp.repeat(jnp.arange(N, dtype=jnp.int64), DEG)
        dst = jax.random.randint(ke, (E,), 0, N, dtype=jnp.int64)
        edge_index = jnp.stack([src, dst], axis=0)
        return {'x': x, 'wc': wc, 'wn': wn, 'bias': bias, 'edge_index': edge_index}
    _L3_gnn_all = _L3_gnn_setup()
    _L3_gnn_in = {k: v for k, v in _L3_gnn_all.items() if k in ('wc', 'wn', 'bias')}
    del _L3_gnn_all

    def _L3_ffn_setup():
        import jax, jax.numpy as jnp
        import numpy as np
        TOP_K = 2

        def quick_gelu(x):
            return x * jax.nn.sigmoid(1.702 * x)
        key = jax.random.key(seed)
        ks = jax.random.split(key, 6)
        B, S, H, I, E = (8, 512, 512, 1024, 8)
        s_h = 1.0 / np.sqrt(H).astype(np.float32)
        s_i = 1.0 / np.sqrt(I).astype(np.float32)
        return {'hidden_states': jax.random.normal(ks[0], (B, S, H), jnp.float32), 'router_w': jax.random.normal(ks[1], (H, E), jnp.float32) * s_h, 'router_b': jnp.zeros((E,), jnp.float32), 'gate_up_proj': jax.random.normal(ks[2], (E, H, 2 * I), jnp.float32) * s_h, 'gate_up_proj_bias': jnp.zeros((E, 2 * I), jnp.float32), 'down_proj': jax.random.normal(ks[3], (E, I, H), jnp.float32) * s_i, 'down_proj_bias': jnp.zeros((E, H), jnp.float32)}
    _L3_ffn_all = _L3_ffn_setup()
    _L3_ffn_in = {k: v for k, v in _L3_ffn_all.items() if k in ('router_w', 'router_b', 'gate_up_proj', 'gate_up_proj_bias', 'down_proj', 'down_proj_bias')}
    del _L3_ffn_all
    return {'x': x, 'src': src, 'dst': dst, 'L0_gnn_W_l': _L0_gnn_in['W_l'], 'L0_gnn_W_r': _L0_gnn_in['W_r'], 'L0_gnn_b': _L0_gnn_in['b'], 'L0_ffn_Wg': _L0_ffn_in['Wg'], 'L0_ffn_bg': _L0_ffn_in['bg'], 'L0_ffn_W1': _L0_ffn_in['W1'], 'L0_ffn_b1': _L0_ffn_in['b1'], 'L0_ffn_W2': _L0_ffn_in['W2'], 'L0_ffn_b2': _L0_ffn_in['b2'], 'L0_ffn_Ws1': _L0_ffn_in['Ws1'], 'L0_ffn_bs1': _L0_ffn_in['bs1'], 'L0_ffn_Ws2': _L0_ffn_in['Ws2'], 'L0_ffn_bs2': _L0_ffn_in['bs2'], 'L1_gnn_alpha': _L1_gnn_in['alpha'], 'L1_gnn_W': _L1_gnn_in['W'], 'L1_gnn_b': _L1_gnn_in['b'], 'L1_ffn_gate_w': _L1_ffn_in['gate_w'], 'L1_ffn_experts': _L1_ffn_in['experts'], 'L2_gnn_W_qkv': _L2_gnn_in['W_qkv'], 'L2_gnn_b_qkv': _L2_gnn_in['b_qkv'], 'L2_gnn_W_ff': _L2_gnn_in['W_ff'], 'L2_gnn_b_ff': _L2_gnn_in['b_ff'], 'L2_ffn_gfc1_w': _L2_ffn_in['gfc1_w'], 'L2_ffn_gfc1_b': _L2_ffn_in['gfc1_b'], 'L2_ffn_gfc2_w': _L2_ffn_in['gfc2_w'], 'L2_ffn_gfc2_b': _L2_ffn_in['gfc2_b'], 'L2_ffn_W1': _L2_ffn_in['W1'], 'L2_ffn_b1': _L2_ffn_in['b1'], 'L2_ffn_W2': _L2_ffn_in['W2'], 'L2_ffn_b2': _L2_ffn_in['b2'], 'L2_ffn_ln_g': _L2_ffn_in['ln_g'], 'L2_ffn_ln_b': _L2_ffn_in['ln_b'], 'L2_ffn_tv_W1': _L2_ffn_in['tv_W1'], 'L2_ffn_tv_b1': _L2_ffn_in['tv_b1'], 'L2_ffn_tv_W2': _L2_ffn_in['tv_W2'], 'L2_ffn_tv_b2': _L2_ffn_in['tv_b2'], 'L2_ffn_tv_ln_g': _L2_ffn_in['tv_ln_g'], 'L2_ffn_tv_ln_b': _L2_ffn_in['tv_ln_b'], 'L3_gnn_wc': _L3_gnn_in['wc'], 'L3_gnn_wn': _L3_gnn_in['wn'], 'L3_gnn_bias': _L3_gnn_in['bias'], 'L3_ffn_router_w': _L3_ffn_in['router_w'], 'L3_ffn_router_b': _L3_ffn_in['router_b'], 'L3_ffn_gate_up_proj': _L3_ffn_in['gate_up_proj'], 'L3_ffn_gate_up_proj_bias': _L3_ffn_in['gate_up_proj_bias'], 'L3_ffn_down_proj': _L3_ffn_in['down_proj'], 'L3_ffn_down_proj_bias': _L3_ffn_in['down_proj_bias']}

def reference(x, src, dst, L0_gnn_W_l, L0_gnn_W_r, L0_gnn_b, L0_ffn_Wg, L0_ffn_bg, L0_ffn_W1, L0_ffn_b1, L0_ffn_W2, L0_ffn_b2, L0_ffn_Ws1, L0_ffn_bs1, L0_ffn_Ws2, L0_ffn_bs2, L1_gnn_alpha, L1_gnn_W, L1_gnn_b, L1_ffn_gate_w, L1_ffn_experts, L2_gnn_W_qkv, L2_gnn_b_qkv, L2_gnn_W_ff, L2_gnn_b_ff, L2_ffn_gfc1_w, L2_ffn_gfc1_b, L2_ffn_gfc2_w, L2_ffn_gfc2_b, L2_ffn_W1, L2_ffn_b1, L2_ffn_W2, L2_ffn_b2, L2_ffn_ln_g, L2_ffn_ln_b, L2_ffn_tv_W1, L2_ffn_tv_b1, L2_ffn_tv_W2, L2_ffn_tv_b2, L2_ffn_tv_ln_g, L2_ffn_tv_ln_b, L3_gnn_wc, L3_gnn_wn, L3_gnn_bias, L3_ffn_router_w, L3_ffn_router_b, L3_ffn_gate_up_proj, L3_ffn_gate_up_proj_bias, L3_ffn_down_proj, L3_ffn_down_proj_bias):
    import jax
    import jax.numpy as jnp

    def _L0_gnn_ref(x, edge_index, W_l, W_r, b):
        import jax, jax.numpy as jnp
        import numpy as np
        N_NODES = 1250
        N_EDGES = 20000
        D_IN = 512
        D_OUT = 512
        src = edge_index[0]
        dst = edge_index[1]
        n = x.shape[0]
        msg = x[src]
        agg = jax.ops.segment_sum(msg, dst, num_segments=n)
        deg = jax.ops.segment_sum(jnp.ones((src.shape[0],), x.dtype), dst, num_segments=n)
        mean = agg / jnp.maximum(deg, 1.0)[:, None]
        h = mean @ W_l + b + x @ W_r
        return h * jax.nn.sigmoid(h)

    def _L0_ffn_ref(x, Wg, bg, W1, b1, W2, b2, Ws1, bs1, Ws2, bs2):
        import jax, jax.numpy as jnp
        import numpy as np
        S, B, D, F, E, K = (1024, 2, 512, 256, 8, 2)
        gate_logits = jnp.einsum('sbd,de->sbe', x, Wg) + bg
        weights, selected = jax.lax.top_k(gate_logits, K)
        weights = jax.nn.softmax(weights.astype(jnp.float32), axis=-1)
        onehot = jax.nn.one_hot(selected, E, dtype=weights.dtype)
        comb = jnp.einsum('sbk,sbke->sbe', weights, onehot)
        h = jax.nn.relu(jnp.einsum('sbd,edf->sbef', x, W1) + b1)
        y = jnp.einsum('sbef,efd->sbed', h, W2) + b2
        out = jnp.einsum('sbe,sbed->sbd', comb, y)
        hs = jax.nn.relu(jnp.einsum('sbd,df->sbf', x, Ws1) + bs1)
        shared = jnp.einsum('sbf,fd->sbd', hs, Ws2) + bs2
        out = out + 1.0 / K * shared
        return out

    def _L1_gnn_ref(x, edge_index, num_nodes, alpha, W, b):
        import jax, jax.numpy as jnp
        import numpy as np
        N = 6250
        DIM = 512
        E = 18750
        src = edge_index[0]
        dst = edge_index[1]
        agg = jax.ops.segment_sum(x[src], dst, num_segments=num_nodes)
        deg = jax.ops.segment_sum(jnp.ones_like(dst, dtype=x.dtype), dst, num_segments=num_nodes)
        deg = jnp.maximum(deg, 1.0)
        agg = agg / deg[:, None]
        return x + alpha * (agg @ W.T + b)

    def _L1_ffn_ref(x, gate_w, experts):
        import jax, jax.numpy as jnp
        import numpy as np
        SINKHORN_ITERS = 8
        TEMPERATURE = 1.0
        EPS = 1e-10

        def sinkhorn(gates):
            t = jnp.log(jnp.clip(gates, EPS)) / TEMPERATURE

            def body(t, _):
                t = t - jax.nn.logsumexp(t, axis=-2, keepdims=True)
                t = t - jax.nn.logsumexp(t, axis=-1, keepdims=True)
                return (t, None)
            t, _ = jax.lax.scan(body, t, None, length=SINKHORN_ITERS)
            return jnp.exp(t)
        b, n, d = x.shape
        h = gate_w.shape[0]
        e = experts.shape[0]
        N = b * n
        m = n // e
        x4 = x[:, None]
        gates = jnp.einsum('bhnd,hde->bhne', x4, gate_w)
        xf = jnp.transpose(x4, (1, 0, 2, 3)).reshape(h, N, d)
        gf = jnp.transpose(gates, (1, 0, 2, 3)).reshape(h, N, e)
        cg = sinkhorn(gf)
        vals, idx = jax.lax.top_k(jnp.transpose(cg, (0, 2, 1)), m)
        gate_values = (vals > 0.5).astype(x.dtype)
        gate_values = jnp.transpose(gate_values, (0, 2, 1))
        idx = jnp.transpose(idx, (0, 2, 1))
        routed = xf[jnp.arange(h)[:, None, None], idx]
        outputs = jnp.einsum('hmei,eio->hmeo', routed, experts)
        outputs = outputs * gate_values[..., None]
        o_dim = outputs.shape[-1]
        src = outputs.reshape(h, m * e, o_dim)
        idx_flat = idx.reshape(h, m * e)

        def combine(idxf, srcf):
            s = jnp.zeros((N, o_dim), srcf.dtype).at[idxf].add(srcf)
            c = jnp.zeros((N,), srcf.dtype).at[idxf].add(1.0)
            return s / (c + 1.0)[:, None]
        out = jax.vmap(combine)(idx_flat, src)
        out = out.reshape(h, b, n, o_dim)
        out = jnp.transpose(out, (1, 0, 2, 3))[:, 0]
        return out

    def _L2_gnn_ref(x, edge_index, W_qkv, b_qkv, W_ff, b_ff):
        import jax, jax.numpy as jnp
        import numpy as np
        from math import sqrt
        N = 6250
        E = 100000
        D_EMB = 512
        DK = 64
        DV = 64
        HEADS = 8

        def _attention_message(Q, K, V, senders, receivers, n_nodes):
            scale = 1.0 / sqrt(Q.shape[-1])
            scores = jnp.einsum('ehd,ehd->eh', Q[receivers], K[senders]) * scale
            smax = jax.ops.segment_max(scores, receivers, num_segments=n_nodes)
            ex = jnp.exp(scores - smax[receivers])
            denom = jax.ops.segment_sum(ex, receivers, num_segments=n_nodes)
            att = ex / denom[receivers]
            out = jax.ops.segment_sum(att[:, :, None] * V[senders], receivers, num_segments=n_nodes)
            return (out, att)
        n_nodes = x.shape[0]
        qkv = x @ W_qkv.T + b_qkv
        Q, K, V = jnp.split(qkv, [DK * HEADS, 2 * DK * HEADS], axis=-1)
        Q = Q.reshape(n_nodes, HEADS, DK)
        K = K.reshape(n_nodes, HEADS, DK)
        V = V.reshape(n_nodes, HEADS, DV)
        senders, receivers = (edge_index[0], edge_index[1])
        msg, _ = _attention_message(Q, K, V, senders, receivers, n_nodes)
        out = msg.reshape(n_nodes, HEADS * DV) @ W_ff.T + b_ff
        return out

    def _L2_ffn_ref(hidden_states, gfc1_w, gfc1_b, gfc2_w, gfc2_b, W1, b1, W2, b2, ln_g, ln_b, tv_W1, tv_b1, tv_W2, tv_b2, tv_ln_g, tv_ln_b):
        import jax, jax.numpy as jnp
        import numpy as np
        B, S, D, F, E = (8, 512, 512, 256, 8)
        INIT_LAMBDA = 0.2
        LN_EPS = 1e-05
        LN_MERGE = 0.03
        x = hidden_states
        gh = jax.nn.relu(jnp.einsum('bsd,hd->bsh', x, gfc1_w) + gfc1_b)
        g = (jnp.einsum('bsh,eh->bse', gh, gfc2_w) + gfc2_b).mean(axis=1)
        W1m = W1 + jnp.einsum('be,efd->bfd', g, tv_W1)
        b1m = b1 + g @ tv_b1
        W2m = W2 + jnp.einsum('be,edf->bdf', g, tv_W2)
        b2m = b2 + g @ tv_b2
        lng = ln_g + LN_MERGE * (tv_ln_g - ln_g).sum(axis=0)
        lnb = ln_b + LN_MERGE * (tv_ln_b - ln_b).sum(axis=0)
        h = jax.nn.relu(jnp.einsum('bsd,bfd->bsf', x, W1m) + b1m[:, None, :])
        out = jnp.einsum('bsf,bdf->bsd', h, W2m) + b2m[:, None, :]
        res = x + out
        mu = res.mean(axis=-1, keepdims=True)
        var = res.var(axis=-1, keepdims=True)
        return (res - mu) * jax.lax.rsqrt(var + LN_EPS) * lng + lnb

    def _L3_gnn_ref(x, wc, wn, bias, edge_index):
        import jax, jax.numpy as jnp
        import numpy as np
        N = 6250
        IN_CH = 512
        OUT_CH = 512
        DEG = 32
        E = N * DEG
        alpha = x @ wc
        beta = x @ wn
        src, dst = (edge_index[0], edge_index[1])
        sums = jax.ops.segment_sum(beta[dst], src, num_segments=x.shape[0])
        counts = jax.ops.segment_sum(jnp.ones_like(src, dtype=beta.dtype), src, num_segments=x.shape[0])
        gamma = sums / counts[:, None]
        return alpha + gamma + bias

    def _L3_ffn_ref(hidden_states, router_w, router_b, gate_up_proj, gate_up_proj_bias, down_proj, down_proj_bias):
        import jax, jax.numpy as jnp
        import numpy as np
        TOP_K = 2

        def quick_gelu(x):
            return x * jax.nn.sigmoid(1.702 * x)
        B, S, H = hidden_states.shape
        E = router_b.shape[0]
        x = hidden_states.reshape(-1, H)
        T = x.shape[0]
        logits = x @ router_w + router_b
        top_w, sel = jax.lax.top_k(logits, TOP_K)
        top_w = jax.nn.softmax(top_w, axis=-1)
        tok_w = jnp.zeros((T, E), x.dtype).at[jnp.arange(T)[:, None], sel].add(top_w)

        def body(acc, params):
            Wgu, bgu, Wd, bd, w_e = params
            gu = x @ Wgu + bgu
            gate, up = jnp.split(gu, 2, axis=-1)
            act = (up + 1.0) * quick_gelu(gate)
            out = act @ Wd + bd
            return (acc + out * w_e[:, None], None)
        acc0 = jnp.zeros((T, H), x.dtype)
        acc, _ = jax.lax.scan(body, acc0, (gate_up_proj, gate_up_proj_bias, down_proj, down_proj_bias, tok_w.T))
        return acc.reshape(B, S, H)
    edge_index = jnp.stack([src, dst])
    x = x + _L0_gnn_ref(_layernorm(x, axis=-1), edge_index, L0_gnn_W_l, L0_gnn_W_r, L0_gnn_b)
    x = x + _L0_ffn_ref(_layernorm(x, axis=-1)[None], L0_ffn_Wg, L0_ffn_bg, L0_ffn_W1, L0_ffn_b1, L0_ffn_W2, L0_ffn_b2, L0_ffn_Ws1, L0_ffn_bs1, L0_ffn_Ws2, L0_ffn_bs2)[0]
    x = x + _L1_gnn_ref(_layernorm(x, axis=-1), edge_index, 1250, L1_gnn_alpha, L1_gnn_W, L1_gnn_b)
    x = x + _L1_ffn_ref(_layernorm(x, axis=-1)[None], L1_ffn_gate_w, L1_ffn_experts)[0]
    x = x + _L2_gnn_ref(_layernorm(x, axis=-1), edge_index, L2_gnn_W_qkv, L2_gnn_b_qkv, L2_gnn_W_ff, L2_gnn_b_ff)
    x = x + _L2_ffn_ref(_layernorm(x, axis=-1)[None], L2_ffn_gfc1_w, L2_ffn_gfc1_b, L2_ffn_gfc2_w, L2_ffn_gfc2_b, L2_ffn_W1, L2_ffn_b1, L2_ffn_W2, L2_ffn_b2, L2_ffn_ln_g, L2_ffn_ln_b, L2_ffn_tv_W1, L2_ffn_tv_b1, L2_ffn_tv_W2, L2_ffn_tv_b2, L2_ffn_tv_ln_g, L2_ffn_tv_ln_b)[0]
    x = x + _L3_gnn_ref(_layernorm(x, axis=-1), L3_gnn_wc, L3_gnn_wn, L3_gnn_bias, edge_index)
    x = x + _L3_ffn_ref(_layernorm(x, axis=-1)[None], L3_ffn_router_w, L3_ffn_router_b, L3_ffn_gate_up_proj, L3_ffn_gate_up_proj_bias, L3_ffn_down_proj, L3_ffn_down_proj_bias)[0]
    return x

_drawn_inputs = setup_inputs


def setup_inputs(seed=0):
    import zlib

    import numpy as np

    out = dict(_drawn_inputs(seed))
    spreads = {'L0_gnn_b': (0.0, 0.1),
     'L0_ffn_bg': (0.0, 0.1),
     'L0_ffn_b1': (0.0, 0.1),
     'L0_ffn_b2': (0.0, 0.1),
     'L0_ffn_bs1': (0.0, 0.1),
     'L0_ffn_bs2': (0.0, 0.1),
     'L2_gnn_b_qkv': (0.0, 0.1),
     'L2_gnn_b_ff': (0.0, 0.1),
     'L2_ffn_gfc1_b': (0.0, 0.8),
     'L2_ffn_gfc2_b': (0.20000000298023224, 0.6),
     'L2_ffn_b1': (0.0, 0.421),
     'L2_ffn_b2': (0.0, 0.1),
     'L2_ffn_ln_g': (1.0, 0.2),
     'L2_ffn_ln_b': (0.0, 0.1),
     'L3_ffn_router_b': (0.0, 0.1),
     'L3_ffn_gate_up_proj_bias': (0.0, 0.31),
     'L3_ffn_down_proj_bias': (0.0, 0.353)}
    factors = {'L1_gnn_b': 3.127,
     'L2_ffn_gfc1_w': 8.0,
     'L2_ffn_gfc2_w': 8.0,
     'L2_ffn_tv_b1': 8.0,
     'L2_ffn_tv_b2': 6.009,
     'L2_ffn_tv_ln_g': 37.443,
     'L2_ffn_tv_ln_b': 28.47,
     'L3_gnn_bias': 3.956}
    for name, (base, spread) in spreads.items():
        noise = np.random.default_rng([zlib.crc32(name.encode()), seed]).standard_normal(out[name].shape)
        drawn = base * np.exp(spread * noise) if base else spread * noise
        out[name] = jnp.asarray(drawn.astype(out[name].dtype))
    for name, factor in factors.items():
        out[name] = (out[name] * factor).astype(out[name].dtype)
    return out
```

```python
import numpy as np
import concourse.bass as bass
from concourse import mybir
from concourse.alu_op_type import AluOpType as ALU
from contextlib import ExitStack

F32, F16, I32 = mybir.dt.float32, mybir.dt.float16, mybir.dt.int32
ACT = mybir.ActivationFunctionType
AX = mybir.AxisListType

N, D, E = 1250, 512, 8
P, NT = 125, 10
KD = D // 128
EDGES = 40000
G, J = 40, 8
CHUNKS = [(0, 512), (512, 512), (1024, N - 1024)]
BIG = 1.0e30


class Kernel:

    def __init__(self, nc, dram):
        self.nc, self.d, self.ctx = nc, dram, ExitStack()

    def sb(self, name, shape, dt=F32, ctx=None):
        return (ctx or self.ctx).enter_context(self.nc.sbuf_tensor(name, shape, dt))

    def ps(self, name, shape, ctx):
        return ctx.enter_context(self.nc.psum_tensor(name, shape, F32))

    def sem(self, name):
        return self.ctx.enter_context(self.nc.semaphore(name))


def build_adjacency(k):
    nc, d = k.nc, k.d
    with ExitStack() as ctx:
        edges_i = k.sb("edges_i", [G, 2, P * J], I32, ctx)
        edges_f = k.sb("edges_f", [G, 2, P * J], F32, ctx)
        ends = k.sb("ends", [G, 2], F32, ctx)
        tiles = k.sb("tiles", [G, 2], F32, ctx)
        bounds = k.sb("bounds", [1, 2, G], I32, ctx)
        node = k.sb("node", [P, 2, J, G + 1], F32, ctx)
        iota = k.sb("iota", [P, N], F16, ctx)
        hot_src = k.sb("hot_src", [P, 2, J, N], F16, ctx)
        hot_dst = k.sb("hot_dst", [P, 4, J, P], F16, ctx)
        off_dst = k.sb("off_dst", [P, 4, J, P], F16, ctx)
        far_dst = k.sb("far_dst", [P, J, P], F16, ctx)
        one = k.sb("one", [P, 1], F32, ctx)
        dst_off = k.sem("dst_off")
        ps_node = k.ps("ps_node", [P, 2, 512], ctx)
        acc = k.ps("acc", [P, 2, 3 * 512], ctx)
        edges_in, x_in, ident_ok, iota_ok = k.sem("edges_in"), k.x_in, k.ident_ok, k.sem("iota_ok")
        edges_ok, node_ps, node_ok, tiles_ok = k.sem("edges_ok"), k.sem("node_ps"), k.sem("node_ok"), k.sem("tiles_ok")
        bounds_ps, bounds_ok, adj_zero = k.sem("bounds_ps"), k.sem("bounds_ok"), k.sem("adj_zero")
        src_hot, dst_hot, group_done = k.sem("src_hot"), k.sem("dst_hot"), k.sem("group_done")
        acc_free, acc_ok = k.sem("acc_free"), k.sem("acc_ok")
        block = ctx.enter_context(nc.Block())

        @block.sync
        def _(sp):
            sp.dma_start(edges_i[:, 0, :], d["dst"].rearrange("(g e) -> g e", g=G)).then_inc(edges_in, 16)
            sp.dma_start(edges_i[:, 1, :], d["src"].rearrange("(g e) -> g e", g=G)).then_inc(edges_in, 16)
            sp.dma_start(k.x[:], d["x"].rearrange("(t p) d -> p t d", p=P)).then_inc(x_in, 16)

        @block.gpsimd
        def _(pool):
            nc.gpsimd.memset(k.ident[:], 0.0)
            pool.drain()
            nc.gpsimd.affine_select(out=k.ident[:], in_=k.ident[:], compare_op=ALU.not_equal, fill=1.0, base=0,
                                    pattern=[[-1, 128]], channel_multiplier=1).then_inc(ident_ok, 1)
            nc.gpsimd.memset(one[:], 1.0).then_inc(iota_ok, 1)
            nc.gpsimd.iota(iota[:], pattern=[[1, N]], base=0, channel_multiplier=0,
                           allow_small_or_imprecise_dtypes=True).then_inc(iota_ok, 1)
            nc.gpsimd.memset(node[:, :, :, G:G + 1], 0.0).then_inc(iota_ok, 1)
            nc.gpsimd.memset(k.adj[:], 0.0).then_inc(adj_zero, 1)
            pool.wait_ge(node_ok, 1)
            pool.wait_ge(bounds_ok, 1)
            pool.drain()
            item = pool.alloc_register("item_pool")
            pool.reg_mov(item, 0)
            with pool.Fori(0, G) as g:
                first = pool.value_load(bounds[0:1, 0, bass.ds(g, 1)], min_val=0, max_val=NT - 1)
                end = pool.value_load(bounds[0:1, 1, bass.ds(g, 1)], min_val=1, max_val=NT)
                with pool.Fori(first, end) as t:
                    i = pool.snap(item, min_val=0, max_val=G * NT)
                    slot = pool.snap(i % 4)
                    pool.wait_ge(acc_ok, i + 1)
                    nc.gpsimd.tensor_tensor(off_dst[:, bass.ds(slot, 1), :, :].rearrange("p a j n -> p (a j) n"),
                                            iota[:, bass.ds(t * P, P)].unsqueeze(1).broadcast_to([P, J, P]),
                                            node[:, 0, :, bass.ds(g, 1)].broadcast_to([P, J, P]),
                                            ALU.subtract).then_inc(dst_off, 1)
                    pool.reg_add(item, item, 1)

        @block.scalar
        def _(act):
            act.wait_ge(iota_ok, 3)
            act.wait_ge(bounds_ok, 1)
            item = act.alloc_register("item_act")
            act.reg_mov(item, 0)
            with act.Fori(0, G) as g:
                first = act.value_load(bounds[0:1, 0, bass.ds(g, 1)], min_val=0, max_val=NT - 1)
                end = act.value_load(bounds[0:1, 1, bass.ds(g, 1)], min_val=1, max_val=NT)
                with act.Fori(first, end) as t:
                    i = act.snap(item, min_val=0, max_val=G * NT)
                    slot = act.snap(i % 4)
                    act.drain()
                    act.wait_ge(dst_off, i + 1)
                    act.reg_add(item, item, 1)
                    nc.scalar.activation(far_dst[:], off_dst[:, bass.ds(slot, 1), :, :], ACT.Abs)
                    act.drain()
                    nc.scalar.activation(hot_dst[:, bass.ds(slot, 1), :, :], far_dst[:], ACT.Relu,
                                         scale=-1.0, bias=one[:]).then_inc(dst_hot, 1)

        @block.tensor
        def _(pe):
            pe.wait_ge(ident_ok, 1)
            pe.wait_ge(edges_ok, 1)
            for w in range(2):
                v = edges_f[:, w, :].rearrange("g (p j) -> g j p", j=J)
                for j in range(J):
                    last = nc.tensor.transpose(ps_node[:, w, j * G:(j + 1) * G], v[:, j, :], k.ident[0:G, 0:G])
            last.then_inc(node_ps, 1)
            pe.wait_ge(tiles_ok, 1)
            pe.wait_ge(node_ok, 1)
            for w in range(2):
                last = nc.tensor.transpose(ps_node[0:1, w, 0:G], tiles[:, w:w + 1], k.ident[0:G, 0:G])
            last.then_inc(bounds_ps, 1)
            pe.wait_ge(bounds_ok, 1)
            item = pe.alloc_register("item_pe")
            pe.reg_mov(item, 0)
            with pe.Fori(0, G // 2) as gg:
                for u in range(2):
                    g = gg * 2 + u
                    first = pe.value_load(bounds[0:1, 0, bass.ds(g, 1)], min_val=0, max_val=NT - 1)
                    end = pe.value_load(bounds[0:1, 1, bass.ds(g, 1)], min_val=1, max_val=NT)
                    with pe.Fori(first, end) as t:
                        i = pe.snap(item, min_val=0, max_val=G * NT)
                        half = pe.snap(i % 2)
                        slot = pe.snap(i % 4)
                        pe.wait_ge(acc_free, i + 1)
                        pe.wait_ge(src_hot, g + 1)
                        pe.wait_ge(dst_hot, i + 1)
                        pe.reg_add(item, item, 1)
                        for j in range(J):
                            for c0, cn in CHUNKS:
                                last = nc.tensor.matmul(acc[:, bass.ds(half, 1), c0:c0 + cn],
                                                        hot_dst[:, bass.ds(slot, 1), j, :],
                                                        hot_src[:, u, j, c0:c0 + cn],
                                                        start=(j == 0), stop=(j == J - 1))
                        last.then_inc(acc_ok, 1)
                    pe.drain().then_inc(group_done, 1)

        @block.vector
        def _(dve):
            dve.wait_ge(edges_in, 32)
            nc.vector.tensor_copy(edges_f[:], edges_i[:]).then_inc(edges_ok, 1)
            dve.drain()
            nc.vector.tensor_reduce(ends[:, 0:1], edges_f[:, 0, :], AX.X, ALU.min)
            nc.vector.tensor_reduce(ends[:, 1:2], edges_f[:, 0, :], AX.X, ALU.max)
            dve.drain()
            nc.vector.tensor_scalar(tiles[:, 0:1], ends[:, 0:1], float(P), None, ALU.is_ge)
            nc.vector.tensor_scalar(tiles[:, 1:2], ends[:, 1:2], float(P), 1.0, ALU.is_ge, ALU.add)
            for t in range(2, NT):
                dve.drain()
                last = nc.vector.scalar_tensor_tensor(out=tiles[:], in0=ends[:], scalar=float(P * t), in1=tiles[:],
                                                      op0=ALU.is_ge, op1=ALU.add)
            last.then_inc(tiles_ok, 1)
            dve.wait_ge(node_ps, 1)
            nc.vector.tensor_copy(node[:, :, :, 0:G],
                                  ps_node[:, :, 0:J * G].rearrange("p w (j g) -> p w j g", j=J)).then_inc(node_ok, 1)
            dve.wait_ge(bounds_ps, 1)
            nc.vector.tensor_copy(bounds[:], ps_node[0:1, :, 0:G]).then_inc(bounds_ok, 1)
            dve.sem_inc(acc_free, 2)
            dve.sem_inc(acc_ok, 4)
            dve.sem_inc(group_done, 1)
            dve.wait_ge(iota_ok, 3)
            dve.drain()

            def one_hots(g, buf):
                for j in range(J):
                    last = nc.vector.tensor_scalar(hot_src[:, buf, j, :], iota[:], node[:, 1, j, bass.ds(g, 1)],
                                                   None, ALU.is_equal)
                last.then_inc(src_hot, 1)

            one_hots(0, 0)
            dve.wait_ge(adj_zero, 1)
            item = dve.alloc_register("item_dve")
            dve.reg_mov(item, 0)
            with dve.Fori(0, G // 2) as gg:
                for u in range(2):
                    g = gg * 2 + u
                    dve.wait_ge(group_done, g + 1)
                    one_hots(g + 1, 1 - u)
                    first = dve.value_load(bounds[0:1, 0, bass.ds(g, 1)], min_val=0, max_val=NT - 1)
                    end = dve.value_load(bounds[0:1, 1, bass.ds(g, 1)], min_val=1, max_val=NT)
                    with dve.Fori(first, end) as t:
                        i = dve.snap(item, min_val=0, max_val=G * NT)
                        half = dve.snap(i % 2)
                        dve.wait_ge(acc_ok, i + 5)
                        nc.vector.tensor_tensor(k.adj[:, bass.ds(t, 1), :], k.adj[:, bass.ds(t, 1), :],
                                                acc[:, bass.ds(half, 1), 0:N], ALU.add).then_inc(acc_free, 1)
                        dve.reg_add(item, item, 1)
                        dve.drain()



def tile_cols(t):
    return slice(t * P, (t + 1) * P)


class Norm:

    def __init__(self, k, name, ctx):
        self.k = k
        self.stats = k.sb(f"{name}_stats", [P, NT, 6], F32, ctx)
        self.mean_var = k.sb(f"{name}_mean_var", [P, NT, 2], F32, ctx)
        self.var = k.sb(f"{name}_var", [P, NT, 1], F32, ctx)
        self.std = k.sb(f"{name}_std", [P, NT, 1], F32, ctx)
        self.rstd = k.sb(f"{name}_rstd", [P, NT, 1], F32, ctx)
        self.var_ok, self.std_ok, self.y_ok, self.yT_ps, self.yT_ok = k.norm_sems
        self.layer, self.base = k.norms, k.norms * NT
        k.norms += 1

    def vector(self, dve):
        nc, k = self.k.nc, self.k
        with dve.Fori(0, NT) as t:
            nc.vector.bn_stats(self.stats[:, bass.ds(t, 1), :], k.x[:, bass.ds(t, 1), :])
        dve.drain()
        for t in range(NT):
            nc.vector.bn_aggr(self.mean_var[:, t, :], self.stats[:, t, :])
        dve.drain()
        nc.vector.tensor_scalar(self.var[:], self.mean_var[:, :, 1:2], 1e-5, None, ALU.add).then_inc(self.var_ok, 1)
        dve.wait_ge(self.std_ok, self.layer + 1)
        nc.vector.reciprocal(self.rstd[:], self.std[:])
        dve.drain()
        with dve.Fori(0, NT) as t:
            nc.vector.tensor_scalar(k.y[:, bass.ds(t, 1), :], k.x[:, bass.ds(t, 1), :],
                                    self.mean_var[:, bass.ds(t, 1), 0], self.rstd[:, bass.ds(t, 1), 0],
                                    ALU.subtract, ALU.mult).then_inc(self.y_ok, 1)
        dve.drain()

    def scalar(self, act):
        nc, k = self.k.nc, self.k
        act.wait_ge(self.var_ok, self.layer + 1)
        nc.scalar.activation(self.std[:], self.var[:], ACT.Sqrt).then_inc(self.std_ok, 1)
        for t in range(NT):
            act.wait_ge(self.yT_ps, self.base + t + 1)
            nc.scalar.copy(k.yT[:, :, tile_cols(t)],
                           k.bank[:, 6 + t % 2, 0:KD * P].rearrange("p (f n) -> p f n", f=KD)).then_inc(self.yT_ok, 1)

    def tensor(self, pe):
        nc, k = self.k.nc, self.k
        for t in range(NT):
            pe.wait_ge(self.y_ok, self.base + t + 1)
            if t >= 2:
                pe.wait_ge(self.yT_ok, self.base + t - 1)
            for f in range(KD):
                last = nc.tensor.transpose(k.bank[:, 6 + t % 2, f * P:(f + 1) * P],
                                           k.y[:, t, f * 128:(f + 1) * 128], k.ident[0:P, 0:P])
            last.then_inc(self.yT_ps, 1)


def graph_layer(k, name, kind):
    nc, d = k.nc, k.d
    first = kind == "sage"
    with ExitStack() as ctx:
        norm = Norm(k, name, ctx)
        w_agg = k.sb(f"{name}_w_agg", [128, KD, D], F32, ctx)
        w_self = k.sb(f"{name}_w_self", [128, KD, D], F32, ctx) if kind != "residual" else None
        bias = k.sb(f"{name}_bias", [P, D], F32, ctx)
        alpha = k.sb(f"{name}_alpha", [P, 1], F32, ctx)
        h = k.sb(f"{name}_h", [P, D], F32, ctx)
        gate = k.sb(f"{name}_gate", [P, 2, D], F32, ctx)
        own = k.sb(f"{name}_own", [P, 2, D], F32, ctx)
        w_in, adjT_ps, adjT_ok = k.sem(f"{name}_w_in"), k.sem(f"{name}_adjT_ps"), k.sem(f"{name}_adjT_ok")
        z_ps, z_ok = k.sem(f"{name}_z_ps"), k.sem(f"{name}_z_ok")
        own_ps, own_ok, pre_ok = k.sem(f"{name}_own_ps"), k.sem(f"{name}_own_ok"), k.sem(f"{name}_pre_ok")
        sum_ps, h_ok, gate_ok = k.sem(f"{name}_sum_ps"), k.sem(f"{name}_h_ok"), k.sem(f"{name}_gate_ok")
        done = k.sem(f"{name}_done")
        weights = {"sage": ("L0_gnn_W_l", "L0_gnn_W_r", "L0_gnn_b"), "residual": ("L1_gnn_W_T", None, "L1_gnn_b"),
                   "sum": ("L3_gnn_wn", "L3_gnn_wc", "L3_gnn_bias")}[kind]
        by_edge = k.adj if kind == "sum" else k.adjT
        scale = k.inv_out if kind == "sum" else k.inv_in
        block = ctx.enter_context(nc.Block())

        @block.sync
        def _(sp):
            if kind == "sum":
                sp.dma_start(k.adj[:], k.adj_saved).then_inc(k.adj_in, 16)
            sp.dma_start(w_agg[:], d[weights[0]].rearrange("(f p) n -> p f n", p=128)).then_inc(w_in, 16)
            if w_self is not None:
                sp.dma_start(w_self[:], d[weights[1]].rearrange("(f p) n -> p f n", p=128)).then_inc(w_in, 16)
            else:
                sp.dma_start(alpha[:], d["L1_gnn_alpha"].partition_broadcast(P)).then_inc(w_in, 16)
            sp.dma_start(bias[:], d[weights[2]].partition_broadcast(P)).then_inc(w_in, 16)

        @block.tensor
        def _(pe):
            if first:
                for s in range(NT):
                    if s >= 2:
                        pe.wait_ge(adjT_ok, s - 1)
                    for t in range(NT):
                        last = nc.tensor.transpose(
                            k.bank[0:P, 3 * (s % 2) + t // 4, (t % 4) * P:(t % 4 + 1) * P],
                            k.adj[:, t, tile_cols(s)], k.ident[0:P, 0:P])
                    last.then_inc(adjT_ps, 1)
            norm.tensor(pe)
            pe.wait_ge(w_in, 48)
            if first:
                pe.wait_ge(adjT_ok, NT)
            for t in range(NT):
                pe.wait_ge(norm.yT_ok, norm.base + t + 1)
                if t >= 2:
                    pe.wait_ge(z_ok, t - 1)
                for f in range(KD):
                    last = nc.tensor.matmul(k.bank[0:P, t % 2, :], k.yT[:, f, tile_cols(t)], w_agg[:, f, :],
                                            start=(f == 0), stop=(f == KD - 1))
                last.then_inc(z_ps, 1)
            for t in range(NT):
                if w_self is not None:
                    if t >= 2:
                        pe.wait_ge(own_ok, t - 1)
                    for f in range(KD):
                        last = nc.tensor.matmul(k.bank[0:P, 4 + t % 2, :], k.yT[:, f, tile_cols(t)], w_self[:, f, :],
                                                start=(f == 0), stop=(f == KD - 1))
                    last.then_inc(own_ps, 1)
                pe.wait_ge(z_ok, NT)
                if kind == "sum" and t == 0:
                    pe.wait_ge(k.adj_in, 16)
                if t >= 2:
                    pe.wait_ge(h_ok, t - 1)
                for s in range(NT):
                    last = nc.tensor.matmul(k.bank[0:P, 2 + t % 2, :], by_edge[:, s, tile_cols(t)], k.z[0:P, s, :],
                                            start=(s == 0), stop=(s == NT - 1))
                last.then_inc(sum_ps, 1)

        @block.scalar
        def _(act):
            if first:
                for s in range(NT):
                    act.wait_ge(adjT_ps, s + 1)
                    b = 3 * (s % 2)
                    nc.scalar.copy(k.adjT[:, s, 0:8 * P].rearrange("p (b n) -> p b n", b=2),
                                   k.bank[0:P, b:b + 2, 0:4 * P])
                    nc.scalar.copy(k.adjT[:, s, 8 * P:N], k.bank[0:P, b + 2, 0:2 * P]).then_inc(adjT_ok, 1)
            norm.scalar(act)
            for t in range(NT):
                act.wait_ge(z_ps, t + 1)
                nc.scalar.copy(k.z[0:P, t, :], k.bank[0:P, t % 2, :]).then_inc(z_ok, 1)
            for t in range(NT):
                if w_self is not None:
                    act.wait_ge(own_ps, t + 1)
                    if t >= 2:
                        act.wait_ge(pre_ok, t - 1)
                    nc.scalar.copy(own[:, t % 2, :], k.bank[0:P, 4 + t % 2, :]).then_inc(own_ok, 1)
                if kind == "sage":
                    act.wait_ge(pre_ok, t + 1)
                    nc.scalar.activation(gate[:, t % 2, :], h[:], ACT.Sigmoid).then_inc(gate_ok, 1)

        @block.vector
        def _(dve):
            if first:
                dve.wait_ge(k.x_in, 16)
            norm.vector(dve)
            dve.wait_ge(w_in, 48)
            if first:
                nc.vector.tensor_reduce(k.degree[:, :, 0], k.adj[:], AX.X, ALU.add)
                dve.wait_ge(adjT_ok, NT)
                nc.vector.tensor_reduce(k.degree[:, :, 1], k.adjT[:], AX.X, ALU.add)
                dve.drain()
                nc.vector.tensor_scalar(k.inv_in[:], k.degree[:, :, 0:1], 1.0, None, ALU.max)
                nc.vector.reciprocal(k.inv_out[:], k.degree[:, :, 1:2])
                nc.vector.tensor_scalar(k.has_in[:], k.degree[:, :, 0:1], 0.0, None, ALU.is_gt)
                dve.drain()
                nc.vector.reciprocal(k.inv_in[:], k.inv_in[:])
                dve.drain()
            for t in range(NT):
                dve.wait_ge(sum_ps, t + 1)
                if w_self is not None:
                    dve.wait_ge(own_ok, t + 1)
                    nc.vector.scalar_tensor_tensor(out=h[:], in0=k.bank[0:P, 2 + t % 2, :], scalar=scale[:, t, :],
                                                   in1=own[:, t % 2, :], op0=ALU.mult, op1=ALU.add).then_inc(h_ok, 1)
                    dve.wait_ge(h_ok, t + 1)
                    nc.vector.tensor_tensor(h[:], h[:], bias[:], ALU.add).then_inc(pre_ok, 1)
                    dve.wait_ge(pre_ok, t + 1)
                    if kind == "sage":
                        dve.wait_ge(gate_ok, t + 1)
                        nc.vector.tensor_tensor(h[:], h[:], gate[:, t % 2, :], ALU.mult)
                        dve.drain()
                else:
                    nc.vector.scalar_tensor_tensor(out=h[:], in0=k.bank[0:P, 2 + t % 2, :], scalar=scale[:, t, :],
                                                   in1=bias[:], op0=ALU.mult, op1=ALU.add).then_inc(h_ok, 1)
                    dve.wait_ge(h_ok, t + 1)
                    nc.vector.scalar_tensor_tensor(out=h[:], in0=h[:], scalar=alpha[:], in1=k.y[:, t, :],
                                                   op0=ALU.mult, op1=ALU.add)
                    dve.drain()
                nc.vector.tensor_tensor(k.x[:, t, :], k.x[:, t, :], h[:], ALU.add).then_inc(done, 1)
                dve.wait_ge(done, t + 1)


class Router:

    def __init__(self, k, name, w_gate, b_gate, ctx, extra=0):
        self.k, self.extra, self.w_gate, self.b_gate = k, extra, w_gate, b_gate
        self.w = k.sb(f"{name}_gate_w", [128, KD, E], F32, ctx)
        self.b = k.sb(f"{name}_gate_b", [P, E], F32, ctx)
        self.logit = k.sb(f"{name}_logit", [P, NT, E], F32, ctx)
        self.best = k.sb(f"{name}_best", [P, NT], F32, ctx)
        self.rank = k.sb(f"{name}_rank", [P, NT, E], F32, ctx)
        self.share = k.sb(f"{name}_share", [P, NT, E + extra], F32, ctx)
        spare = k.y[:].rearrange("p t d -> p (t d)")
        table = NT * E * E
        self.shareT = spare[0:E + extra, 2 * table:2 * table + N]
        self.above, self.equal = (spare[:, i * table:(i + 1) * table].rearrange("p (t e o) -> p t e o", t=NT, e=E)
                                  for i in range(2))
        self.earlier = k.sb(f"{name}_earlier", [P, E, E], F32, ctx)
        (self.gate_in, self.earlier_ok, self.logit_ps, self.shift_ok, self.exp_ok, self.share_ok, self.shareT_ps,
         self.shareT_ok) = k.router_sems
        self.turn = k.routers
        k.routers += 1

    def sync(self, sp):
        sp.dma_start(self.w[:], self.w_gate.rearrange("(f p) e -> p f e", p=128)).then_inc(self.gate_in, 16)
        sp.dma_start(self.b[:], self.b_gate.partition_broadcast(P)).then_inc(self.gate_in, 16)

    def gpsimd(self, pool):
        nc = self.k.nc
        nc.gpsimd.memset(self.earlier[:], 1.0)
        pool.drain()
        nc.gpsimd.affine_select(out=self.earlier[:], in_=self.earlier[:], compare_op=ALU.is_gt, fill=0.0, base=0,
                                pattern=[[1, E], [-1, E]], channel_multiplier=0).then_inc(self.earlier_ok, 1)

    def tensor_logits(self, pe, norm):
        nc, k = self.k.nc, self.k
        pe.wait_ge(self.gate_in, 32 * self.turn + 32)
        pe.wait_ge(norm.yT_ok, norm.base + NT)
        for t in range(NT):
            for f in range(KD):
                last = nc.tensor.matmul(k.bank[0:P, 5, t * E:(t + 1) * E], k.yT[:, f, tile_cols(t)], self.w[:, f, :],
                                        start=(f == 0), stop=(f == KD - 1))
        last.then_inc(self.logit_ps, 1)

    def scalar_exp(self, act):
        act.wait_ge(self.shift_ok, self.turn + 1)
        self.k.nc.scalar.activation(self.logit[:], self.logit[:], ACT.Exp).then_inc(self.exp_ok, 1)

    def vector(self, dve):
        nc, k, wide = self.k.nc, self.k, [P, NT, E, E]
        dve.wait_ge(self.logit_ps, self.turn + 1)
        dve.wait_ge(self.gate_in, 32 * self.turn + 32)
        dve.wait_ge(self.earlier_ok, self.turn + 1)
        nc.vector.tensor_tensor(self.logit[:], k.bank[0:P, 5, 0:NT * E].rearrange("p (t e) -> p t e", t=NT),
                                self.b[:].unsqueeze(1).broadcast_to([P, NT, E]), ALU.add)
        dve.drain()
        mine = self.logit[:].unsqueeze(3).broadcast_to(wide)
        other = self.logit[:].unsqueeze(2).broadcast_to(wide)
        nc.vector.tensor_tensor(self.above, other, mine, ALU.is_gt)
        nc.vector.tensor_tensor(self.equal, other, mine, ALU.is_equal)
        nc.vector.tensor_reduce(self.best[:], self.logit[:], AX.X, ALU.max)
        dve.drain()
        nc.vector.tensor_tensor(self.equal, self.equal, self.earlier[:].unsqueeze(1).broadcast_to(wide), ALU.mult)
        nc.vector.tensor_tensor(self.logit[:], self.logit[:], self.best[:].unsqueeze(2).broadcast_to([P, NT, E]),
                                ALU.subtract).then_inc(self.shift_ok, 1)
        dve.drain()
        nc.vector.tensor_tensor(self.above, self.above, self.equal, ALU.add)
        dve.drain()
        nc.vector.tensor_reduce(self.rank[:], self.above, AX.X, ALU.add)
        dve.drain()
        dve.wait_ge(self.exp_ok, self.turn + 1)
        nc.vector.scalar_tensor_tensor(out=self.rank[:], in0=self.rank[:], scalar=1.5, in1=self.logit[:],
                                       op0=ALU.is_lt, op1=ALU.mult)
        dve.drain()
        nc.vector.tensor_reduce(self.best[:], self.rank[:], AX.X, ALU.add)
        dve.drain()
        nc.vector.reciprocal(self.best[:], self.best[:])
        if self.extra:
            nc.vector.memset(self.share[:, :, E:E + 1], 0.5)
        dve.drain()
        nc.vector.tensor_tensor(self.share[:, :, 0:E], self.rank[:], self.best[:].unsqueeze(2).broadcast_to([P, NT, E]),
                                ALU.mult)
        dve.drain()
        dve.sem_inc(self.share_ok, 1)

    def tensor_shares(self, pe):
        nc, k = self.k.nc, self.k
        pe.wait_ge(self.share_ok, self.turn + 1)
        for t in range(NT):
            last = nc.tensor.transpose(k.bank[0:E + self.extra, 4 + t // 4, (t % 4) * P:(t % 4 + 1) * P],
                                       self.share[:, t, :], k.ident[0:P, 0:P])
        last.then_inc(self.shareT_ps, 1)

    def scalar_shares(self, act):
        nc, k = self.k.nc, self.k
        act.wait_ge(self.shareT_ps, self.turn + 1)
        nc.scalar.copy(self.shareT[:, 0:8 * P].rearrange("p (b n) -> p b n", b=2), k.bank[0:E + self.extra, 4:6, 0:4 * P])
        nc.scalar.copy(self.shareT[:, 8 * P:N], k.bank[0:E + self.extra, 6, 0:2 * P]).then_inc(self.shareT_ok, 1)


TOKENS = [(0, 417), (417, 417), (834, N - 834)]


def routed_layer(k, name, kind):
    nc, d = k.nc, k.d
    gated = kind == "gated"
    extra = 0 if gated else 1
    FIN, FH = (16, 8) if gated else (2, 2)
    with ExitStack() as ctx:
        norm = Norm(k, name, ctx)
        pre = "L3_ffn_" if gated else "L0_ffn_"
        router = Router(k, name, d["L3_ffn_router_w" if gated else "L0_ffn_Wg"],
                        d["L3_ffn_router_b" if gated else "L0_ffn_bg"], ctx, extra)
        w1 = k.sb(f"{name}_w1", [128, 2, KD, FIN * 128], F32, ctx)
        w2 = k.sb(f"{name}_w2", [128, 2, FH, D], F32, ctx)
        b1 = k.sb(f"{name}_b1", [128, E + extra, FIN], F32, ctx)
        b1_now = k.sb(f"{name}_b1_now", [128, 2, FIN], F32, ctx)
        b2 = k.sb(f"{name}_b2", [E + extra, D], F32, ctx)
        if gated:
            hT = k.sb(f"{name}_hT", [128, FH, N], F32, ctx)
            b1_gate = k.sb(f"{name}_b1_gate", [128, E, FH], F32, ctx)
            b1_up = k.sb(f"{name}_b1_up", [128, E, FH], F32, ctx)
            sig = k.sb(f"{name}_sig", [128, 2, 417], F32, ctx)
            half = k.sb(f"{name}_half", [128, 2, 417], F32, ctx)
        else:
            hT = k.z[:].rearrange("p t d -> p (t d)")[:, 0:FH * N].rearrange("p (f n) -> p f n", f=FH)
        w1_in = [k.sem(f"{name}_w1_in{u}") for u in range(2)]
        w2_in = [k.sem(f"{name}_w2_in{u}") for u in range(2)]
        b_in, first_done = k.sem(f"{name}_b_in"), k.sem(f"{name}_first_done")
        first_ps, hidden_ok = k.sem(f"{name}_first_ps"), k.sem(f"{name}_hidden_ok")
        out_ps, out_used, bias_ok, sig_ok = (k.sem(f"{name}_{s}") for s in ("out_ps", "out_used", "bias_ok", "sig_ok"))
        added = k.sem(f"{name}_added")
        RING1, RING2 = (2, 4) if gated else (3, 4)
        STEPS = FH * 3
        block = ctx.enter_context(nc.Block())

        def view1(w):
            return w.rearrange("(f p) n -> p f n", p=128)

        @block.sync
        def _(sp):
            router.sync(sp)
            if gated:
                src1, src2 = d["L3_ffn_gate_up_proj"], d["L3_ffn_down_proj"]
            else:
                src1, src2 = d["L0_ffn_W1"], d["L0_ffn_W2"]
            src1 = src1.rearrange("e (f p) n -> p e f n", p=128)
            src2 = src2.rearrange("e (f p) n -> p e f n", p=128)
            for e in range(2):
                sp.dma_start(w1[:, e], src1[:, e]).then_inc(w1_in[e], 16)
                if e == 0:
                    sp.dma_start(b1[:, 0:E], d["L3_ffn_gate_up_proj_bias_P" if gated else "L0_ffn_b1_P"]).then_inc(b_in, 16)
                    sp.dma_start(b2[0:E], d["L3_ffn_down_proj_bias" if gated else "L0_ffn_b2"]).then_inc(b_in, 16)
                    if not gated:
                        sp.dma_start(b1[:, E:E + 1], d["L0_ffn_bs1_P"]).then_inc(b_in, 16)
                        sp.dma_start(b2[E:E + 1], d["L0_ffn_bs2"].unsqueeze(0)).then_inc(b_in, 16)
                sp.dma_start(w2[:, e], src2[:, e]).then_inc(w2_in[e], 16)
            with sp.Fori(1, E // 2) as h:
                for u in range(2):
                    e = h * 2 + u
                    sp.wait_ge(first_done, e - 1)
                    sp.dma_start(w1[:, u:u + 1], src1[:, bass.ds(e, 1)]).then_inc(w1_in[u], 16)
                    sp.wait_ge(out_ps, (e - 1) * NT)
                    sp.dma_start(w2[:, u:u + 1], src2[:, bass.ds(e, 1)]).then_inc(w2_in[u], 16)
            if not gated:
                sp.wait_ge(first_done, E - 1)
                sp.dma_start(w1[:, 0], view1(d["L0_ffn_Ws1"])).then_inc(w1_in[0], 16)
                sp.wait_ge(out_ps, (E - 1) * NT)
                sp.dma_start(w2[:, 0], view1(d["L0_ffn_Ws2"])).then_inc(w2_in[0], 16)

        @block.gpsimd
        def _(pool):
            router.gpsimd(pool)

        @block.tensor
        def _(pe):
            norm.tensor(pe)
            router.tensor_logits(pe, norm)

            def expert(e, turn, u):
                pe.wait_ge(w1_in[u], turn * 16 + 16)
                for n in range(STEPS):
                    f, (c0, cn) = n // 3, TOKENS[n % 3]
                    pe.wait_ge(hidden_ok, e * STEPS + n + 1)
                    for part in range(2 if gated else 1):
                        b = n % RING1 * (2 if gated else 1) + part
                        for kk in range(KD):
                            col = (part * FH + f) * 128
                            last = nc.tensor.matmul(k.bank[:, b, 0:cn], w1[:, u, kk, col:col + 128],
                                                    k.yT[:, kk, c0:c0 + cn], start=(kk == 0), stop=(kk == KD - 1))
                    last.then_inc(first_ps, 1)
                pe.wait_ge(hidden_ok, (e + 1) * STEPS + RING1)
                pe.wait_ge(w2_in[u], turn * 16 + 16)
                pe.sem_inc(first_done, 1)
                for t in range(NT):
                    pe.wait_ge(out_used, e * NT + t + 1)
                    for f in range(FH):
                        last = nc.tensor.matmul(k.bank[0:P, 4 + (t + 2 * u) % 4, :],
                                                hT[:, f, tile_cols(t)], w2[:, u, f, :],
                                                start=(f == 0), stop=(f == FH - 1))
                    last.then_inc(out_ps, 1)

            with pe.Fori(0, E // 2) as h:
                for u in range(2):
                    expert(h * 2 + u, h, u)
            if not gated:
                expert(E, E // 2, 0)
            pe.wait_ge(out_used, RING2 + (E + extra) * NT)
            router.tensor_shares(pe)
            pe.wait_ge(router.shareT_ok, router.turn + 1)
            pe.wait_ge(b_in, 32 if gated else 64)
            for t in range(NT):
                if t >= 2:
                    pe.wait_ge(added, t - 1)
                nc.tensor.matmul(k.bank[0:P, t % 2, :], router.shareT[:, tile_cols(t)], b2[:],
                                 start=True, stop=True).then_inc(out_ps, 1)

        @block.scalar
        def _(act):
            norm.scalar(act)
            router.scalar_exp(act)
            act.wait_ge(b_in, 32 if gated else 64)
            if gated:
                act.wait_ge(bias_ok, 1)

            def expert(e, u):
                act.drain()
                bias = b1_gate if gated else b1
                nc.scalar.copy(b1_now[:, u:u + 1, 0:FH], bias[:, bass.ds(e, 1), :])
                act.drain()
                for n in range(STEPS):
                    f, (c0, cn) = n // 3, TOKENS[n % 3]
                    act.wait_ge(first_ps, e * STEPS + n + 1)
                    if gated:
                        nc.scalar.activation(sig[:, n % 2, 0:cn], k.bank[:, n % 2 * 2, 0:cn], ACT.Sigmoid,
                                             bias=b1_now[:, u, f:f + 1], scale=1.702).then_inc(sig_ok, 1)
                    else:
                        nc.scalar.activation(hT[:, f, c0:c0 + cn], k.bank[:, n % 3, 0:cn], ACT.Relu,
                                             bias=b1_now[:, u, f:f + 1]).then_inc(hidden_ok, 1)

            with act.Fori(0, E // 2) as h:
                for u in range(2):
                    expert(h * 2 + u, u)
            if not gated:
                expert(E, 0)
            router.scalar_shares(act)

        @block.vector
        def _(dve):
            norm.vector(dve)
            router.vector(dve)
            if gated:
                dve.wait_ge(b_in, 32)
                nc.vector.tensor_scalar(b1_gate[:], b1[:, :, 0:FH], 1.702, None, ALU.mult)
                nc.vector.tensor_scalar(b1_up[:], b1[:, :, FH:FIN], 1.0, None, ALU.add)
                dve.drain()
                dve.sem_inc(bias_ok, 1)
            dve.sem_inc(hidden_ok, RING1)
            dve.sem_inc(out_used, RING2)

            def expert(e, u):
                if gated:
                    for n in range(STEPS):
                        f, (c0, cn) = n // 3, TOKENS[n % 3]
                        dve.wait_ge(sig_ok, e * STEPS + n + 1)
                        nc.vector.scalar_tensor_tensor(out=half[:, n % 2, 0:cn], in0=k.bank[:, n % 2 * 2, 0:cn],
                                                       scalar=b1[:, bass.ds(e, 1), f], in1=sig[:, n % 2, 0:cn],
                                                       op0=ALU.add, op1=ALU.mult)
                        dve.drain()
                        nc.vector.scalar_tensor_tensor(out=hT[:, f, c0:c0 + cn], in0=k.bank[:, n % 2 * 2 + 1, 0:cn],
                                                       scalar=b1_up[:, bass.ds(e, 1), f], in1=half[:, n % 2, 0:cn],
                                                       op0=ALU.add, op1=ALU.mult).then_inc(hidden_ok, 1)
                dve.drain()
                for t in range(NT):
                    dve.wait_ge(out_ps, e * NT + t + 1)
                    nc.vector.scalar_tensor_tensor(out=k.x[:, t, :], in0=k.bank[0:P, 4 + (t + 2 * u) % 4, :],
                                                   scalar=router.share[:, t, bass.ds(e, 1)], in1=k.x[:, t, :],
                                                   op0=ALU.mult, op1=ALU.add).then_inc(out_used, 1)

            with dve.Fori(0, E // 2) as h:
                for u in range(2):
                    expert(h * 2 + u, u)
            if not gated:
                expert(E, 0)
            dve.drain()
            for t in range(NT):
                dve.wait_ge(out_ps, (E + extra) * NT + t + 1)
                nc.vector.tensor_tensor(k.x[:, t, :], k.x[:, t, :], k.bank[0:P, t % 2, :], ALU.add).then_inc(added, 1)


SINKHORN, TOP = 8, N // E


def balanced_layer(k, name):
    nc, d = k.nc, k.d
    with ExitStack() as ctx:
        norm = Norm(k, name, ctx)
        w_gate = k.sb(f"{name}_w_gate", [128, KD, E], F32, ctx)
        ones = k.sb(f"{name}_ones", [P, P], F32, ctx)
        gate = k.sb(f"{name}_gate", [P, NT, E], F32, ctx)
        col = k.sb(f"{name}_col", [P, E], F32, ctx)
        row = k.sb(f"{name}_row", [P, NT], F32, ctx)
        gateT = k.sb(f"{name}_gateT", [E, N], F32, ctx)
        left = k.sb(f"{name}_left", [E, N], F32, ctx)
        top = k.sb(f"{name}_top", [E, 8], F32, ctx)
        zeros = k.sb(f"{name}_zeros", [E, N], F32, ctx)
        equal = k.sb(f"{name}_equal", [E, N], F32, ctx)
        count = k.sb(f"{name}_count", [E, N], F32, ctx)
        above = k.sb(f"{name}_above", [E, 2], F32, ctx)
        taken = k.sb(f"{name}_taken", [P, NT, E], F32, ctx)
        share = k.sb(f"{name}_share", [P, NT, E], F32, ctx)
        w = k.sb(f"{name}_w", [128, 2, KD, D], F32, ctx)
        gate_in, gate_ps, scaled = k.sem(f"{name}_gate_in"), k.sem(f"{name}_gate_ps"), k.sem(f"{name}_scaled")
        col_ps, gateT_ps, taken_ok = k.sem(f"{name}_col_ps"), k.sem(f"{name}_gateT_ps"), k.sem(f"{name}_taken_ok")
        taken_ps, out_ps, out_used = k.sem(f"{name}_taken_ps"), k.sem(f"{name}_out_ps"), k.sem(f"{name}_out_used")
        ones_ok, w_in = k.sem(f"{name}_ones_ok"), [k.sem(f"{name}_w_in{u}") for u in range(2)]
        block = ctx.enter_context(nc.Block())
        src = d["L1_ffn_experts"].rearrange("e (f p) n -> p e f n", p=128)

        @block.sync
        def _(sp):
            sp.dma_start(w_gate[:], d["L1_ffn_gate_w"].rearrange("h (f p) e -> p (h f) e", p=128)).then_inc(gate_in, 16)
            for e in range(2):
                sp.dma_start(w[:, e], src[:, e]).then_inc(w_in[e], 16)
            with sp.Fori(1, E // 2) as h:
                for u in range(2):
                    e = h * 2 + u
                    sp.wait_ge(out_ps, (e - 1) * NT)
                    sp.dma_start(w[:, u:u + 1], src[:, bass.ds(e, 1)]).then_inc(w_in[u], 16)

        @block.gpsimd
        def _(pool):
            nc.gpsimd.memset(ones[:], 1.0)
            nc.gpsimd.memset(zeros[:], 0.0).then_inc(ones_ok, 1)

        @block.scalar
        def _(act):
            norm.scalar(act)

        @block.tensor
        def _(pe):
            norm.tensor(pe)
            pe.wait_ge(gate_in, 16)
            pe.wait_ge(norm.yT_ok, norm.base + NT)
            for t in range(NT):
                for f in range(KD):
                    last = nc.tensor.matmul(k.bank[0:P, 5, t * E:(t + 1) * E], k.yT[:, f, tile_cols(t)], w_gate[:, f, :],
                                            start=(f == 0), stop=(f == KD - 1))
            last.then_inc(gate_ps, 1)
            pe.wait_ge(ones_ok, 1)
            with pe.Fori(0, SINKHORN) as i:
                pe.wait_ge(scaled, i + 1)
                nc.tensor.matmul(k.bank[0:P, 4, 0:NT * E], ones[:], gate[:].rearrange("p t e -> p (t e)"),
                                 start=True, stop=True).then_inc(col_ps, 1)
            pe.wait_ge(scaled, SINKHORN + 1)
            for t in range(NT):
                last = nc.tensor.transpose(k.bank[0:E, t // 4, (t % 4) * P:(t % 4 + 1) * P], gate[:, t, :],
                                           k.ident[0:P, 0:P])
            last.then_inc(gateT_ps, 1)
            pe.wait_ge(taken_ok, 1)
            for t in range(NT):
                last = nc.tensor.transpose(k.bank[0:P, 4, t * E:(t + 1) * E], gateT[:, tile_cols(t)], k.ident[0:E, 0:E])
            last.then_inc(taken_ps, 1)

            def expert(e, turn, u):
                pe.wait_ge(w_in[u], turn * 16 + 16)
                for t in range(NT):
                    pe.wait_ge(out_used, e * NT + t + 1)
                    for f in range(KD):
                        last = nc.tensor.matmul(k.bank[0:P, (t + 2 * u) % 4, :], k.yT[:, f, tile_cols(t)], w[:, u, f, :],
                                                start=(f == 0), stop=(f == KD - 1))
                    last.then_inc(out_ps, 1)

            with pe.Fori(0, E // 2) as h:
                for u in range(2):
                    expert(h * 2 + u, h, u)

        @block.vector
        def _(dve):
            norm.vector(dve)
            dve.wait_ge(gate_ps, 1)
            nc.vector.tensor_scalar(gate[:], k.bank[0:P, 5, 0:NT * E].rearrange("p (t e) -> p t e", t=NT), 1e-10, None,
                                    ALU.max).then_inc(scaled, 1)
            with dve.Fori(0, SINKHORN) as i:
                dve.wait_ge(col_ps, i + 1)
                nc.vector.tensor_reduce(col[:], k.bank[0:P, 4, 0:NT * E].rearrange("p (t e) -> p e t", t=NT), AX.X, ALU.add)
                dve.drain()
                nc.vector.reciprocal(col[:], col[:])
                dve.drain()
                nc.vector.tensor_tensor(gate[:], gate[:], col[:].unsqueeze(1).broadcast_to([P, NT, E]), ALU.mult)
                dve.drain()
                nc.vector.tensor_reduce(row[:], gate[:], AX.X, ALU.add)
                dve.drain()
                nc.vector.reciprocal(row[:], row[:])
                dve.drain()
                nc.vector.tensor_tensor(gate[:], gate[:], row[:].unsqueeze(2).broadcast_to([P, NT, E]),
                                        ALU.mult).then_inc(scaled, 1)
            dve.wait_ge(gateT_ps, 1)
            for c0, b, cn in ((0, 0, 4 * P), (4 * P, 1, 4 * P), (8 * P, 2, 2 * P)):
                nc.vector.tensor_copy(gateT[:, c0:c0 + cn], k.bank[0:E, b, 0:cn])
                nc.vector.tensor_copy(left[:, c0:c0 + cn], k.bank[0:E, b, 0:cn])
            dve.drain()
            with dve.Fori(0, (TOP - 1) // 8) as i:
                nc.vector.max(top[:], left[:])
                dve.drain()
                nc.vector.match_replace(left[:], top[:], left[:], -1.0)
                dve.drain()
            nc.vector.max(top[:], left[:])
            dve.drain()
            least = top[:, (TOP - 1) % 8:(TOP - 1) % 8 + 1]
            nc.vector.tensor_scalar(equal[:], gateT[:], least, None, ALU.is_equal)
            nc.vector.tensor_scalar(left[:], gateT[:], least, None, ALU.is_gt)
            dve.drain()
            nc.vector.tensor_reduce(above[:, 0:1], left[:], AX.X, ALU.add)
            dve.wait_ge(ones_ok, 1)
            nc.vector.tensor_tensor_scan(count[:], equal[:], zeros[:], 0.0, ALU.add, ALU.add)
            dve.drain()
            nc.vector.tensor_scalar(above[:, 1:2], above[:, 0:1], -1.0, float(TOP), ALU.mult, ALU.add)
            dve.drain()
            nc.vector.scalar_tensor_tensor(out=count[:], in0=count[:], scalar=above[:, 1:2], in1=equal[:],
                                           op0=ALU.is_le, op1=ALU.mult)
            dve.drain()
            nc.vector.tensor_tensor(gateT[:], count[:], left[:], ALU.add).then_inc(taken_ok, 1)
            dve.wait_ge(taken_ps, 1)
            nc.vector.tensor_copy(taken[:], k.bank[0:P, 4, 0:NT * E].rearrange("p (t e) -> p t e", t=NT))
            dve.drain()
            nc.vector.tensor_reduce(row[:], taken[:], AX.X, ALU.add)
            nc.vector.tensor_scalar(share[:], gate[:], 0.5, None, ALU.is_gt)
            dve.drain()
            nc.vector.tensor_scalar(row[:], row[:], 1.0, None, ALU.add)
            nc.vector.tensor_tensor(share[:], share[:], taken[:], ALU.mult)
            dve.drain()
            nc.vector.reciprocal(row[:], row[:])
            dve.drain()
            nc.vector.tensor_tensor(share[:], share[:], row[:].unsqueeze(2).broadcast_to([P, NT, E]), ALU.mult)
            dve.sem_inc(out_used, 4)

            def expert(e, u):
                dve.drain()
                for t in range(NT):
                    dve.wait_ge(out_ps, e * NT + t + 1)
                    nc.vector.scalar_tensor_tensor(out=k.x[:, t, :], in0=k.bank[0:P, (t + 2 * u) % 4, :],
                                                   scalar=share[:, t, bass.ds(e, 1)], in1=k.x[:, t, :],
                                                   op0=ALU.mult, op1=ALU.add).then_inc(out_used, 1)

            with dve.Fori(0, E // 2) as h:
                for u in range(2):
                    expert(h * 2 + u, u)


HEADS, DH = 8, 64


def attention_layer(k, name):
    nc, d = k.nc, k.d
    PAIRS, STEPS = HEADS // 2, 2 * NT
    with ExitStack() as ctx:
        norm = Norm(k, name, ctx)
        qT = k.sb(f"{name}_qT", [128, PAIRS, N], F32, ctx)
        kT = k.sb(f"{name}_kT", [128, PAIRS, N], F32, ctx)
        v = k.sb(f"{name}_v", [P, NT, D], F32, ctx)
        work = k.sb(f"{name}_work", [128, KD * 3 * D], F32, ctx)
        w_qkv = work[:].rearrange("p (f n) -> p f n", f=KD)
        prob = work[0:P, 0:2 * N].rearrange("p (b n) -> p b n", b=2)
        probT = work[0:P, 2 * N:4 * N].rearrange("p (b s n) -> p b s n", b=2, s=NT)
        w_ff = qT[:].rearrange("p h n -> p (h n)")[:, 0:KD * D].rearrange("p (f n) -> p f n", f=KD)
        q_now = k.sb(f"{name}_q_now", [128, 2, N], F32, ctx)
        b_v = k.sb(f"{name}_b_v", [P, D], F32, ctx)
        b_ff = k.sb(f"{name}_b_ff", [P, D], F32, ctx)
        b_qk = k.sb(f"{name}_b_qk", [128, 12], F32, ctx)
        top = k.sb(f"{name}_top", [P, 2, 2], F32, ctx)
        den_now = k.sb(f"{name}_den_now", [P, 4, 1], F32, ctx)
        den = k.sb(f"{name}_den", [P, HEADS, NT], F32, ctx)
        msg = k.y
        spare = k.y[:].rearrange("p t d -> p (t d)")
        w_in, b_in, spilled, b_ok = (k.sem(f"{name}_{s}") for s in ("w_in", "b_in", "spilled", "b_ok"))
        floor_ok, ln_ok, mask_ok = (k.sem(f"{name}_{s}") for s in ("floor_ok", "ln_ok", "mask_ok"))
        qk_ps, qk_ok, v_ps, v_ok = (k.sem(f"{name}_{s}") for s in ("qk_ps", "qk_ok", "v_ps", "v_ok"))
        q_ok, score_ps, max_ok, prob_ok = (k.sem(f"{name}_{s}") for s in ("q_ok", "score_ps", "max_ok", "prob_ok"))
        probT_ps, probT_a, probT_v = (k.sem(f"{name}_{s}") for s in ("probT_ps", "probT_a", "probT_v"))
        pv_ps, pv_ok, msg_ok, msgT_ps, msgT_ok, ff_in, ff_ps, ff_ok = (
            k.sem(f"{name}_{s}") for s in ("pv_ps", "pv_ok", "msg_ok", "msgT_ps", "msgT_ok", "ff_in", "ff_ps", "ff_ok"))
        seen = k.sem(f"{name}_seen")
        block = ctx.enter_context(nc.Block())

        @block.sync
        def _(sp):
            sp.dma_start(k.adj_saved, k.adj[:]).then_inc(spilled, 16)
            sp.dma_start(w_qkv, d["L2_gnn_W_qkv_T"].rearrange("(f p) n -> p f n", p=128)).then_inc(w_in, 16)
            sp.dma_start(b_qk[:], d["L2_gnn_b_qkv_P"].rearrange("p a f -> p (a f)")).then_inc(b_in, 16)
            sp.dma_start(b_v[:], d["L2_gnn_b_qkv"][2 * D:3 * D].partition_broadcast(P)).then_inc(b_in, 16)
            sp.dma_start(b_ff[:], d["L2_gnn_b_ff"].partition_broadcast(P)).then_inc(b_in, 16)
            sp.wait_ge(q_ok, HEADS)
            sp.dma_start(w_ff, d["L2_gnn_W_ff_T"].rearrange("(f p) n -> p f n", p=128)).then_inc(ff_in, 16)

        @block.gpsimd
        def _(pool):
            nc.gpsimd.memset(q_now[DH:128, 0, :], 0.0)
            nc.gpsimd.memset(q_now[0:DH, 1, :], 0.0)
            pool.wait_ge(qk_ok, 24)
            for u in range(2):
                rows = slice(DH * u, DH * (u + 1))
                nc.gpsimd.tensor_copy(q_now[rows, u, :], qT[rows, 0, :]).then_inc(q_ok, 1)
            with pool.Fori(1, PAIRS) as pair:
                for u in range(2):
                    rows = slice(DH * u, DH * (u + 1))
                    pool.drain()
                    pool.wait_ge(score_ps, pair * STEPS - NT + NT * u)
                    pool.sem_inc(seen, 1)
                    nc.gpsimd.tensor_copy(q_now[rows, u, :], qT[rows, bass.ds(pair, 1), :]).then_inc(q_ok, 1)

        @block.tensor
        def _(pe):
            norm.tensor(pe)
            pe.wait_ge(w_in, 16)
            pe.wait_ge(norm.yT_ok, norm.base + NT)
            for n in range(24):
                c0, cn = TOKENS[n % 3]
                if n >= 3:
                    pe.wait_ge(qk_ok, n - 2)
                for f in range(KD):
                    last = nc.tensor.matmul(k.bank[:, n % 3, 0:cn], w_qkv[:, f, n // 3 * 128:(n // 3 + 1) * 128],
                                            k.yT[:, f, c0:c0 + cn], start=(f == 0), stop=(f == KD - 1))
                last.then_inc(qk_ps, 1)
            for t in range(NT):
                if t >= 2:
                    pe.wait_ge(v_ok, t - 1)
                for f in range(KD):
                    last = nc.tensor.matmul(k.bank[0:P, 3 + t % 2, :], k.yT[:, f, tile_cols(t)], w_qkv[:, f, 2 * D:3 * D],
                                            start=(f == 0), stop=(f == KD - 1))
                last.then_inc(v_ps, 1)
            pe.wait_ge(qk_ok, 24)
            pe.wait_ge(v_ok, NT)

            def scores(pair, n):
                if n % NT == 0:
                    pe.wait_ge(q_ok, pair * 2 + n // NT + 1)
                pe.wait_ge(max_ok, pair * STEPS + n + 1)
                for c, (c0, cn) in enumerate(CHUNKS):
                    last = nc.tensor.matmul(k.bank[0:P, c, 0:cn], q_now[:, n // NT, tile_cols(n % NT)],
                                            kT[:, bass.ds(pair, 1), c0:c0 + cn], start=True, stop=True)
                last.then_inc(score_ps, 1)

            def transposes(pair, n):
                pe.wait_ge(prob_ok, pair * STEPS + n + 1)
                if n >= 1:
                    pe.wait_ge(probT_a, pair * STEPS + n)
                    pe.wait_ge(probT_v, pair * STEPS + n)
                for s in range(NT):
                    last = nc.tensor.transpose(k.bank[0:P, 3 + s // 4, s % 4 * P:(s % 4 + 1) * P],
                                               prob[:, n % 2, tile_cols(s)], k.ident[0:P, 0:P])
                last.then_inc(probT_ps, 1)

            def values(pair, n):
                pe.wait_ge(probT_a, pair * STEPS + n + 1)
                pe.wait_ge(probT_v, pair * STEPS + n + 1)
                pe.wait_ge(pv_ok, pair * STEPS + n + 1)
                for s in range(NT):
                    last = nc.tensor.matmul(k.bank[0:P, 6 + n % 2, 0:DH], probT[:, n % 2, s, :],
                                            v[:, s, bass.ds(pair * 2 * DH + n // NT * DH, DH)],
                                            start=(s == 0), stop=(s == NT - 1))
                last.then_inc(pv_ps, 1)

            with pe.Fori(0, PAIRS) as pair:
                for n in range(STEPS + 2):
                    if n < STEPS:
                        scores(pair, n)
                    if 1 <= n <= STEPS:
                        transposes(pair, n - 1)
                    if n >= 2:
                        values(pair, n - 2)
            for t in range(NT):
                pe.wait_ge(msg_ok, t + 1)
                if t >= 2:
                    pe.wait_ge(msgT_ok, t - 1)
                for f in range(KD):
                    last = nc.tensor.transpose(k.bank[:, 6 + t % 2, f * P:(f + 1) * P], msg[:, t, f * 128:(f + 1) * 128],
                                               k.ident[0:P, 0:P])
                last.then_inc(msgT_ps, 1)
            pe.wait_ge(ff_in, 16)
            for t in range(NT):
                pe.wait_ge(msgT_ok, t + 1)
                if t >= 2:
                    pe.wait_ge(ff_ok, t - 1)
                for f in range(KD):
                    last = nc.tensor.matmul(k.bank[0:P, t % 2, :], k.yT[:, f, tile_cols(t)], w_ff[:, f, :],
                                            start=(f == 0), stop=(f == KD - 1))
                last.then_inc(ff_ps, 1)

        @block.scalar
        def _(act):
            norm.scalar(act)
            act.wait_ge(b_ok, 1)
            for n in range(24):
                f, (c0, cn) = n // 3, TOKENS[n % 3]
                act.wait_ge(qk_ps, n + 1)
                out = qT if f < PAIRS else kT
                nc.scalar.activation(out[:, f % PAIRS, c0:c0 + cn], k.bank[:, n % 3, 0:cn], ACT.Identity,
                                     bias=b_qk[:, f:f + 1], scale=DH ** -0.5 if f < PAIRS else 1.0).then_inc(qk_ok, 1)
            for t in range(NT):
                act.wait_ge(floor_ok, t + 1)
                nc.scalar.activation(spare[:, t % 4 * N:(t % 4 + 1) * N], spare[:, t % 4 * N:(t % 4 + 1) * N],
                                     ACT.Ln).then_inc(ln_ok, 1)
            with act.Fori(0, PAIRS) as pair:
                for n in range(STEPS + 1):
                    if n < STEPS:
                        act.wait_ge(max_ok, pair * STEPS + n + 2)
                        nc.scalar.activation(prob[:, n % 2, :], prob[:, n % 2, :], ACT.Exp, bias=top[:, n % 2, 1:2],
                                             accum_out=den_now[:, n % 4, :]).then_inc(prob_ok, 1)
                    if n >= 1:
                        act.wait_ge(probT_ps, pair * STEPS + n)
                        nc.scalar.copy(probT[:, (n - 1) % 2, 0:8, :].rearrange("p (b s) n -> p b (s n)", b=2),
                                       k.bank[0:P, 3:5, 0:4 * P]).then_inc(probT_a, 1)
            for t in range(NT):
                act.wait_ge(msgT_ps, t + 1)
                nc.scalar.copy(k.yT[:, :, tile_cols(t)],
                               k.bank[:, 6 + t % 2, 0:KD * P].rearrange("p (f n) -> p f n", f=KD)).then_inc(msgT_ok, 1)

        @block.vector
        def _(dve):
            norm.vector(dve)
            dve.wait_ge(b_in, 48)
            nc.vector.tensor_scalar(b_qk[:, 0:PAIRS], b_qk[:, 0:PAIRS], DH ** -0.5, None, ALU.mult).then_inc(b_ok, 1)
            dve.wait_ge(spilled, 16)
            dve.wait_ge(norm.yT_ps, norm.base + NT)

            def floor(t):
                nc.vector.tensor_scalar(spare[:, t % 4 * N:(t % 4 + 1) * N], k.adj[:, t, :], 1.0, None,
                                        ALU.max).then_inc(floor_ok, 1)

            def values(t):
                dve.wait_ge(v_ps, t + 1)
                nc.vector.tensor_tensor(v[:, t, :], k.bank[0:P, 3 + t % 2, :], b_v[:], ALU.add).then_inc(v_ok, 1)

            for t in range(4):
                floor(t)
            for t in range(NT):
                values(t)
            for t in range(NT):
                dve.wait_ge(ln_ok, t + 1)
                nc.vector.tensor_scalar(k.adj[:, t, :], k.adj[:, t, :], 0.0, -BIG, ALU.is_equal, ALU.mult)
                dve.drain()
                nc.vector.tensor_tensor(k.adj[:, t, :], k.adj[:, t, :], spare[:, t % 4 * N:(t % 4 + 1) * N], ALU.add)
                dve.drain()
                if t + 4 < NT:
                    floor(t + 4)
            dve.drain()
            dve.sem_inc(max_ok, 1)
            dve.sem_inc(pv_ok, 2)

            def copies(pair, n):
                dve.wait_ge(probT_ps, pair * STEPS + n + 1)
                nc.vector.tensor_copy(probT[:, n % 2, 8:10, :], k.bank[0:P, 5, 0:2 * P]).then_inc(probT_v, 1)

            def sums(pair, n):
                dve.wait_ge(pv_ps, pair * STEPS + n + 1)
                nc.vector.tensor_copy(msg[:, n % NT, bass.ds(pair * 2 * DH + n // NT * DH, DH)],
                                      k.bank[0:P, 6 + n % 2, 0:DH]).then_inc(pv_ok, 1)
                nc.vector.tensor_copy(den[:, bass.ds(pair * 2 + n // NT, 1), n % NT:n % NT + 1], den_now[:, n % 4, :])

            with dve.Fori(0, PAIRS) as pair:
                for n in range(STEPS + 3):
                    if n < STEPS:
                        dve.wait_ge(score_ps, pair * STEPS + n + 1)
                        dve.sem_inc(seen, 1)
                        nc.vector.tensor_tensor_reduce(out=prob[:, n % 2, :], in0=k.bank[0:P, 0:3, :].rearrange(
                            "p b n -> p (b n)")[:, 0:N], in1=k.adj[:, n % NT, :], scale=1.0, scalar=-3.0 * BIG,
                            op0=ALU.add, op1=ALU.max, accum_out=top[:, n % 2, 0:1])
                        dve.drain()
                        nc.vector.tensor_scalar(top[:, n % 2, 1:2], top[:, n % 2, 0:1], -1.0, None,
                                                ALU.mult).then_inc(max_ok, 1)
                    if 2 <= n <= STEPS + 1:
                        copies(pair, n - 2)
                    if n >= 3:
                        sums(pair, n - 3)
                dve.drain()
            nc.vector.reciprocal(den[:], den[:])
            dve.drain()
            nc.vector.tensor_tensor(den[:], den[:], k.has_in[:, :, 0].unsqueeze(1).broadcast_to([P, HEADS, NT]), ALU.mult)
            dve.drain()
            for t in range(NT):
                row = msg[:, t, :].rearrange("p (h c) -> p h c", h=HEADS)
                nc.vector.tensor_tensor(row, row, den[:, :, t:t + 1].broadcast_to([P, HEADS, DH]),
                                        ALU.mult).then_inc(msg_ok, 1)
            for t in range(NT):
                nc.vector.tensor_tensor(k.x[:, t, :], k.x[:, t, :], b_ff[:], ALU.add)
            for t in range(NT):
                dve.drain() if t == 0 else None
                dve.wait_ge(ff_ps, t + 1)
                nc.vector.tensor_tensor(k.x[:, t, :], k.x[:, t, :], k.bank[0:P, t % 2, :], ALU.add).then_inc(ff_ok, 1)


F2 = 256


def merged_layer(k, name):
    nc, d = k.nc, k.d
    TABLE = KD * F2
    with ExitStack() as ctx:
        norm = Norm(k, name, ctx)
        w_g1 = k.sb(f"{name}_w_g1", [128, KD, D], F32, ctx)
        b_g1 = k.sb(f"{name}_b_g1", [128, KD], F32, ctx)
        w_g2 = k.sb(f"{name}_w_g2", [128, KD, E], F32, ctx)
        b_g2 = k.sb(f"{name}_b_g2", [128, E], F32, ctx)
        b_g2_col = k.sb(f"{name}_b_g2_col", [E, 1], F32, ctx)
        tv1 = k.sb(f"{name}_tv1", [128, 2, KD, F2], F32, ctx)
        tv2 = k.sb(f"{name}_tv2", [128, 2, F2 // 128, D], F32, ctx)
        w1 = k.sb(f"{name}_w1", [128, KD, F2], F32, ctx)
        w2 = k.sb(f"{name}_w2", [128, F2 // 128, D], F32, ctx)
        b1 = k.sb(f"{name}_b1", [128, 2], F32, ctx)
        tv_b1 = k.sb(f"{name}_tv_b1", [128, E, 2], F32, ctx)
        rows = k.sb(f"{name}_rows", [E + 1, 3, D], F32, ctx)
        coef = k.sb(f"{name}_coef", [E + 1, 2, P], F32, ctx)
        zero = k.sb(f"{name}_zero", [128, 417], F32, ctx)
        hidden = k.sb(f"{name}_hidden", [128, 2, 417], F32, ctx)
        part = k.sb(f"{name}_part", [128, KD, 3], F32, ctx)
        mean_h = k.sb(f"{name}_mean_h", [128, KD], F32, ctx)
        mean_wide = k.sb(f"{name}_mean_wide", [128, KD, 128], F32, ctx)
        g = k.sb(f"{name}_g", [128, E], F32, ctx)
        norm_g = k.sb(f"{name}_norm_g", [P, 2, D], F32, ctx)
        hT = k.sb(f"{name}_hT", [128, 2, N], F32, ctx)
        res = k.sb(f"{name}_res", [P, NT, D], F32, ctx)
        stats = k.sb(f"{name}_stats2", [P, NT, 6], F32, ctx)
        mv = k.sb(f"{name}_mv2", [P, NT, 2], F32, ctx)
        rstd = k.sb(f"{name}_rstd2", [P, NT, 1], F32, ctx)
        w_in, small_in, tv_in = k.sem(f"{name}_w_in"), k.sem(f"{name}_small_in"), [k.sem(f"{name}_tv_in{u}") for u in range(2)]
        coef_ok, gate_ps, gate_ok, mean_ok, g_ps, g_ok = (
            k.sem(f"{name}_{s}") for s in ("coef_ok", "gate_ps", "gate_ok", "mean_ok", "g_ps", "g_ok"))
        merged, coef8_ok, w1_ok, w2_ok, norm_ps = (
            k.sem(f"{name}_{s}") for s in ("merged", "coef8_ok", "w1_ok", "w2_ok", "norm_ps"))
        h_ps, h_ok, out_ps, out_used, var_ok, std_ok = (
            k.sem(f"{name}_{s}") for s in ("h_ps", "h_ok", "out_ps", "out_used", "res_var_ok", "res_std_ok"))
        block = ctx.enter_context(nc.Block())
        src1 = d["L2_ffn_tv_W1_T"].rearrange("e (f p) n -> p e f n", p=128)
        src2 = d["L2_ffn_tv_W2_T"].rearrange("e (f p) n -> p e f n", p=128)

        @block.sync
        def _(sp):
            sp.dma_start(w_g1[:], d["L2_ffn_gfc1_w_T"].rearrange("(f p) n -> p f n", p=128)).then_inc(w_in, 16)
            sp.dma_start(w_g2[:], d["L2_ffn_gfc2_w_T"].rearrange("(f p) n -> p f n", p=128)).then_inc(w_in, 16)
            sp.dma_start(w1[:], d["L2_ffn_W1_T"].rearrange("(f p) n -> p f n", p=128)).then_inc(w_in, 16)
            sp.dma_start(w2[:], d["L2_ffn_W2_T"].rearrange("(f p) n -> p f n", p=128)).then_inc(w_in, 16)
            sp.dma_start(b_g1[:], d["L2_ffn_gfc1_b_P"].rearrange("p a f -> p (a f)")).then_inc(small_in, 16)
            sp.dma_start(b_g2[:], d["L2_ffn_gfc2_b"].partition_broadcast(128)).then_inc(small_in, 16)
            sp.dma_start(b_g2_col[:], d["L2_ffn_gfc2_b"].unsqueeze(1)).then_inc(small_in, 16)
            sp.dma_start(b1[:], d["L2_ffn_b1_P"].rearrange("p a f -> p (a f)")).then_inc(small_in, 16)
            sp.dma_start(tv_b1[:], d["L2_ffn_tv_b1_P"]).then_inc(small_in, 16)
            for i, (tables, shared) in enumerate((("tv_b2", "b2"), ("tv_ln_g", "ln_g"), ("tv_ln_b", "ln_b"))):
                sp.dma_start(rows[0:E, i, :], d[f"L2_ffn_{tables}"]).then_inc(small_in, 16)
                sp.dma_start(rows[E:E + 1, i, :], d[f"L2_ffn_{shared}"].unsqueeze(0)).then_inc(small_in, 16)
            for e in range(E):
                if e >= 2:
                    sp.wait_ge(merged, 2 * e - 2)
                sp.dma_start(tv1[:, e % 2], src1[:, e]).then_inc(tv_in[e % 2], 16)
                sp.dma_start(tv2[:, e % 2], src2[:, e]).then_inc(tv_in[e % 2], 16)

        @block.gpsimd
        def _(pool):
            nc.gpsimd.memset(coef[:, 0, :], 1.0)
            nc.gpsimd.memset(coef[:, 1, :], 1.0 - E * 0.03)
            nc.gpsimd.memset(zero[:], 0.0)
            pool.drain()
            nc.gpsimd.memset(coef[0:E, 1, :], 0.03).then_inc(coef_ok, 1)

        @block.tensor
        def _(pe):
            pe.wait_ge(coef_ok, 1)
            pe.wait_ge(small_in, 16 * 11)
            for i in range(2):
                last = nc.tensor.matmul(k.bank[0:P, 3 + i, :], coef[:, 1, :], rows[:, 1 + i, :], start=True, stop=True)
            last.then_inc(norm_ps, 1)
            norm.tensor(pe)
            pe.wait_ge(w_in, 64)
            pe.wait_ge(norm.yT_ok, norm.base + NT)
            for n in range(12):
                f, (c0, cn) = n // 3, TOKENS[n % 3]
                if n >= 3:
                    pe.wait_ge(gate_ok, n - 2)
                for kk in range(KD):
                    last = nc.tensor.matmul(k.bank[:, n % 3, 0:cn], w_g1[:, kk, f * 128:(f + 1) * 128],
                                            k.yT[:, kk, c0:c0 + cn], start=(kk == 0), stop=(kk == KD - 1))
                last.then_inc(gate_ps, 1)
            pe.wait_ge(mean_ok, 1)
            for f in range(KD):
                nc.tensor.matmul(k.bank[:, 0, 0:E], mean_wide[:, f, :], w_g2[:, f, :], start=(f == 0), stop=(f == KD - 1))
            for f in range(KD):
                last = nc.tensor.matmul(k.bank[0:E, 1, 0:P], w_g2[:, f, :], mean_wide[:, f, 0:P],
                                        start=(f == 0), stop=(f == KD - 1))
            last.then_inc(g_ps, 1)
            pe.wait_ge(w1_ok, 1)
            for n in range(6):
                f, (c0, cn) = n // 3, TOKENS[n % 3]
                if n >= 3:
                    pe.wait_ge(h_ok, n - 2)
                for kk in range(KD):
                    last = nc.tensor.matmul(k.bank[:, n % 3, 0:cn], w1[:, kk, f * 128:(f + 1) * 128],
                                            k.yT[:, kk, c0:c0 + cn], start=(kk == 0), stop=(kk == KD - 1))
                last.then_inc(h_ps, 1)
            pe.wait_ge(h_ok, 6)
            pe.wait_ge(w2_ok, 1)
            for t in range(NT):
                if t >= 4:
                    pe.wait_ge(out_used, t - 3)
                nc.tensor.matmul(k.bank[0:P, 4 + t % 4, :], coef[:, 0, :], rows[:, 0, :], start=True, stop=False)
                for f in range(2):
                    last = nc.tensor.matmul(k.bank[0:P, 4 + t % 4, :], hT[:, f, tile_cols(t)], w2[:, f, :],
                                            start=False, stop=(f == 1))
                last.then_inc(out_ps, 1)

        @block.scalar
        def _(act):
            norm.scalar(act)
            act.wait_ge(small_in, 16 * 11)
            for n in range(12):
                f, (c0, cn) = n // 3, TOKENS[n % 3]
                act.wait_ge(gate_ps, n + 1)
                if n >= 2:
                    act.wait_ge(gate_ok, n - 1)
                nc.scalar.activation(hidden[:, n % 2, 0:cn], k.bank[:, n % 3, 0:cn], ACT.Relu, bias=b_g1[:, f:f + 1],
                                     accum_out=part[:, f, n % 3:n % 3 + 1]).then_inc(gate_ok, 1)
            act.drain()
            act.sem_inc(gate_ok, 1)
            act.wait_ge(w1_ok, 1)
            for n in range(6):
                f, (c0, cn) = n // 3, TOKENS[n % 3]
                act.wait_ge(h_ps, n + 1)
                nc.scalar.activation(hT[:, f, c0:c0 + cn], k.bank[:, n % 3, 0:cn], ACT.Relu,
                                     bias=b1[:, f:f + 1]).then_inc(h_ok, 1)
            act.wait_ge(var_ok, 1)
            nc.scalar.activation(rstd[:], rstd[:], ACT.Sqrt).then_inc(std_ok, 1)

        @block.vector
        def _(dve):
            norm.vector(dve)
            dve.wait_ge(norm_ps, 1)
            nc.vector.tensor_copy(norm_g[:], k.bank[0:P, 3:5, :])
            dve.wait_ge(gate_ok, 13)
            nc.vector.tensor_reduce(mean_h[:], part[:], AX.X, ALU.add)
            dve.drain()
            nc.vector.tensor_scalar(mean_h[:], mean_h[:], 1.0 / N, None, ALU.mult)
            dve.drain()
            nc.vector.tensor_copy(mean_wide[:], mean_h[:].unsqueeze(2).broadcast_to([128, KD, 128])).then_inc(mean_ok, 1)
            dve.wait_ge(g_ps, 1)
            dve.wait_ge(small_in, 16 * 11)
            nc.vector.tensor_tensor(g[:], k.bank[:, 0, 0:E], b_g2[:], ALU.add)
            nc.vector.tensor_scalar(coef[0:E, 0, :], k.bank[0:E, 1, 0:P], b_g2_col[:], None, ALU.add)
            dve.drain()
            dve.wait_ge(w_in, 64)
            for e in range(E):
                dve.wait_ge(tv_in[e % 2], 32 * (e // 2 + 1))
                nc.vector.scalar_tensor_tensor(out=w1[:], in0=tv1[:, e % 2], scalar=g[:, e:e + 1], in1=w1[:],
                                               op0=ALU.mult, op1=ALU.add).then_inc(merged, 1)
                nc.vector.scalar_tensor_tensor(out=b1[:], in0=tv_b1[:, e, :], scalar=g[:, e:e + 1], in1=b1[:],
                                               op0=ALU.mult, op1=ALU.add)
                if e == E - 1:
                    dve.drain()
                    dve.sem_inc(w1_ok, 1)
                nc.vector.scalar_tensor_tensor(out=w2[:], in0=tv2[:, e % 2], scalar=g[:, e:e + 1], in1=w2[:],
                                               op0=ALU.mult, op1=ALU.add).then_inc(merged, 1)
                dve.drain()
            dve.sem_inc(w2_ok, 1)
            for t in range(NT):
                dve.wait_ge(out_ps, t + 1)
                nc.vector.tensor_tensor(res[:, t, :], k.y[:, t, :], k.bank[0:P, 4 + t % 4, :], ALU.add).then_inc(out_used, 1)
                dve.wait_ge(out_used, t + 1)
                nc.vector.bn_stats(stats[:, t, :], res[:, t, :])
                dve.drain()
                nc.vector.bn_aggr(mv[:, t, :], stats[:, t, :])
            dve.drain()
            nc.vector.tensor_scalar(rstd[:], mv[:, :, 1:2], 1e-5, None, ALU.add).then_inc(var_ok, 1)
            dve.wait_ge(std_ok, 1)
            nc.vector.reciprocal(rstd[:], rstd[:])
            dve.drain()
            with dve.Fori(0, NT) as t:
                now = res[:, bass.ds(t, 1), :]
                nc.vector.tensor_scalar(now, now, mv[:, bass.ds(t, 1), 0], rstd[:, bass.ds(t, 1), 0],
                                        ALU.subtract, ALU.mult)
                dve.drain()
                nc.vector.tensor_tensor(now, now, norm_g[:, 0:1, :], ALU.mult)
                nc.vector.tensor_tensor(k.x[:, bass.ds(t, 1), :], k.x[:, bass.ds(t, 1), :], norm_g[:, 1:2, :], ALU.add)
                dve.drain()
                nc.vector.tensor_tensor(k.x[:, bass.ds(t, 1), :], k.x[:, bass.ds(t, 1), :], now, ALU.add)


def write_out(k):
    nc, d = k.nc, k.d
    out_done = k.sem("out_done")
    with ExitStack() as ctx:
        block = ctx.enter_context(nc.Block())

        @block.sync
        def _(sp):
            sp.dma_start(d["out"].rearrange("(t p) d -> p t d", p=P), k.x[:]).then_inc(out_done, 16)
            sp.wait_ge(out_done, 16)



def program(nc, dram, stop=8):
    k = Kernel(nc, dram)
    with k.ctx:
        k.x = k.sb("x", [P, NT, D])
        k.ident = k.sb("ident", [128, 128])
        k.degree = k.sb("degree", [P, NT, 2])
        k.inv_in, k.inv_out, k.has_in = (k.sb(n, [P, NT, 1]) for n in ("inv_in", "inv_out", "has_in"))
        k.adj_saved = nc.dram_tensor("adj_saved", (P, NT, N), F32, kind="Internal").ap()
        k.norms, k.routers = 0, 0
        k.norm_sems = [k.sem(n) for n in ("norm_var_ok", "norm_std_ok", "y_ok", "yT_ps", "yT_ok")]
        k.router_sems = [k.sem(n) for n in ("gate_in", "earlier_ok", "logit_ps", "shift_ok", "exp_ok", "share_ok",
                                            "shareT_ps", "shareT_ok")]
        k.x_in, k.ident_ok, k.adj_in = k.sem("x_in"), k.sem("ident_ok"), k.sem("adj_in")
        k.y = k.sb("y", [P, NT, D])
        k.yT = k.sb("yT", [128, KD, N])
        adjacency = k.ctx.enter_context(ExitStack())
        k.adj = k.sb("adj", [P, NT, N], F32, adjacency)
        build_adjacency(k)
        k.bank = k.ps("bank", [128, 8, 512], k.ctx)
        layers = ExitStack()
        with layers:
            k.z = k.sb("z", [128, NT, D], F32, layers)
            k.adjT = k.sb("adjT", [P, NT, N], F32, layers)
            graph_layer(k, "l0_gnn", "sage")
            if stop > 1:
                routed_layer(k, "l0_ffn", "relu")
            if stop > 2:
                graph_layer(k, "l1_gnn", "residual")
        if stop > 3:
            balanced_layer(k, "l1_ffn")
        if stop > 4:
            attention_layer(k, "l2_gnn")
        if stop > 5:
            merged_layer(k, "l2_ffn")
        if stop > 6:
            with ExitStack() as sums:
                k.z = k.sb("z3", [128, NT, D], F32, sums)
                graph_layer(k, "l3_gnn", "sum")
        adjacency.close()
        if stop > 7:
            routed_layer(k, "l3_ffn", "gated")
        write_out(k)


INPUTS = ['x', 'src', 'dst', 'L0_gnn_W_l', 'L0_gnn_W_r', 'L0_gnn_b', 'L0_ffn_Wg', 'L0_ffn_bg', 'L0_ffn_W1', 'L0_ffn_W2',
          'L0_ffn_b2', 'L0_ffn_Ws1', 'L0_ffn_Ws2', 'L0_ffn_bs2', 'L1_gnn_alpha', 'L1_gnn_b', 'L1_ffn_gate_w',
          'L1_ffn_experts', 'L2_gnn_b_qkv', 'L2_gnn_b_ff', 'L2_ffn_gfc2_b', 'L2_ffn_b2', 'L2_ffn_ln_g', 'L2_ffn_ln_b', 'L2_ffn_tv_b2',
          'L2_ffn_tv_ln_g', 'L2_ffn_tv_ln_b', 'L3_gnn_wc', 'L3_gnn_wn', 'L3_gnn_bias', 'L3_ffn_router_w',
          'L3_ffn_router_b', 'L3_ffn_gate_up_proj', 'L3_ffn_down_proj', 'L3_ffn_down_proj_bias']


def laid_out(inputs):
    a = {n: np.ascontiguousarray(inputs[n]) for n in INPUTS}
    for n in ('L1_gnn_W', 'L2_gnn_W_qkv', 'L2_gnn_W_ff', 'L2_ffn_gfc1_w', 'L2_ffn_gfc2_w', 'L2_ffn_W1', 'L2_ffn_W2'):
        a[n + "_T"] = np.ascontiguousarray(np.asarray(inputs[n]).T)
    for n in ('L2_ffn_tv_W1', 'L2_ffn_tv_W2'):
        a[n + "_T"] = np.ascontiguousarray(np.asarray(inputs[n]).transpose(0, 2, 1))
    for n in ('L0_ffn_b1', 'L0_ffn_bs1', 'L2_gnn_b_qkv', 'L2_ffn_gfc1_b', 'L2_ffn_b1', 'L2_ffn_tv_b1',
              'L3_ffn_gate_up_proj_bias'):
        b = np.asarray(inputs[n])
        rows = b.reshape(-1, b.shape[-1] // 128, 128)
        a[n + "_P"] = np.ascontiguousarray(rows.transpose(2, 0, 1))
    return {n: v.reshape(1) if v.ndim == 0 else v for n, v in a.items()}


def kernel(**inputs):
    import concourse.bacc as bacc
    from concourse.bass_utils import run_bass_kernel_spmd

    nc = bacc.Bacc("TRN2", target_bir_lowering=False, num_devices=1)
    arrays = laid_out(inputs)
    dram = {n: nc.dram_tensor(f"in_{n}", v.shape, mybir.dt.from_np(v.dtype), kind="ExternalInput").ap()
            for n, v in arrays.items()}
    dram["out"] = nc.dram_tensor("result", (N, D), F32, kind="ExternalOutput").ap()
    program(nc, dram)
    r = run_bass_kernel_spmd(nc, [{f"in_{n}": v for n, v in arrays.items()}], core_ids=[0])
    return r.results[0]["result"]
```

```python
import numpy as np
import concourse.bass as bass
from concourse import mybir
from concourse.alu_op_type import AluOpType as ALU
from contextlib import ExitStack

F32, F16, I32 = mybir.dt.float32, mybir.dt.float16, mybir.dt.int32
ACT = mybir.ActivationFunctionType
AX = mybir.AxisListType

N, D, E = 1250, 512, 8
P, NT = 125, 10
KD = D // 128
EDGES = 40000
G, J = 40, 8
CHUNKS = [(0, 512), (512, 512), (1024, N - 1024)]
BIG = 1.0e30


class Kernel:

    def __init__(self, nc, dram):
        self.nc, self.d, self.ctx = nc, dram, ExitStack()

    def sb(self, name, shape, dt=F32, ctx=None):
        return (ctx or self.ctx).enter_context(self.nc.sbuf_tensor(name, shape, dt))

    def ps(self, name, shape, ctx):
        return ctx.enter_context(self.nc.psum_tensor(name, shape, F32))

    def sem(self, name):
        return self.ctx.enter_context(self.nc.semaphore(name))


def build_adjacency(k):
    nc, d = k.nc, k.d
    with ExitStack() as ctx:
        edges_i = k.sb("edges_i", [G, 2, P * J], I32, ctx)
        edges_f = k.sb("edges_f", [G, 2, P * J], F32, ctx)
        ends = k.sb("ends", [G, 2], F32, ctx)
        tiles = k.sb("tiles", [G, 2], F32, ctx)
        bounds = k.sb("bounds", [1, 2, G], I32, ctx)
        node = k.sb("node", [P, 2, J, G + 1], F32, ctx)
        iota = k.sb("iota", [P, N], F16, ctx)
        hot_src = k.sb("hot_src", [P, 2, J, N], F16, ctx)
        hot_dst = k.sb("hot_dst", [P, 4, J, P], F16, ctx)
        off_dst = k.sb("off_dst", [P, 4, J, P], F16, ctx)
        far_dst = k.sb("far_dst", [P, J, P], F16, ctx)
        one = k.sb("one", [P, 1], F32, ctx)
        dst_off = k.sem("dst_off")
        ps_node = k.ps("ps_node", [P, 2, 512], ctx)
        acc = k.ps("acc", [P, 2, 3 * 512], ctx)
        edges_in, x_in, ident_ok, iota_ok = k.sem("edges_in"), k.x_in, k.ident_ok, k.sem("iota_ok")
        edges_ok, node_ps, node_ok, tiles_ok = k.sem("edges_ok"), k.sem("node_ps"), k.sem("node_ok"), k.sem("tiles_ok")
        bounds_ps, bounds_ok, adj_zero = k.sem("bounds_ps"), k.sem("bounds_ok"), k.sem("adj_zero")
        src_hot, dst_hot, group_done = k.sem("src_hot"), k.sem("dst_hot"), k.sem("group_done")
        acc_free, acc_ok = k.sem("acc_free"), k.sem("acc_ok")
        block = ctx.enter_context(nc.Block())

        @block.sync
        def _(sp):
            sp.dma_start(edges_i[:, 0, :], d["dst"].rearrange("(g e) -> g e", g=G)).then_inc(edges_in, 16)
            sp.dma_start(edges_i[:, 1, :], d["src"].rearrange("(g e) -> g e", g=G)).then_inc(edges_in, 16)
            sp.dma_start(k.x[:], d["x"].rearrange("(t p) d -> p t d", p=P)).then_inc(x_in, 16)

        @block.gpsimd
        def _(pool):
            nc.gpsimd.memset(k.ident[:], 0.0)
            pool.drain()
            nc.gpsimd.affine_select(out=k.ident[:], in_=k.ident[:], compare_op=ALU.not_equal, fill=1.0, base=0,
                                    pattern=[[-1, 128]], channel_multiplier=1).then_inc(ident_ok, 1)
            nc.gpsimd.memset(one[:], 1.0).then_inc(iota_ok, 1)
            nc.gpsimd.iota(iota[:], pattern=[[1, N]], base=0, channel_multiplier=0,
                           allow_small_or_imprecise_dtypes=True).then_inc(iota_ok, 1)
            nc.gpsimd.memset(node[:, :, :, G:G + 1], 0.0).then_inc(iota_ok, 1)
            nc.gpsimd.memset(k.adj[:], 0.0).then_inc(adj_zero, 1)
            pool.wait_ge(node_ok, 1)
            pool.wait_ge(bounds_ok, 1)
            pool.drain()
            item = pool.alloc_register("item_pool")
            pool.reg_mov(item, 0)
            with pool.Fori(0, G) as g:
                first = pool.value_load(bounds[0:1, 0, bass.ds(g, 1)], min_val=0, max_val=NT - 1)
                end = pool.value_load(bounds[0:1, 1, bass.ds(g, 1)], min_val=1, max_val=NT)
                with pool.Fori(first, end) as t:
                    i = pool.snap(item, min_val=0, max_val=G * NT)
                    slot = pool.snap(i % 4)
                    pool.wait_ge(acc_ok, i + 1)
                    nc.gpsimd.tensor_tensor(off_dst[:, bass.ds(slot, 1), :, :].rearrange("p a j n -> p (a j) n"),
                                            iota[:, bass.ds(t * P, P)].unsqueeze(1).broadcast_to([P, J, P]),
                                            node[:, 0, :, bass.ds(g, 1)].broadcast_to([P, J, P]),
                                            ALU.subtract).then_inc(dst_off, 1)
                    pool.reg_add(item, item, 1)

        @block.scalar
        def _(act):
            act.wait_ge(iota_ok, 3)
            act.wait_ge(bounds_ok, 1)
            item = act.alloc_register("item_act")
            act.reg_mov(item, 0)
            with act.Fori(0, G) as g:
                first = act.value_load(bounds[0:1, 0, bass.ds(g, 1)], min_val=0, max_val=NT - 1)
                end = act.value_load(bounds[0:1, 1, bass.ds(g, 1)], min_val=1, max_val=NT)
                with act.Fori(first, end) as t:
                    i = act.snap(item, min_val=0, max_val=G * NT)
                    slot = act.snap(i % 4)
                    act.drain()
                    act.wait_ge(dst_off, i + 1)
                    act.reg_add(item, item, 1)
                    nc.scalar.activation(far_dst[:], off_dst[:, bass.ds(slot, 1), :, :], ACT.Abs)
                    act.drain()
                    nc.scalar.activation(hot_dst[:, bass.ds(slot, 1), :, :], far_dst[:], ACT.Relu,
                                         scale=-1.0, bias=one[:]).then_inc(dst_hot, 1)

        @block.tensor
        def _(pe):
            pe.wait_ge(ident_ok, 1)
            pe.wait_ge(edges_ok, 1)
            for w in range(2):
                v = edges_f[:, w, :].rearrange("g (p j) -> g j p", j=J)
                for j in range(J):
                    last = nc.tensor.transpose(ps_node[:, w, j * G:(j + 1) * G], v[:, j, :], k.ident[0:G, 0:G])
            last.then_inc(node_ps, 1)
            pe.wait_ge(tiles_ok, 1)
            pe.wait_ge(node_ok, 1)
            for w in range(2):
                last = nc.tensor.transpose(ps_node[0:1, w, 0:G], tiles[:, w:w + 1], k.ident[0:G, 0:G])
            last.then_inc(bounds_ps, 1)
            pe.wait_ge(bounds_ok, 1)
            item = pe.alloc_register("item_pe")
            pe.reg_mov(item, 0)
            with pe.Fori(0, G // 2) as gg:
                for u in range(2):
                    g = gg * 2 + u
                    first = pe.value_load(bounds[0:1, 0, bass.ds(g, 1)], min_val=0, max_val=NT - 1)
                    end = pe.value_load(bounds[0:1, 1, bass.ds(g, 1)], min_val=1, max_val=NT)
                    with pe.Fori(first, end) as t:
                        i = pe.snap(item, min_val=0, max_val=G * NT)
                        half = pe.snap(i % 2)
                        slot = pe.snap(i % 4)
                        pe.wait_ge(acc_free, i + 1)
                        pe.wait_ge(src_hot, g + 1)
                        pe.wait_ge(dst_hot, i + 1)
                        pe.reg_add(item, item, 1)
                        for j in range(J):
                            for c0, cn in CHUNKS:
                                last = nc.tensor.matmul(acc[:, bass.ds(half, 1), c0:c0 + cn],
                                                        hot_dst[:, bass.ds(slot, 1), j, :],
                                                        hot_src[:, u, j, c0:c0 + cn],
                                                        start=(j == 0), stop=(j == J - 1))
                        last.then_inc(acc_ok, 1)
                    pe.drain().then_inc(group_done, 1)

        @block.vector
        def _(dve):
            dve.wait_ge(edges_in, 32)
            nc.vector.tensor_copy(edges_f[:], edges_i[:]).then_inc(edges_ok, 1)
            dve.drain()
            nc.vector.tensor_reduce(ends[:, 0:1], edges_f[:, 0, :], AX.X, ALU.min)
            nc.vector.tensor_reduce(ends[:, 1:2], edges_f[:, 0, :], AX.X, ALU.max)
            dve.drain()
            nc.vector.tensor_scalar(tiles[:, 0:1], ends[:, 0:1], float(P), None, ALU.is_ge)
            nc.vector.tensor_scalar(tiles[:, 1:2], ends[:, 1:2], float(P), 1.0, ALU.is_ge, ALU.add)
            for t in range(2, NT):
                dve.drain()
                last = nc.vector.scalar_tensor_tensor(out=tiles[:], in0=ends[:], scalar=float(P * t), in1=tiles[:],
                                                      op0=ALU.is_ge, op1=ALU.add)
            last.then_inc(tiles_ok, 1)
            dve.wait_ge(node_ps, 1)
            nc.vector.tensor_copy(node[:, :, :, 0:G],
                                  ps_node[:, :, 0:J * G].rearrange("p w (j g) -> p w j g", j=J)).then_inc(node_ok, 1)
            dve.wait_ge(bounds_ps, 1)
            nc.vector.tensor_copy(bounds[:], ps_node[0:1, :, 0:G]).then_inc(bounds_ok, 1)
            dve.sem_inc(acc_free, 2)
            dve.sem_inc(acc_ok, 4)
            dve.sem_inc(group_done, 1)
            dve.wait_ge(iota_ok, 3)
            dve.drain()

            def one_hots(g, buf):
                for j in range(J):
                    last = nc.vector.tensor_scalar(hot_src[:, buf, j, :], iota[:], node[:, 1, j, bass.ds(g, 1)],
                                                   None, ALU.is_equal)
                last.then_inc(src_hot, 1)

            one_hots(0, 0)
            dve.wait_ge(adj_zero, 1)
            item = dve.alloc_register("item_dve")
            dve.reg_mov(item, 0)
            with dve.Fori(0, G // 2) as gg:
                for u in range(2):
                    g = gg * 2 + u
                    dve.wait_ge(group_done, g + 1)
                    one_hots(g + 1, 1 - u)
                    first = dve.value_load(bounds[0:1, 0, bass.ds(g, 1)], min_val=0, max_val=NT - 1)
                    end = dve.value_load(bounds[0:1, 1, bass.ds(g, 1)], min_val=1, max_val=NT)
                    with dve.Fori(first, end) as t:
                        i = dve.snap(item, min_val=0, max_val=G * NT)
                        half = dve.snap(i % 2)
                        dve.wait_ge(acc_ok, i + 5)
                        nc.vector.tensor_tensor(k.adj[:, bass.ds(t, 1), :], k.adj[:, bass.ds(t, 1), :],
                                                acc[:, bass.ds(half, 1), 0:N], ALU.add).then_inc(acc_free, 1)
                        dve.reg_add(item, item, 1)
                        dve.drain()



def tile_cols(t):
    return slice(t * P, (t + 1) * P)


class Norm:

    def __init__(self, k, name, ctx):
        self.k = k
        self.stats = k.sb(f"{name}_stats", [P, NT, 6], F32, ctx)
        self.mean_var = k.sb(f"{name}_mean_var", [P, NT, 2], F32, ctx)
        self.var = k.sb(f"{name}_var", [P, NT, 1], F32, ctx)
        self.std = k.sb(f"{name}_std", [P, NT, 1], F32, ctx)
        self.rstd = k.sb(f"{name}_rstd", [P, NT, 1], F32, ctx)
        self.var_ok, self.std_ok, self.y_ok, self.yT_ps, self.yT_ok = k.norm_sems
        self.layer, self.base = k.norms, k.norms * NT
        k.norms += 1

    def vector(self, dve):
        nc, k = self.k.nc, self.k
        with dve.Fori(0, NT) as t:
            nc.vector.bn_stats(self.stats[:, bass.ds(t, 1), :], k.x[:, bass.ds(t, 1), :])
        dve.drain()
        for t in range(NT):
            nc.vector.bn_aggr(self.mean_var[:, t, :], self.stats[:, t, :])
        dve.drain()
        nc.vector.tensor_scalar(self.var[:], self.mean_var[:, :, 1:2], 1e-5, None, ALU.add).then_inc(self.var_ok, 1)
        dve.wait_ge(self.std_ok, self.layer + 1)
        nc.vector.reciprocal(self.rstd[:], self.std[:])
        dve.drain()
        with dve.Fori(0, NT) as t:
            nc.vector.tensor_scalar(k.y[:, bass.ds(t, 1), :], k.x[:, bass.ds(t, 1), :],
                                    self.mean_var[:, bass.ds(t, 1), 0], self.rstd[:, bass.ds(t, 1), 0],
                                    ALU.subtract, ALU.mult).then_inc(self.y_ok, 1)
        dve.drain()

    def scalar(self, act):
        nc, k = self.k.nc, self.k
        act.wait_ge(self.var_ok, self.layer + 1)
        nc.scalar.activation(self.std[:], self.var[:], ACT.Sqrt).then_inc(self.std_ok, 1)
        for t in range(NT):
            act.wait_ge(self.yT_ps, self.base + t + 1)
            nc.scalar.copy(k.yT[:, :, tile_cols(t)],
                           k.bank[:, 6 + t % 2, 0:KD * P].rearrange("p (f n) -> p f n", f=KD)).then_inc(self.yT_ok, 1)

    def tensor(self, pe):
        nc, k = self.k.nc, self.k
        for t in range(NT):
            pe.wait_ge(self.y_ok, self.base + t + 1)
            if t >= 2:
                pe.wait_ge(self.yT_ok, self.base + t - 1)
            for f in range(KD):
                last = nc.tensor.transpose(k.bank[:, 6 + t % 2, f * P:(f + 1) * P],
                                           k.y[:, t, f * 128:(f + 1) * 128], k.ident[0:P, 0:P])
            last.then_inc(self.yT_ps, 1)


def graph_layer(k, name, kind):
    nc, d = k.nc, k.d
    first = kind == "sage"
    with ExitStack() as ctx:
        norm = Norm(k, name, ctx)
        w_agg = k.sb(f"{name}_w_agg", [128, KD, D], F32, ctx)
        w_self = k.sb(f"{name}_w_self", [128, KD, D], F32, ctx) if kind != "residual" else None
        bias = k.sb(f"{name}_bias", [P, D], F32, ctx)
        alpha = k.sb(f"{name}_alpha", [P, 1], F32, ctx)
        h = k.sb(f"{name}_h", [P, D], F32, ctx)
        gate = k.sb(f"{name}_gate", [P, 2, D], F32, ctx)
        own = k.sb(f"{name}_own", [P, 2, D], F32, ctx)
        w_in, adjT_ps, adjT_ok, z_ps, z_ok, own_ps, own_ok, pre_ok, sum_ps, h_ok, gate_ok, done = k.graph_sems
        base, own_base, w_base = k.graphs * NT, k.graphs_own * NT, k.graphs * 48
        k.graphs += 1
        k.graphs_own += kind != "residual"
        weights = {"sage": ("L0_gnn_W_l", "L0_gnn_W_r", "L0_gnn_b"), "residual": ("L1_gnn_W_T", None, "L1_gnn_b"),
                   "sum": ("L3_gnn_wn", "L3_gnn_wc", "L3_gnn_bias")}[kind]
        by_edge = k.adj if kind == "sum" else k.adjT
        scale = k.inv_out if kind == "sum" else k.inv_in
        block = ctx.enter_context(nc.Block())

        @block.sync
        def _(sp):
            if kind == "sum":
                sp.dma_start(k.adj[:], k.adj_saved).then_inc(k.adj_in, 16)
            sp.dma_start(w_agg[:], d[weights[0]].rearrange("(f p) n -> p f n", p=128)).then_inc(w_in, 16)
            if w_self is not None:
                sp.dma_start(w_self[:], d[weights[1]].rearrange("(f p) n -> p f n", p=128)).then_inc(w_in, 16)
            else:
                sp.dma_start(alpha[:], d["L1_gnn_alpha"].partition_broadcast(P)).then_inc(w_in, 16)
            sp.dma_start(bias[:], d[weights[2]].partition_broadcast(P)).then_inc(w_in, 16)

        @block.tensor
        def _(pe):
            if first:
                for s in range(NT):
                    if s >= 2:
                        pe.wait_ge(adjT_ok, s - 1)
                    for t in range(NT):
                        last = nc.tensor.transpose(
                            k.bank[0:P, 3 * (s % 2) + t // 4, (t % 4) * P:(t % 4 + 1) * P],
                            k.adj[:, t, tile_cols(s)], k.ident[0:P, 0:P])
                    last.then_inc(adjT_ps, 1)
            norm.tensor(pe)
            pe.wait_ge(w_in, w_base + 48)
            if first:
                pe.wait_ge(adjT_ok, NT)
            for t in range(NT):
                pe.wait_ge(norm.yT_ok, norm.base + t + 1)
                if t >= 2:
                    pe.wait_ge(z_ok, base + t - 1)
                for f in range(KD):
                    last = nc.tensor.matmul(k.bank[0:P, t % 2, :], k.yT[:, f, tile_cols(t)], w_agg[:, f, :],
                                            start=(f == 0), stop=(f == KD - 1))
                last.then_inc(z_ps, 1)
            for t in range(NT):
                if w_self is not None:
                    if t >= 2:
                        pe.wait_ge(own_ok, own_base + t - 1)
                    for f in range(KD):
                        last = nc.tensor.matmul(k.bank[0:P, 4 + t % 2, :], k.yT[:, f, tile_cols(t)], w_self[:, f, :],
                                                start=(f == 0), stop=(f == KD - 1))
                    last.then_inc(own_ps, 1)
                pe.wait_ge(z_ok, base + NT)
                if kind == "sum" and t == 0:
                    pe.wait_ge(k.adj_in, 16)
                if t >= 2:
                    pe.wait_ge(h_ok, base + t - 1)
                for s in range(NT):
                    last = nc.tensor.matmul(k.bank[0:P, 2 + t % 2, :], by_edge[:, s, tile_cols(t)], k.z[0:P, s, :],
                                            start=(s == 0), stop=(s == NT - 1))
                last.then_inc(sum_ps, 1)

        @block.scalar
        def _(act):
            if first:
                for s in range(NT):
                    act.wait_ge(adjT_ps, s + 1)
                    b = 3 * (s % 2)
                    nc.scalar.copy(k.adjT[:, s, 0:8 * P].rearrange("p (b n) -> p b n", b=2),
                                   k.bank[0:P, b:b + 2, 0:4 * P])
                    nc.scalar.copy(k.adjT[:, s, 8 * P:N], k.bank[0:P, b + 2, 0:2 * P]).then_inc(adjT_ok, 1)
            norm.scalar(act)
            for t in range(NT):
                act.wait_ge(z_ps, base + t + 1)
                nc.scalar.copy(k.z[0:P, t, :], k.bank[0:P, t % 2, :]).then_inc(z_ok, 1)
            for t in range(NT):
                if w_self is not None:
                    act.wait_ge(own_ps, own_base + t + 1)
                    if t >= 2:
                        act.wait_ge(pre_ok, own_base + t - 1)
                    nc.scalar.copy(own[:, t % 2, :], k.bank[0:P, 4 + t % 2, :]).then_inc(own_ok, 1)
                if kind == "sage":
                    act.wait_ge(pre_ok, own_base + t + 1)
                    nc.scalar.activation(gate[:, t % 2, :], h[:], ACT.Sigmoid).then_inc(gate_ok, 1)

        @block.vector
        def _(dve):
            if first:
                dve.wait_ge(k.x_in, 16)
            norm.vector(dve)
            dve.wait_ge(w_in, w_base + 48)
            if first:
                nc.vector.tensor_reduce(k.degree[:, :, 0], k.adj[:], AX.X, ALU.add)
                dve.wait_ge(adjT_ok, NT)
                nc.vector.tensor_reduce(k.degree[:, :, 1], k.adjT[:], AX.X, ALU.add)
                dve.drain()
                nc.vector.tensor_scalar(k.inv_in[:], k.degree[:, :, 0:1], 1.0, None, ALU.max)
                nc.vector.reciprocal(k.inv_out[:], k.degree[:, :, 1:2])
                nc.vector.tensor_scalar(k.has_in[:], k.degree[:, :, 0:1], 0.0, None, ALU.is_gt)
                dve.drain()
                nc.vector.reciprocal(k.inv_in[:], k.inv_in[:])
                dve.drain()
            for t in range(NT):
                dve.wait_ge(sum_ps, base + t + 1)
                if w_self is not None:
                    dve.wait_ge(own_ok, own_base + t + 1)
                    nc.vector.scalar_tensor_tensor(out=h[:], in0=k.bank[0:P, 2 + t % 2, :], scalar=scale[:, t, :],
                                                   in1=own[:, t % 2, :], op0=ALU.mult, op1=ALU.add).then_inc(h_ok, 1)
                    dve.wait_ge(h_ok, base + t + 1)
                    nc.vector.tensor_tensor(h[:], h[:], bias[:], ALU.add).then_inc(pre_ok, 1)
                    dve.wait_ge(pre_ok, own_base + t + 1)
                    if kind == "sage":
                        dve.wait_ge(gate_ok, t + 1)
                        nc.vector.tensor_tensor(h[:], h[:], gate[:, t % 2, :], ALU.mult)
                        dve.drain()
                else:
                    nc.vector.scalar_tensor_tensor(out=h[:], in0=k.bank[0:P, 2 + t % 2, :], scalar=scale[:, t, :],
                                                   in1=bias[:], op0=ALU.mult, op1=ALU.add).then_inc(h_ok, 1)
                    dve.wait_ge(h_ok, base + t + 1)
                    nc.vector.scalar_tensor_tensor(out=h[:], in0=h[:], scalar=alpha[:], in1=k.y[:, t, :],
                                                   op0=ALU.mult, op1=ALU.add)
                    dve.drain()
                nc.vector.tensor_tensor(k.x[:, t, :], k.x[:, t, :], h[:], ALU.add).then_inc(done, 1)
                dve.wait_ge(done, base + t + 1)


class Router:

    def __init__(self, k, name, w_gate, b_gate, ctx, extra=0):
        self.k, self.extra, self.w_gate, self.b_gate = k, extra, w_gate, b_gate
        self.w = k.sb(f"{name}_gate_w", [128, KD, E], F32, ctx)
        self.b = k.sb(f"{name}_gate_b", [P, E], F32, ctx)
        self.logit = k.sb(f"{name}_logit", [P, NT, E], F32, ctx)
        self.best = k.sb(f"{name}_best", [P, NT], F32, ctx)
        self.rank = k.sb(f"{name}_rank", [P, NT, E], F32, ctx)
        self.share = k.sb(f"{name}_share", [P, NT, E + extra], F32, ctx)
        spare = k.y[:].rearrange("p t d -> p (t d)")
        table = NT * E * E
        self.shareT = spare[0:E + extra, 2 * table:2 * table + N]
        self.above, self.equal = (spare[:, i * table:(i + 1) * table].rearrange("p (t e o) -> p t e o", t=NT, e=E)
                                  for i in range(2))
        self.earlier = k.sb(f"{name}_earlier", [P, E, E], F32, ctx)
        self.chosen = k.sb(f"{name}_chosen", [P, NT, E], F32, ctx)
        (self.gate_in, self.earlier_ok, self.logit_ps, self.shift_ok, self.exp_ok, self.share_ok, self.shareT_ps,
         self.shareT_ok) = k.router_sems
        self.turn = k.routers
        k.routers += 1

    def sync(self, sp):
        sp.dma_start(self.w[:], self.w_gate.rearrange("(f p) e -> p f e", p=128)).then_inc(self.gate_in, 16)
        sp.dma_start(self.b[:], self.b_gate.partition_broadcast(P)).then_inc(self.gate_in, 16)

    def gpsimd(self, pool):
        nc = self.k.nc
        nc.gpsimd.memset(self.earlier[:], 1.0)
        pool.drain()
        nc.gpsimd.affine_select(out=self.earlier[:], in_=self.earlier[:], compare_op=ALU.is_gt, fill=0.0, base=0,
                                pattern=[[1, E], [-1, E]], channel_multiplier=0).then_inc(self.earlier_ok, 1)

    def tensor_logits(self, pe, norm):
        nc, k = self.k.nc, self.k
        pe.wait_ge(self.gate_in, 32 * self.turn + 32)
        pe.wait_ge(norm.yT_ok, norm.base + NT)
        for t in range(NT):
            for f in range(KD):
                last = nc.tensor.matmul(k.bank[0:P, 5, t * E:(t + 1) * E], k.yT[:, f, tile_cols(t)], self.w[:, f, :],
                                        start=(f == 0), stop=(f == KD - 1))
        last.then_inc(self.logit_ps, 1)

    def scalar_exp(self, act):
        act.wait_ge(self.shift_ok, self.turn + 1)
        self.k.nc.scalar.activation(self.logit[:], self.logit[:], ACT.Exp).then_inc(self.exp_ok, 1)

    def vector(self, dve, chosen_ok=None):
        nc, k, wide = self.k.nc, self.k, [P, NT, E, E]
        dve.wait_ge(self.logit_ps, self.turn + 1)
        dve.wait_ge(self.gate_in, 32 * self.turn + 32)
        dve.wait_ge(self.earlier_ok, self.turn + 1)
        nc.vector.tensor_tensor(self.logit[:], k.bank[0:P, 5, 0:NT * E].rearrange("p (t e) -> p t e", t=NT),
                                self.b[:].unsqueeze(1).broadcast_to([P, NT, E]), ALU.add)
        dve.drain()
        mine = self.logit[:].unsqueeze(3).broadcast_to(wide)
        other = self.logit[:].unsqueeze(2).broadcast_to(wide)
        nc.vector.tensor_tensor(self.above, other, mine, ALU.is_gt)
        nc.vector.tensor_tensor(self.equal, other, mine, ALU.is_equal)
        nc.vector.tensor_reduce(self.best[:], self.logit[:], AX.X, ALU.max)
        dve.drain()
        nc.vector.tensor_tensor(self.equal, self.equal, self.earlier[:].unsqueeze(1).broadcast_to(wide), ALU.mult)
        nc.vector.tensor_tensor(self.logit[:], self.logit[:], self.best[:].unsqueeze(2).broadcast_to([P, NT, E]),
                                ALU.subtract).then_inc(self.shift_ok, 1)
        dve.drain()
        nc.vector.tensor_tensor(self.above, self.above, self.equal, ALU.add)
        dve.drain()
        nc.vector.tensor_reduce(self.rank[:], self.above, AX.X, ALU.add)
        dve.drain()
        if chosen_ok is not None:
            nc.vector.tensor_scalar(self.chosen[:], self.rank[:], 1.5, None, ALU.is_lt).then_inc(chosen_ok, 1)
        dve.wait_ge(self.exp_ok, self.turn + 1)
        nc.vector.scalar_tensor_tensor(out=self.rank[:], in0=self.rank[:], scalar=1.5, in1=self.logit[:],
                                       op0=ALU.is_lt, op1=ALU.mult)
        dve.drain()
        nc.vector.tensor_reduce(self.best[:], self.rank[:], AX.X, ALU.add)
        dve.drain()
        nc.vector.reciprocal(self.best[:], self.best[:])
        if self.extra:
            nc.vector.memset(self.share[:, :, E:E + 1], 0.5)
        dve.drain()
        nc.vector.tensor_tensor(self.share[:, :, 0:E], self.rank[:], self.best[:].unsqueeze(2).broadcast_to([P, NT, E]),
                                ALU.mult)
        dve.drain()
        dve.sem_inc(self.share_ok, 1)

    def tensor_shares(self, pe):
        nc, k = self.k.nc, self.k
        pe.wait_ge(self.share_ok, self.turn + 1)
        for t in range(NT):
            last = nc.tensor.transpose(k.bank[0:E + self.extra, 4 + t // 4, (t % 4) * P:(t % 4 + 1) * P],
                                       self.share[:, t, :], k.ident[0:P, 0:P])
        last.then_inc(self.shareT_ps, 1)

    def scalar_shares(self, act):
        nc, k = self.k.nc, self.k
        act.wait_ge(self.shareT_ps, self.turn + 1)
        nc.scalar.copy(self.shareT[:, 0:8 * P].rearrange("p (b n) -> p b n", b=2), k.bank[0:E + self.extra, 4:6, 0:4 * P])
        nc.scalar.copy(self.shareT[:, 8 * P:N], k.bank[0:E + self.extra, 6, 0:2 * P]).then_inc(self.shareT_ok, 1)


TOKENS = [(0, 417), (417, 417), (834, N - 834)]


def routed_layer(k, name, kind):
    nc, d = k.nc, k.d
    gated = kind == "gated"
    extra = 0 if gated else 1
    FIN, FH = (16, 8) if gated else (2, 2)
    with ExitStack() as ctx:
        norm = Norm(k, name, ctx)
        pre = "L3_ffn_" if gated else "L0_ffn_"
        router = Router(k, name, d["L3_ffn_router_w" if gated else "L0_ffn_Wg"],
                        d["L3_ffn_router_b" if gated else "L0_ffn_bg"], ctx, extra)
        w1 = k.sb(f"{name}_w1", [128, 2, KD, FIN * 128], F32, ctx)
        w2 = k.sb(f"{name}_w2", [128, 2, FH, D], F32, ctx)
        b1 = k.sb(f"{name}_b1", [128, E + extra, FIN], F32, ctx)
        b1_now = k.sb(f"{name}_b1_now", [128, 2, FIN], F32, ctx)
        b2 = k.sb(f"{name}_b2", [E + extra, D], F32, ctx)
        if gated:
            hT = k.sb(f"{name}_hT", [128, FH, N], F32, ctx)
            b1_gate = k.sb(f"{name}_b1_gate", [128, E, FH], F32, ctx)
            b1_up = k.sb(f"{name}_b1_up", [128, E, FH], F32, ctx)
            sig = k.sb(f"{name}_sig", [128, 2, 417], F32, ctx)
            half = k.sb(f"{name}_half", [128, 2, 417], F32, ctx)
        else:
            hT = k.z[:].rearrange("p t d -> p (t d)")[:, 0:FH * N].rearrange("p (f n) -> p f n", f=FH)
        w1_in = [k.sem(f"{name}_w1_in{u}") for u in range(2)]
        w2_in = [k.sem(f"{name}_w2_in{u}") for u in range(2)]
        b_in, first_done = k.sem(f"{name}_b_in"), k.sem(f"{name}_first_done")
        first_ps, hidden_ok = k.sem(f"{name}_first_ps"), k.sem(f"{name}_hidden_ok")
        out_ps, out_used, bias_ok, sig_ok = (k.sem(f"{name}_{s}") for s in ("out_ps", "out_used", "bias_ok", "sig_ok"))
        added = k.sem(f"{name}_added")
        RING1, RING2 = (2, 4) if gated else (3, 4)
        STEPS = FH * 3
        block = ctx.enter_context(nc.Block())

        def view1(w):
            return w.rearrange("(f p) n -> p f n", p=128)

        @block.sync
        def _(sp):
            router.sync(sp)
            if gated:
                src1, src2 = d["L3_ffn_gate_up_proj"], d["L3_ffn_down_proj"]
            else:
                src1, src2 = d["L0_ffn_W1"], d["L0_ffn_W2"]
            src1 = src1.rearrange("e (f p) n -> p e f n", p=128)
            src2 = src2.rearrange("e (f p) n -> p e f n", p=128)
            for e in range(2):
                sp.dma_start(w1[:, e], src1[:, e]).then_inc(w1_in[e], 16)
                if e == 0:
                    sp.dma_start(b1[:, 0:E], d["L3_ffn_gate_up_proj_bias_P" if gated else "L0_ffn_b1_P"]).then_inc(b_in, 16)
                    sp.dma_start(b2[0:E], d["L3_ffn_down_proj_bias" if gated else "L0_ffn_b2"]).then_inc(b_in, 16)
                    if not gated:
                        sp.dma_start(b1[:, E:E + 1], d["L0_ffn_bs1_P"]).then_inc(b_in, 16)
                        sp.dma_start(b2[E:E + 1], d["L0_ffn_bs2"].unsqueeze(0)).then_inc(b_in, 16)
                sp.dma_start(w2[:, e], src2[:, e]).then_inc(w2_in[e], 16)
            with sp.Fori(1, E // 2) as h:
                for u in range(2):
                    e = h * 2 + u
                    sp.wait_ge(first_done, e - 1)
                    sp.dma_start(w1[:, u:u + 1], src1[:, bass.ds(e, 1)]).then_inc(w1_in[u], 16)
                    sp.wait_ge(out_ps, (e - 1) * NT)
                    sp.dma_start(w2[:, u:u + 1], src2[:, bass.ds(e, 1)]).then_inc(w2_in[u], 16)
            if not gated:
                sp.wait_ge(first_done, E - 1)
                sp.dma_start(w1[:, 0], view1(d["L0_ffn_Ws1"])).then_inc(w1_in[0], 16)
                sp.wait_ge(out_ps, (E - 1) * NT)
                sp.dma_start(w2[:, 0], view1(d["L0_ffn_Ws2"])).then_inc(w2_in[0], 16)

        @block.gpsimd
        def _(pool):
            router.gpsimd(pool)

        @block.tensor
        def _(pe):
            norm.tensor(pe)
            router.tensor_logits(pe, norm)

            def expert(e, turn, u):
                pe.wait_ge(w1_in[u], turn * 16 + 16)
                for n in range(STEPS):
                    f, (c0, cn) = n // 3, TOKENS[n % 3]
                    pe.wait_ge(hidden_ok, e * STEPS + n + 1)
                    for part in range(2 if gated else 1):
                        b = n % RING1 * (2 if gated else 1) + part
                        for kk in range(KD):
                            col = (part * FH + f) * 128
                            last = nc.tensor.matmul(k.bank[:, b, 0:cn], w1[:, u, kk, col:col + 128],
                                                    k.yT[:, kk, c0:c0 + cn], start=(kk == 0), stop=(kk == KD - 1))
                    last.then_inc(first_ps, 1)
                pe.wait_ge(hidden_ok, (e + 1) * STEPS + RING1)
                pe.wait_ge(w2_in[u], turn * 16 + 16)
                pe.sem_inc(first_done, 1)
                for t in range(NT):
                    pe.wait_ge(out_used, e * NT + t + 1)
                    for f in range(FH):
                        last = nc.tensor.matmul(k.bank[0:P, 4 + (t + 2 * u) % 4, :],
                                                hT[:, f, tile_cols(t)], w2[:, u, f, :],
                                                start=(f == 0), stop=(f == FH - 1))
                    last.then_inc(out_ps, 1)

            with pe.Fori(0, E // 2) as h:
                for u in range(2):
                    expert(h * 2 + u, h, u)
            if not gated:
                expert(E, E // 2, 0)
            pe.wait_ge(out_used, RING2 + (E + extra) * NT)
            router.tensor_shares(pe)
            pe.wait_ge(router.shareT_ok, router.turn + 1)
            pe.wait_ge(b_in, 32 if gated else 64)
            for t in range(NT):
                if t >= 2:
                    pe.wait_ge(added, t - 1)
                nc.tensor.matmul(k.bank[0:P, t % 2, :], router.shareT[:, tile_cols(t)], b2[:],
                                 start=True, stop=True).then_inc(out_ps, 1)

        @block.scalar
        def _(act):
            norm.scalar(act)
            router.scalar_exp(act)
            act.wait_ge(b_in, 32 if gated else 64)
            if gated:
                act.wait_ge(bias_ok, 1)

            def expert(e, u):
                act.drain()
                bias = b1_gate if gated else b1
                nc.scalar.copy(b1_now[:, u:u + 1, 0:FH], bias[:, bass.ds(e, 1), :])
                act.drain()
                for n in range(STEPS):
                    f, (c0, cn) = n // 3, TOKENS[n % 3]
                    act.wait_ge(first_ps, e * STEPS + n + 1)
                    if gated:
                        nc.scalar.activation(sig[:, n % 2, 0:cn], k.bank[:, n % 2 * 2, 0:cn], ACT.Sigmoid,
                                             bias=b1_now[:, u, f:f + 1], scale=1.702).then_inc(sig_ok, 1)
                    else:
                        nc.scalar.activation(hT[:, f, c0:c0 + cn], k.bank[:, n % 3, 0:cn], ACT.Relu,
                                             bias=b1_now[:, u, f:f + 1]).then_inc(hidden_ok, 1)

            with act.Fori(0, E // 2) as h:
                for u in range(2):
                    expert(h * 2 + u, u)
            if not gated:
                expert(E, 0)
            router.scalar_shares(act)

        @block.vector
        def _(dve):
            norm.vector(dve)
            router.vector(dve)
            if gated:
                dve.wait_ge(b_in, 32)
                nc.vector.tensor_scalar(b1_gate[:], b1[:, :, 0:FH], 1.702, None, ALU.mult)
                nc.vector.tensor_scalar(b1_up[:], b1[:, :, FH:FIN], 1.0, None, ALU.add)
                dve.drain()
                dve.sem_inc(bias_ok, 1)
            dve.sem_inc(hidden_ok, RING1)
            dve.sem_inc(out_used, RING2)

            def expert(e, u):
                if gated:
                    for n in range(STEPS):
                        f, (c0, cn) = n // 3, TOKENS[n % 3]
                        dve.wait_ge(sig_ok, e * STEPS + n + 1)
                        nc.vector.scalar_tensor_tensor(out=half[:, n % 2, 0:cn], in0=k.bank[:, n % 2 * 2, 0:cn],
                                                       scalar=b1[:, bass.ds(e, 1), f], in1=sig[:, n % 2, 0:cn],
                                                       op0=ALU.add, op1=ALU.mult)
                        dve.drain()
                        nc.vector.scalar_tensor_tensor(out=hT[:, f, c0:c0 + cn], in0=k.bank[:, n % 2 * 2 + 1, 0:cn],
                                                       scalar=b1_up[:, bass.ds(e, 1), f], in1=half[:, n % 2, 0:cn],
                                                       op0=ALU.add, op1=ALU.mult).then_inc(hidden_ok, 1)
                dve.drain()
                for t in range(NT):
                    dve.wait_ge(out_ps, e * NT + t + 1)
                    nc.vector.scalar_tensor_tensor(out=k.x[:, t, :], in0=k.bank[0:P, 4 + (t + 2 * u) % 4, :],
                                                   scalar=router.share[:, t, bass.ds(e, 1)], in1=k.x[:, t, :],
                                                   op0=ALU.mult, op1=ALU.add).then_inc(out_used, 1)

            with dve.Fori(0, E // 2) as h:
                for u in range(2):
                    expert(h * 2 + u, u)
            if not gated:
                expert(E, 0)
            dve.drain()
            for t in range(NT):
                dve.wait_ge(out_ps, (E + extra) * NT + t + 1)
                nc.vector.tensor_tensor(k.x[:, t, :], k.x[:, t, :], k.bank[0:P, t % 2, :], ALU.add).then_inc(added, 1)


SINKHORN, TOP = 8, N // E


def balanced_layer(k, name):
    nc, d = k.nc, k.d
    with ExitStack() as ctx:
        norm = Norm(k, name, ctx)
        w_gate = k.sb(f"{name}_w_gate", [128, KD, E], F32, ctx)
        ones = k.sb(f"{name}_ones", [P, P], F32, ctx)
        gate = k.sb(f"{name}_gate", [P, NT, E], F32, ctx)
        col = k.sb(f"{name}_col", [P, E], F32, ctx)
        row = k.sb(f"{name}_row", [P, NT], F32, ctx)
        gateT = k.sb(f"{name}_gateT", [E, N], F32, ctx)
        left = k.sb(f"{name}_left", [E, N], F32, ctx)
        top = k.sb(f"{name}_top", [E, 8], F32, ctx)
        zeros = k.sb(f"{name}_zeros", [E, N], F32, ctx)
        equal = k.sb(f"{name}_equal", [E, N], F32, ctx)
        count = k.sb(f"{name}_count", [E, N], F32, ctx)
        above = k.sb(f"{name}_above", [E, 2], F32, ctx)
        taken = k.sb(f"{name}_taken", [P, NT, E], F32, ctx)
        share = k.sb(f"{name}_share", [P, NT, E], F32, ctx)
        w = k.sb(f"{name}_w", [128, 2, KD, D], F32, ctx)
        gate_in, gate_ps, scaled = k.sem(f"{name}_gate_in"), k.sem(f"{name}_gate_ps"), k.sem(f"{name}_scaled")
        col_ps, gateT_ps, taken_ok = k.sem(f"{name}_col_ps"), k.sem(f"{name}_gateT_ps"), k.sem(f"{name}_taken_ok")
        taken_ps, out_ps, out_used = k.sem(f"{name}_taken_ps"), k.sem(f"{name}_out_ps"), k.sem(f"{name}_out_used")
        ones_ok, w_in = k.sem(f"{name}_ones_ok"), [k.sem(f"{name}_w_in{u}") for u in range(2)]
        block = ctx.enter_context(nc.Block())
        src = d["L1_ffn_experts"].rearrange("e (f p) n -> p e f n", p=128)

        @block.sync
        def _(sp):
            sp.dma_start(w_gate[:], d["L1_ffn_gate_w"].rearrange("h (f p) e -> p (h f) e", p=128)).then_inc(gate_in, 16)
            for e in range(2):
                sp.dma_start(w[:, e], src[:, e]).then_inc(w_in[e], 16)
            with sp.Fori(1, E // 2) as h:
                for u in range(2):
                    e = h * 2 + u
                    sp.wait_ge(out_ps, (e - 1) * NT)
                    sp.dma_start(w[:, u:u + 1], src[:, bass.ds(e, 1)]).then_inc(w_in[u], 16)

        @block.gpsimd
        def _(pool):
            nc.gpsimd.memset(ones[:], 1.0)
            nc.gpsimd.memset(zeros[:], 0.0).then_inc(ones_ok, 1)

        @block.scalar
        def _(act):
            norm.scalar(act)

        @block.tensor
        def _(pe):
            norm.tensor(pe)
            pe.wait_ge(gate_in, 16)
            pe.wait_ge(norm.yT_ok, norm.base + NT)
            for t in range(NT):
                for f in range(KD):
                    last = nc.tensor.matmul(k.bank[0:P, 5, t * E:(t + 1) * E], k.yT[:, f, tile_cols(t)], w_gate[:, f, :],
                                            start=(f == 0), stop=(f == KD - 1))
            last.then_inc(gate_ps, 1)
            pe.wait_ge(ones_ok, 1)
            with pe.Fori(0, SINKHORN) as i:
                pe.wait_ge(scaled, i + 1)
                nc.tensor.matmul(k.bank[0:P, 4, 0:NT * E], ones[:], gate[:].rearrange("p t e -> p (t e)"),
                                 start=True, stop=True).then_inc(col_ps, 1)
            pe.wait_ge(scaled, SINKHORN + 1)
            for t in range(NT):
                last = nc.tensor.transpose(k.bank[0:E, t // 4, (t % 4) * P:(t % 4 + 1) * P], gate[:, t, :],
                                           k.ident[0:P, 0:P])
            last.then_inc(gateT_ps, 1)
            pe.wait_ge(taken_ok, 1)
            for t in range(NT):
                last = nc.tensor.transpose(k.bank[0:P, 4, t * E:(t + 1) * E], gateT[:, tile_cols(t)], k.ident[0:E, 0:E])
            last.then_inc(taken_ps, 1)

            def expert(e, turn, u):
                pe.wait_ge(w_in[u], turn * 16 + 16)
                for t in range(NT):
                    pe.wait_ge(out_used, e * NT + t + 1)
                    for f in range(KD):
                        last = nc.tensor.matmul(k.bank[0:P, (t + 2 * u) % 4, :], k.yT[:, f, tile_cols(t)], w[:, u, f, :],
                                                start=(f == 0), stop=(f == KD - 1))
                    last.then_inc(out_ps, 1)

            with pe.Fori(0, E // 2) as h:
                for u in range(2):
                    expert(h * 2 + u, h, u)

        @block.vector
        def _(dve):
            norm.vector(dve)
            dve.wait_ge(gate_ps, 1)
            nc.vector.tensor_scalar(gate[:], k.bank[0:P, 5, 0:NT * E].rearrange("p (t e) -> p t e", t=NT), 1e-10, None,
                                    ALU.max).then_inc(scaled, 1)
            with dve.Fori(0, SINKHORN) as i:
                dve.wait_ge(col_ps, i + 1)
                nc.vector.tensor_reduce(col[:], k.bank[0:P, 4, 0:NT * E].rearrange("p (t e) -> p e t", t=NT), AX.X, ALU.add)
                dve.drain()
                nc.vector.reciprocal(col[:], col[:])
                dve.drain()
                nc.vector.tensor_tensor(gate[:], gate[:], col[:].unsqueeze(1).broadcast_to([P, NT, E]), ALU.mult)
                dve.drain()
                nc.vector.tensor_reduce(row[:], gate[:], AX.X, ALU.add)
                dve.drain()
                nc.vector.reciprocal(row[:], row[:])
                dve.drain()
                nc.vector.tensor_tensor(gate[:], gate[:], row[:].unsqueeze(2).broadcast_to([P, NT, E]),
                                        ALU.mult).then_inc(scaled, 1)
            dve.wait_ge(gateT_ps, 1)
            for c0, b, cn in ((0, 0, 4 * P), (4 * P, 1, 4 * P), (8 * P, 2, 2 * P)):
                nc.vector.tensor_copy(gateT[:, c0:c0 + cn], k.bank[0:E, b, 0:cn])
                nc.vector.tensor_copy(left[:, c0:c0 + cn], k.bank[0:E, b, 0:cn])
            dve.drain()
            with dve.Fori(0, (TOP - 1) // 8) as i:
                nc.vector.max(top[:], left[:])
                dve.drain()
                nc.vector.match_replace(left[:], top[:], left[:], -1.0)
                dve.drain()
            nc.vector.max(top[:], left[:])
            dve.drain()
            least = top[:, (TOP - 1) % 8:(TOP - 1) % 8 + 1]
            nc.vector.tensor_scalar(equal[:], gateT[:], least, None, ALU.is_equal)
            nc.vector.tensor_scalar(left[:], gateT[:], least, None, ALU.is_gt)
            dve.drain()
            nc.vector.tensor_reduce(above[:, 0:1], left[:], AX.X, ALU.add)
            dve.wait_ge(ones_ok, 1)
            nc.vector.tensor_tensor_scan(count[:], equal[:], zeros[:], 0.0, ALU.add, ALU.add)
            dve.drain()
            nc.vector.tensor_scalar(above[:, 1:2], above[:, 0:1], -1.0, float(TOP), ALU.mult, ALU.add)
            dve.drain()
            nc.vector.scalar_tensor_tensor(out=count[:], in0=count[:], scalar=above[:, 1:2], in1=equal[:],
                                           op0=ALU.is_le, op1=ALU.mult)
            dve.drain()
            nc.vector.tensor_tensor(gateT[:], count[:], left[:], ALU.add).then_inc(taken_ok, 1)
            dve.wait_ge(taken_ps, 1)
            nc.vector.tensor_copy(taken[:], k.bank[0:P, 4, 0:NT * E].rearrange("p (t e) -> p t e", t=NT))
            dve.drain()
            nc.vector.tensor_reduce(row[:], taken[:], AX.X, ALU.add)
            nc.vector.tensor_scalar(share[:], gate[:], 0.5, None, ALU.is_gt)
            dve.drain()
            nc.vector.tensor_scalar(row[:], row[:], 1.0, None, ALU.add)
            nc.vector.tensor_tensor(share[:], share[:], taken[:], ALU.mult)
            dve.drain()
            nc.vector.reciprocal(row[:], row[:])
            dve.drain()
            nc.vector.tensor_tensor(share[:], share[:], row[:].unsqueeze(2).broadcast_to([P, NT, E]), ALU.mult)
            dve.sem_inc(out_used, 4)

            def expert(e, u):
                dve.drain()
                for t in range(NT):
                    dve.wait_ge(out_ps, e * NT + t + 1)
                    nc.vector.scalar_tensor_tensor(out=k.x[:, t, :], in0=k.bank[0:P, (t + 2 * u) % 4, :],
                                                   scalar=share[:, t, bass.ds(e, 1)], in1=k.x[:, t, :],
                                                   op0=ALU.mult, op1=ALU.add).then_inc(out_used, 1)

            with dve.Fori(0, E // 2) as h:
                for u in range(2):
                    expert(h * 2 + u, u)


HEADS, DH = 8, 64
SCORE_RING = 5
PIECES = [(0, 4), (4, 7), (7, 10)]


def attention_layer(k, name):
    nc, d = k.nc, k.d
    PAIRS, STEPS = HEADS // 2, 2 * NT
    with ExitStack() as ctx:
        norm = Norm(k, name, ctx)
        qT = k.sb(f"{name}_qT", [128, PAIRS, N], F32, ctx)
        kT = k.sb(f"{name}_kT", [128, PAIRS, N], F32, ctx)
        v = k.sb(f"{name}_v", [P, NT, D], F32, ctx)
        work = k.sb(f"{name}_work", [128, KD * 3 * D], F32, ctx)
        w_qkv = work[:].rearrange("p (f n) -> p f n", f=KD)
        prob = work[0:P, 0:2 * N].rearrange("p (b n) -> p b n", b=2)
        probT = work[0:P, 2 * N:4 * N].rearrange("p (b s n) -> p b s n", b=2, s=NT)
        w_ff = qT[:].rearrange("p h n -> p (h n)")[:, 0:KD * D].rearrange("p (f n) -> p f n", f=KD)
        q_now = k.sb(f"{name}_q_now", [128, 2, N], F32, ctx)
        b_v = k.sb(f"{name}_b_v", [P, D], F32, ctx)
        b_ff = k.sb(f"{name}_b_ff", [P, D], F32, ctx)
        b_qk = k.sb(f"{name}_b_qk", [128, 12], F32, ctx)
        low = k.sb(f"{name}_low", [P, 2, 3], F32, ctx)
        den_now = k.sb(f"{name}_den_now", [P, 4, 1], F32, ctx)
        den = k.sb(f"{name}_den", [P, HEADS, NT], F32, ctx)
        msg = k.y
        spare = k.y[:].rearrange("p t d -> p (t d)")
        w_in, b_in, spilled, b_ok = (k.sem(f"{name}_{s}") for s in ("w_in", "b_in", "spilled", "b_ok"))
        floor_ok, ln_ok, mask_ok = (k.sem(f"{name}_{s}") for s in ("floor_ok", "ln_ok", "mask_ok"))
        qk_ps, qk_ok, v_ps, v_ok = (k.sem(f"{name}_{s}") for s in ("qk_ps", "qk_ok", "v_ps", "v_ok"))
        q_ok, score_ps, part_ok, prob_ok = (k.sem(f"{name}_{s}") for s in ("q_ok", "score_ps", "part_ok", "prob_ok"))
        probT_ps, probT_a, probT_v = (k.sem(f"{name}_{s}") for s in ("probT_ps", "probT_a", "probT_v"))
        pv_ps, pv_ok, msg_ok, msgT_ps, msgT_ok, ff_in, ff_ps, ff_ok = (
            k.sem(f"{name}_{s}") for s in ("pv_ps", "pv_ok", "msg_ok", "msgT_ps", "msgT_ok", "ff_in", "ff_ps", "ff_ok"))
        seen = k.sem(f"{name}_seen")
        block = ctx.enter_context(nc.Block())

        @block.sync
        def _(sp):
            sp.dma_start(k.adj_saved, k.adj[:]).then_inc(spilled, 16)
            sp.dma_start(w_qkv, d["L2_gnn_W_qkv_T"].rearrange("(f p) n -> p f n", p=128)).then_inc(w_in, 16)
            sp.dma_start(b_qk[:], d["L2_gnn_b_qkv_P"].rearrange("p a f -> p (a f)")).then_inc(b_in, 16)
            sp.dma_start(b_v[:], d["L2_gnn_b_qkv"][2 * D:3 * D].partition_broadcast(P)).then_inc(b_in, 16)
            sp.dma_start(b_ff[:], d["L2_gnn_b_ff"].partition_broadcast(P)).then_inc(b_in, 16)
            sp.wait_ge(q_ok, HEADS)
            sp.dma_start(w_ff, d["L2_gnn_W_ff_T"].rearrange("(f p) n -> p f n", p=128)).then_inc(ff_in, 16)

        @block.gpsimd
        def _(pool):
            nc.gpsimd.memset(q_now[DH:128, 0, :], 0.0)
            nc.gpsimd.memset(q_now[0:DH, 1, :], 0.0)
            pool.wait_ge(qk_ok, 24)
            for u in range(2):
                rows = slice(DH * u, DH * (u + 1))
                nc.gpsimd.tensor_copy(q_now[rows, u, :], qT[rows, 0, :]).then_inc(q_ok, 1)
            with pool.Fori(1, PAIRS) as pair:
                for u in range(2):
                    rows = slice(DH * u, DH * (u + 1))
                    pool.drain()
                    pool.wait_ge(score_ps, (pair * STEPS - NT + NT * u) * 3)
                    pool.sem_inc(seen, 1)
                    nc.gpsimd.tensor_copy(q_now[rows, u, :], qT[rows, bass.ds(pair, 1), :]).then_inc(q_ok, 1)

        @block.tensor
        def _(pe):
            norm.tensor(pe)
            pe.wait_ge(w_in, 16)
            pe.wait_ge(norm.yT_ok, norm.base + NT)
            for n in range(24):
                c0, cn = TOKENS[n % 3]
                if n >= 3:
                    pe.wait_ge(qk_ok, n - 2)
                for f in range(KD):
                    last = nc.tensor.matmul(k.bank[:, n % 3, 0:cn], w_qkv[:, f, n // 3 * 128:(n // 3 + 1) * 128],
                                            k.yT[:, f, c0:c0 + cn], start=(f == 0), stop=(f == KD - 1))
                last.then_inc(qk_ps, 1)
            for t in range(NT):
                if t >= 2:
                    pe.wait_ge(v_ok, t - 1)
                for f in range(KD):
                    last = nc.tensor.matmul(k.bank[0:P, 3 + t % 2, :], k.yT[:, f, tile_cols(t)], w_qkv[:, f, 2 * D:3 * D],
                                            start=(f == 0), stop=(f == KD - 1))
                last.then_inc(v_ps, 1)
            pe.wait_ge(qk_ok, 24)
            pe.wait_ge(v_ok, NT)

            def scores(pair, n):
                if n % NT == 0:
                    pe.wait_ge(q_ok, pair * 2 + n // NT + 1)
                for c, (c0, cn) in enumerate(TOKENS):
                    i = 3 * n + c
                    pe.wait_ge(part_ok, pair * STEPS * 3 + i + 1)
                    nc.tensor.matmul(k.bank[0:P, i % SCORE_RING, 0:cn], q_now[:, n // NT, tile_cols(n % NT)],
                                     kT[:, bass.ds(pair, 1), c0:c0 + cn], start=True, stop=True).then_inc(score_ps, 1)

            def transposes(pair, n, piece):
                if piece == 0:
                    pe.wait_ge(prob_ok, pair * STEPS + n + 1)
                i = n * 3 + piece
                if piece == 0 and n:
                    pe.wait_ge(probT_v, pair * STEPS + n)
                if piece == 1 and n:
                    pe.wait_ge(probT_a, (pair * STEPS + n) * 2)
                if piece == 2:
                    pe.wait_ge(probT_a, (pair * STEPS + n) * 2 + 1)
                first, end = PIECES[piece]
                for s in range(first, end):
                    last = nc.tensor.transpose(k.bank[0:P, 5 + i % 2, (s - first) * P:(s - first + 1) * P],
                                               prob[:, n % 2, tile_cols(s)], k.ident[0:P, 0:P])
                last.then_inc(probT_ps, 1)

            def values(pair, n):
                pe.wait_ge(probT_a, (pair * STEPS + n) * 2 + 2)
                pe.wait_ge(probT_v, pair * STEPS + n + 1)
                pe.wait_ge(pv_ok, pair * STEPS + n + 1)
                for s in range(NT):
                    last = nc.tensor.matmul(k.bank[0:P, 7, 0:DH], probT[:, n % 2, s, :],
                                            v[:, s, bass.ds(pair * 2 * DH + n // NT * DH, DH)],
                                            start=(s == 0), stop=(s == NT - 1))
                last.then_inc(pv_ps, 1)

            with pe.Fori(0, PAIRS) as pair:
                scores(pair, 0)
                for n in range(STEPS + 1):
                    if n + 1 < STEPS:
                        scores(pair, n + 1)
                    if n < STEPS:
                        transposes(pair, n, 0)
                        transposes(pair, n, 1)
                    if n >= 1:
                        values(pair, n - 1)
                    if n < STEPS:
                        transposes(pair, n, 2)
            for t in range(NT):
                pe.wait_ge(msg_ok, t + 1)
                if t >= 2:
                    pe.wait_ge(msgT_ok, t - 1)
                for f in range(KD):
                    last = nc.tensor.transpose(k.bank[:, 6 + t % 2, f * P:(f + 1) * P], msg[:, t, f * 128:(f + 1) * 128],
                                               k.ident[0:P, 0:P])
                last.then_inc(msgT_ps, 1)
            pe.wait_ge(ff_in, 16)
            for t in range(NT):
                pe.wait_ge(msgT_ok, t + 1)
                if t >= 2:
                    pe.wait_ge(ff_ok, t - 1)
                for f in range(KD):
                    last = nc.tensor.matmul(k.bank[0:P, t % 2, :], k.yT[:, f, tile_cols(t)], w_ff[:, f, :],
                                            start=(f == 0), stop=(f == KD - 1))
                last.then_inc(ff_ps, 1)

        @block.scalar
        def _(act):
            norm.scalar(act)
            act.wait_ge(b_ok, 1)
            for n in range(24):
                f, (c0, cn) = n // 3, TOKENS[n % 3]
                act.wait_ge(qk_ps, n + 1)
                out = qT if f < PAIRS else kT
                nc.scalar.activation(out[:, f % PAIRS, c0:c0 + cn], k.bank[:, n % 3, 0:cn], ACT.Identity,
                                     bias=b_qk[:, f:f + 1], scale=-DH ** -0.5 if f < PAIRS else 1.0).then_inc(qk_ok, 1)
            for t in range(NT):
                act.wait_ge(floor_ok, t + 1)
                nc.scalar.activation(spare[:, t % 4 * N:(t % 4 + 1) * N], spare[:, t % 4 * N:(t % 4 + 1) * N],
                                     ACT.Ln).then_inc(ln_ok, 1)
            with act.Fori(0, PAIRS) as pair:
                for n in range(STEPS):
                    act.wait_ge(part_ok, pair * STEPS * 3 + 3 * n + 3 + SCORE_RING)
                    nc.scalar.activation(prob[:, n % 2, :], prob[:, n % 2, :], ACT.Exp, bias=low[:, n % 2, 2:3], scale=-1.0,
                                         accum_out=den_now[:, n % 4, :]).then_inc(prob_ok, 1)
                    for piece in (0, 2):
                        act.wait_ge(probT_ps, (pair * STEPS + n) * 3 + piece + 1)
                        first, end = PIECES[piece]
                        nc.scalar.copy(probT[:, n % 2, first:end, :].rearrange("p s n -> p (s n)"),
                                       k.bank[0:P, 5 + (n * 3 + piece) % 2, 0:(end - first) * P]).then_inc(probT_a, 1)
            for t in range(NT):
                act.wait_ge(msgT_ps, t + 1)
                nc.scalar.copy(k.yT[:, :, tile_cols(t)],
                               k.bank[:, 6 + t % 2, 0:KD * P].rearrange("p (f n) -> p f n", f=KD)).then_inc(msgT_ok, 1)

        @block.vector
        def _(dve):
            norm.vector(dve)
            dve.wait_ge(b_in, 48)
            nc.vector.tensor_scalar(b_qk[:, 0:PAIRS], b_qk[:, 0:PAIRS], -DH ** -0.5, None, ALU.mult).then_inc(b_ok, 1)
            dve.wait_ge(spilled, 16)
            dve.wait_ge(norm.yT_ps, norm.base + NT)

            def floor(t):
                nc.vector.tensor_scalar(spare[:, t % 4 * N:(t % 4 + 1) * N], k.adj[:, t, :], 1.0, None,
                                        ALU.max).then_inc(floor_ok, 1)

            def values(t):
                dve.wait_ge(v_ps, t + 1)
                nc.vector.tensor_tensor(v[:, t, :], k.bank[0:P, 3 + t % 2, :], b_v[:], ALU.add).then_inc(v_ok, 1)

            for t in range(4):
                floor(t)
            for t in range(NT):
                values(t)
            for t in range(NT):
                dve.wait_ge(ln_ok, t + 1)
                nc.vector.tensor_scalar(k.adj[:, t, :], k.adj[:, t, :], 0.0, BIG, ALU.is_equal, ALU.mult)
                dve.drain()
                nc.vector.tensor_tensor(k.adj[:, t, :], k.adj[:, t, :], spare[:, t % 4 * N:(t % 4 + 1) * N],
                                        ALU.subtract)
                dve.drain()
                if t + 4 < NT:
                    floor(t + 4)
            dve.drain()
            dve.sem_inc(part_ok, SCORE_RING)
            dve.sem_inc(pv_ok, 1)

            def minima(pair, n):
                for c, (c0, cn) in enumerate(TOKENS):
                    i = 3 * n + c
                    dve.wait_ge(score_ps, pair * STEPS * 3 + i + 1)
                    dve.sem_inc(seen, 1)
                    nc.vector.tensor_tensor_reduce(out=prob[:, n % 2, c0:c0 + cn], in0=k.bank[0:P, i % SCORE_RING, 0:cn],
                                                   in1=k.adj[:, n % NT, c0:c0 + cn], scale=1.0,
                                                   scalar=low[:, n % 2, c - 1:c] if c else 3.0 * BIG,
                                                   op0=ALU.add, op1=ALU.min, accum_out=low[:, n % 2, c:c + 1])
                    dve.drain()
                    dve.sem_inc(part_ok, 1)

            def piece(pair, n):
                dve.wait_ge(probT_ps, (pair * STEPS + n) * 3 + 2)
                first, end = PIECES[1]
                nc.vector.tensor_copy(probT[:, n % 2, first:end, :].rearrange("p s n -> p (s n)"),
                                      k.bank[0:P, 5 + (n * 3 + 1) % 2, 0:(end - first) * P]).then_inc(probT_v, 1)

            def sums(pair, n):
                dve.wait_ge(pv_ps, pair * STEPS + n + 1)
                nc.vector.tensor_copy(msg[:, n % NT, bass.ds(pair * 2 * DH + n // NT * DH, DH)],
                                      k.bank[0:P, 7, 0:DH]).then_inc(pv_ok, 1)
                nc.vector.tensor_copy(den[:, bass.ds(pair * 2 + n // NT, 1), n % NT:n % NT + 1], den_now[:, n % 4, :])

            with dve.Fori(0, PAIRS) as pair:
                for n in range(STEPS + 2):
                    if n < STEPS:
                        minima(pair, n)
                    if 1 <= n <= STEPS:
                        piece(pair, n - 1)
                    if n >= 2:
                        sums(pair, n - 2)
                dve.drain()
            nc.vector.reciprocal(den[:], den[:])
            dve.drain()
            nc.vector.tensor_tensor(den[:], den[:], k.has_in[:, :, 0].unsqueeze(1).broadcast_to([P, HEADS, NT]), ALU.mult)
            dve.drain()
            for t in range(NT):
                row = msg[:, t, :].rearrange("p (h c) -> p h c", h=HEADS)
                nc.vector.tensor_tensor(row, row, den[:, :, t:t + 1].broadcast_to([P, HEADS, DH]),
                                        ALU.mult).then_inc(msg_ok, 1)
            for t in range(NT):
                nc.vector.tensor_tensor(k.x[:, t, :], k.x[:, t, :], b_ff[:], ALU.add)
            for t in range(NT):
                dve.drain() if t == 0 else None
                dve.wait_ge(ff_ps, t + 1)
                nc.vector.tensor_tensor(k.x[:, t, :], k.x[:, t, :], k.bank[0:P, t % 2, :], ALU.add).then_inc(ff_ok, 1)


F2 = 256


def merged_layer(k, name):
    nc, d = k.nc, k.d
    TABLE = KD * F2
    with ExitStack() as ctx:
        norm = Norm(k, name, ctx)
        w_g1 = k.sb(f"{name}_w_g1", [128, KD, D], F32, ctx)
        b_g1 = k.sb(f"{name}_b_g1", [128, KD], F32, ctx)
        w_g2 = k.sb(f"{name}_w_g2", [128, KD, E], F32, ctx)
        b_g2 = k.sb(f"{name}_b_g2", [128, E], F32, ctx)
        b_g2_col = k.sb(f"{name}_b_g2_col", [E, 1], F32, ctx)
        tv1 = k.sb(f"{name}_tv1", [128, 2, KD, F2], F32, ctx)
        tv2 = k.sb(f"{name}_tv2", [128, 2, F2 // 128, D], F32, ctx)
        w1 = k.sb(f"{name}_w1", [128, KD, F2], F32, ctx)
        w2 = k.sb(f"{name}_w2", [128, F2 // 128, D], F32, ctx)
        b1 = k.sb(f"{name}_b1", [128, 2], F32, ctx)
        tv_b1 = k.sb(f"{name}_tv_b1", [128, E, 2], F32, ctx)
        rows = k.sb(f"{name}_rows", [E + 1, 3, D], F32, ctx)
        coef = k.sb(f"{name}_coef", [E + 1, 2, P], F32, ctx)
        zero = k.sb(f"{name}_zero", [128, 417], F32, ctx)
        hidden = k.sb(f"{name}_hidden", [128, 2, 417], F32, ctx)
        part = k.sb(f"{name}_part", [128, KD, 3], F32, ctx)
        mean_h = k.sb(f"{name}_mean_h", [128, KD], F32, ctx)
        mean_wide = k.sb(f"{name}_mean_wide", [128, KD, 128], F32, ctx)
        g = k.sb(f"{name}_g", [128, E], F32, ctx)
        norm_g = k.sb(f"{name}_norm_g", [P, 2, D], F32, ctx)
        hT = k.sb(f"{name}_hT", [128, 2, N], F32, ctx)
        res = k.sb(f"{name}_res", [P, NT, D], F32, ctx)
        stats = k.sb(f"{name}_stats2", [P, NT, 6], F32, ctx)
        mv = k.sb(f"{name}_mv2", [P, NT, 2], F32, ctx)
        rstd = k.sb(f"{name}_rstd2", [P, NT, 1], F32, ctx)
        w_in, small_in, tv_in = k.sem(f"{name}_w_in"), k.sem(f"{name}_small_in"), [k.sem(f"{name}_tv_in{u}") for u in range(2)]
        coef_ok, gate_ps, gate_ok, mean_ok, g_ps, g_ok = (
            k.sem(f"{name}_{s}") for s in ("coef_ok", "gate_ps", "gate_ok", "mean_ok", "g_ps", "g_ok"))
        merged, coef8_ok, w1_ok, w2_ok, norm_ps = (
            k.sem(f"{name}_{s}") for s in ("merged", "coef8_ok", "w1_ok", "w2_ok", "norm_ps"))
        h_ps, h_ok, out_ps, out_used, var_ok, std_ok = (
            k.sem(f"{name}_{s}") for s in ("h_ps", "h_ok", "out_ps", "out_used", "res_var_ok", "res_std_ok"))
        block = ctx.enter_context(nc.Block())
        src1 = d["L2_ffn_tv_W1_T"].rearrange("e (f p) n -> p e f n", p=128)
        src2 = d["L2_ffn_tv_W2_T"].rearrange("e (f p) n -> p e f n", p=128)

        @block.sync
        def _(sp):
            sp.dma_start(w_g1[:], d["L2_ffn_gfc1_w_T"].rearrange("(f p) n -> p f n", p=128)).then_inc(w_in, 16)
            sp.dma_start(w_g2[:], d["L2_ffn_gfc2_w_T"].rearrange("(f p) n -> p f n", p=128)).then_inc(w_in, 16)
            sp.dma_start(w1[:], d["L2_ffn_W1_T"].rearrange("(f p) n -> p f n", p=128)).then_inc(w_in, 16)
            sp.dma_start(w2[:], d["L2_ffn_W2_T"].rearrange("(f p) n -> p f n", p=128)).then_inc(w_in, 16)
            sp.dma_start(b_g1[:], d["L2_ffn_gfc1_b_P"].rearrange("p a f -> p (a f)")).then_inc(small_in, 16)
            sp.dma_start(b_g2[:], d["L2_ffn_gfc2_b"].partition_broadcast(128)).then_inc(small_in, 16)
            sp.dma_start(b_g2_col[:], d["L2_ffn_gfc2_b"].unsqueeze(1)).then_inc(small_in, 16)
            sp.dma_start(b1[:], d["L2_ffn_b1_P"].rearrange("p a f -> p (a f)")).then_inc(small_in, 16)
            sp.dma_start(tv_b1[:], d["L2_ffn_tv_b1_P"]).then_inc(small_in, 16)
            for i, (tables, shared) in enumerate((("tv_b2", "b2"), ("tv_ln_g", "ln_g"), ("tv_ln_b", "ln_b"))):
                sp.dma_start(rows[0:E, i, :], d[f"L2_ffn_{tables}"]).then_inc(small_in, 16)
                sp.dma_start(rows[E:E + 1, i, :], d[f"L2_ffn_{shared}"].unsqueeze(0)).then_inc(small_in, 16)
            for e in range(E):
                if e >= 2:
                    sp.wait_ge(merged, 2 * e - 2)
                sp.dma_start(tv1[:, e % 2], src1[:, e]).then_inc(tv_in[e % 2], 16)
                sp.dma_start(tv2[:, e % 2], src2[:, e]).then_inc(tv_in[e % 2], 16)

        @block.gpsimd
        def _(pool):
            nc.gpsimd.memset(coef[:, 0, :], 1.0)
            nc.gpsimd.memset(coef[:, 1, :], 1.0 - E * 0.03)
            nc.gpsimd.memset(zero[:], 0.0)
            pool.drain()
            nc.gpsimd.memset(coef[0:E, 1, :], 0.03).then_inc(coef_ok, 1)

        @block.tensor
        def _(pe):
            pe.wait_ge(coef_ok, 1)
            pe.wait_ge(small_in, 16 * 11)
            for i in range(2):
                last = nc.tensor.matmul(k.bank[0:P, 3 + i, :], coef[:, 1, :], rows[:, 1 + i, :], start=True, stop=True)
            last.then_inc(norm_ps, 1)
            norm.tensor(pe)
            pe.wait_ge(w_in, 64)
            pe.wait_ge(norm.yT_ok, norm.base + NT)
            for n in range(12):
                f, (c0, cn) = n // 3, TOKENS[n % 3]
                if n >= 3:
                    pe.wait_ge(gate_ok, n - 2)
                for kk in range(KD):
                    last = nc.tensor.matmul(k.bank[:, n % 3, 0:cn], w_g1[:, kk, f * 128:(f + 1) * 128],
                                            k.yT[:, kk, c0:c0 + cn], start=(kk == 0), stop=(kk == KD - 1))
                last.then_inc(gate_ps, 1)
            pe.wait_ge(mean_ok, 1)
            for f in range(KD):
                nc.tensor.matmul(k.bank[:, 0, 0:E], mean_wide[:, f, :], w_g2[:, f, :], start=(f == 0), stop=(f == KD - 1))
            for f in range(KD):
                last = nc.tensor.matmul(k.bank[0:E, 1, 0:P], w_g2[:, f, :], mean_wide[:, f, 0:P],
                                        start=(f == 0), stop=(f == KD - 1))
            last.then_inc(g_ps, 1)
            pe.wait_ge(w1_ok, 1)
            for n in range(6):
                f, (c0, cn) = n // 3, TOKENS[n % 3]
                if n >= 3:
                    pe.wait_ge(h_ok, n - 2)
                for kk in range(KD):
                    last = nc.tensor.matmul(k.bank[:, n % 3, 0:cn], w1[:, kk, f * 128:(f + 1) * 128],
                                            k.yT[:, kk, c0:c0 + cn], start=(kk == 0), stop=(kk == KD - 1))
                last.then_inc(h_ps, 1)
            pe.wait_ge(h_ok, 6)
            pe.wait_ge(w2_ok, 1)
            for t in range(NT):
                if t >= 4:
                    pe.wait_ge(out_used, t - 3)
                nc.tensor.matmul(k.bank[0:P, 4 + t % 4, :], coef[:, 0, :], rows[:, 0, :], start=True, stop=False)
                for f in range(2):
                    last = nc.tensor.matmul(k.bank[0:P, 4 + t % 4, :], hT[:, f, tile_cols(t)], w2[:, f, :],
                                            start=False, stop=(f == 1))
                last.then_inc(out_ps, 1)

        @block.scalar
        def _(act):
            norm.scalar(act)
            act.wait_ge(small_in, 16 * 11)
            for n in range(12):
                f, (c0, cn) = n // 3, TOKENS[n % 3]
                act.wait_ge(gate_ps, n + 1)
                if n >= 2:
                    act.wait_ge(gate_ok, n - 1)
                nc.scalar.activation(hidden[:, n % 2, 0:cn], k.bank[:, n % 3, 0:cn], ACT.Relu, bias=b_g1[:, f:f + 1],
                                     accum_out=part[:, f, n % 3:n % 3 + 1]).then_inc(gate_ok, 1)
            act.drain()
            act.sem_inc(gate_ok, 1)
            act.wait_ge(w1_ok, 1)
            for n in range(6):
                f, (c0, cn) = n // 3, TOKENS[n % 3]
                act.wait_ge(h_ps, n + 1)
                nc.scalar.activation(hT[:, f, c0:c0 + cn], k.bank[:, n % 3, 0:cn], ACT.Relu,
                                     bias=b1[:, f:f + 1]).then_inc(h_ok, 1)
            act.wait_ge(var_ok, 1)
            nc.scalar.activation(rstd[:], rstd[:], ACT.Sqrt).then_inc(std_ok, 1)

        @block.vector
        def _(dve):
            norm.vector(dve)
            dve.wait_ge(norm_ps, 1)
            nc.vector.tensor_copy(norm_g[:], k.bank[0:P, 3:5, :])
            dve.wait_ge(gate_ok, 13)
            nc.vector.tensor_reduce(mean_h[:], part[:], AX.X, ALU.add)
            dve.drain()
            nc.vector.tensor_scalar(mean_h[:], mean_h[:], 1.0 / N, None, ALU.mult)
            dve.drain()
            nc.vector.tensor_copy(mean_wide[:], mean_h[:].unsqueeze(2).broadcast_to([128, KD, 128])).then_inc(mean_ok, 1)
            dve.wait_ge(g_ps, 1)
            dve.wait_ge(small_in, 16 * 11)
            nc.vector.tensor_tensor(g[:], k.bank[:, 0, 0:E], b_g2[:], ALU.add)
            nc.vector.tensor_scalar(coef[0:E, 0, :], k.bank[0:E, 1, 0:P], b_g2_col[:], None, ALU.add)
            dve.drain()
            dve.wait_ge(w_in, 64)
            for e in range(E):
                dve.wait_ge(tv_in[e % 2], 32 * (e // 2 + 1))
                nc.vector.scalar_tensor_tensor(out=w1[:], in0=tv1[:, e % 2], scalar=g[:, e:e + 1], in1=w1[:],
                                               op0=ALU.mult, op1=ALU.add).then_inc(merged, 1)
                nc.vector.scalar_tensor_tensor(out=b1[:], in0=tv_b1[:, e, :], scalar=g[:, e:e + 1], in1=b1[:],
                                               op0=ALU.mult, op1=ALU.add)
                if e == E - 1:
                    dve.drain()
                    dve.sem_inc(w1_ok, 1)
                nc.vector.scalar_tensor_tensor(out=w2[:], in0=tv2[:, e % 2], scalar=g[:, e:e + 1], in1=w2[:],
                                               op0=ALU.mult, op1=ALU.add).then_inc(merged, 1)
                dve.drain()
            dve.sem_inc(w2_ok, 1)
            for t in range(NT):
                dve.wait_ge(out_ps, t + 1)
                nc.vector.tensor_tensor(res[:, t, :], k.y[:, t, :], k.bank[0:P, 4 + t % 4, :], ALU.add).then_inc(out_used, 1)
                dve.wait_ge(out_used, t + 1)
                nc.vector.bn_stats(stats[:, t, :], res[:, t, :])
                dve.drain()
                nc.vector.bn_aggr(mv[:, t, :], stats[:, t, :])
            dve.drain()
            nc.vector.tensor_scalar(rstd[:], mv[:, :, 1:2], 1e-5, None, ALU.add).then_inc(var_ok, 1)
            dve.wait_ge(std_ok, 1)
            nc.vector.reciprocal(rstd[:], rstd[:])
            dve.drain()
            with dve.Fori(0, NT) as t:
                now = res[:, bass.ds(t, 1), :]
                nc.vector.tensor_scalar(now, now, mv[:, bass.ds(t, 1), 0], rstd[:, bass.ds(t, 1), 0],
                                        ALU.subtract, ALU.mult)
                dve.drain()
                nc.vector.tensor_tensor(now, now, norm_g[:, 0:1, :], ALU.mult)
                nc.vector.tensor_tensor(k.x[:, bass.ds(t, 1), :], k.x[:, bass.ds(t, 1), :], norm_g[:, 1:2, :], ALU.add)
                dve.drain()
                nc.vector.tensor_tensor(k.x[:, bass.ds(t, 1), :], k.x[:, bass.ds(t, 1), :], now, ALU.add)


SLOTS = 128
ITEMS = (2 * N + E * (SLOTS - 1)) // SLOTS


class Dispatch:

    def __init__(self, k, name, ctx):
        self.k = k
        wide = [P, NT, E]
        self.before = k.sb(f"{name}_before", [P, P], F32, ctx)
        self.ones = k.sb(f"{name}_ones", [P, P], F32, ctx)
        self.total = k.sb(f"{name}_total", wide, F32, ctx)
        self.pos = k.sb(f"{name}_pos", wide, F32, ctx)
        self.items = k.sb(f"{name}_items", [P, E], F32, ctx)
        self.first = k.sb(f"{name}_first", [P, E + 1], F32, ctx)
        self.nth = k.sb(f"{name}_nth", wide, F32, ctx)
        self.pick = k.sb(f"{name}_pick", [P, 2, NT, E], F32, ctx)
        self.slot_f = k.sb(f"{name}_slot_f", [P, 2, NT], F32, ctx)
        self.slot_of = k.sb(f"{name}_slot_of", [P, 2, NT], I32, ctx)
        self.pair = k.sb(f"{name}_pair", [P, 2, NT, 2], F32, ctx)
        self.first_item = k.sb(f"{name}_first_item", [1, E + 1], I32, ctx)
        self.rows = k.sb(f"{name}_list_rows", [ITEMS + 2, SLOTS, 2], F32, ctx)
        self.nodes = k.sb(f"{name}_nodes", [SLOTS, ITEMS + 2], I32, ctx)
        self.shares = k.sb(f"{name}_shares", [SLOTS, ITEMS + 2], F32, ctx)
        (self.const_ok, self.chosen_ok, self.count_ps, self.slots_ok, self.cleared, self.listed, self.list_in,
         self.list_ps, self.list_ok) = (
            k.sem(f"{name}_{s}") for s in ("const_ok", "chosen_ok", "count_ps", "slots_ok", "cleared", "listed",
                                           "list_in", "list_ps", "list_ok"))

    def gpsimd_constants(self, pool):
        nc, k = self.k.nc, self.k
        nc.gpsimd.memset(self.before[:], 1.0)
        nc.gpsimd.memset(self.ones[:], 1.0)
        nc.gpsimd.memset(self.rows[:], 0.0)
        pool.drain()
        nc.gpsimd.affine_select(out=self.before[:], in_=self.before[:], compare_op=ALU.is_gt, fill=0.0, base=0,
                                pattern=[[1, P]], channel_multiplier=-1)
        nc.gpsimd.iota(self.rows[:, :, 0], pattern=[[1, SLOTS]], base=N, channel_multiplier=0,
                       allow_small_or_imprecise_dtypes=True)
        for kth in range(2):
            nc.gpsimd.iota(self.pair[:, kth, :, 0], pattern=[[P, NT]], base=0, channel_multiplier=1,
                           allow_small_or_imprecise_dtypes=True)
        pool.drain()
        pool.sem_inc(self.const_ok, 1)
        nc.gpsimd.dma_start(k.slot_list.rearrange("(i s) a -> i s a", s=SLOTS), self.rows[:]).then_inc(self.cleared, 16)

    def gpsimd_list(self, pool):
        nc, k = self.k.nc, self.k
        pool.wait_ge(self.cleared, 16)
        pool.wait_ge(self.slots_ok, 1)
        for kth in range(2):
            for t in range(NT):
                nc.gpsimd.indirect_dma_start(
                    k.slot_list, bass.IndirectOffsetOnAxis(ap=self.slot_of[:, kth, t:t + 1], axis=0),
                    self.pair[:, kth, t, :], None).then_inc(self.listed, 16)
        pool.wait_ge(self.listed, 2 * NT * 16)
        nc.gpsimd.dma_start(self.rows[:], k.slot_list.rearrange("(i s) a -> i s a", s=SLOTS)).then_inc(self.list_in, 16)

    def tensor_counts(self, pe, chosen):
        nc, k = self.k.nc, self.k
        pe.wait_ge(self.const_ok, 1)
        pe.wait_ge(self.chosen_ok, 1)
        flat = chosen.rearrange("p t e -> p (t e)")
        nc.tensor.matmul(k.bank[0:P, 0, 0:NT * E], self.before[:], flat, start=True, stop=True)
        nc.tensor.matmul(k.bank[0:P, 1, 0:NT * E], self.ones[:], flat, start=True, stop=True).then_inc(self.count_ps, 1)

    def tensor_list(self, pe):
        nc, k = self.k.nc, self.k
        pe.wait_ge(self.list_in, 16)
        for a in range(2):
            last = nc.tensor.transpose(k.bank[0:SLOTS, a, 0:ITEMS + 2], self.rows[:, :, a],
                                       k.ident[0:ITEMS + 2, 0:ITEMS + 2])
        last.then_inc(self.list_ps, 1)

    def vector_slots(self, dve, chosen, share, earlier, scratch):
        nc, k = self.k.nc, self.k
        nc.vector.tensor_tensor(scratch, chosen.unsqueeze(2).broadcast_to([P, NT, E, E]),
                                earlier.unsqueeze(1).broadcast_to([P, NT, E, E]), ALU.mult)
        dve.wait_ge(self.count_ps, 1)
        nc.vector.tensor_copy(self.total[:], k.bank[0:P, 1, 0:NT * E].rearrange("p (t e) -> p t e", t=NT))
        nc.vector.tensor_copy(self.pos[:], k.bank[0:P, 0, 0:NT * E].rearrange("p (t e) -> p t e", t=NT))
        dve.drain()
        nc.vector.tensor_reduce(self.nth[:], scratch, AX.X, ALU.add)
        for t in range(1, NT):
            nc.vector.tensor_tensor(self.total[:, t, :], self.total[:, t, :], self.total[:, t - 1, :], ALU.add)
            dve.drain()
        nc.vector.tensor_tensor(self.pos[:, 1:NT, :], self.pos[:, 1:NT, :], self.total[:, 0:NT - 1, :], ALU.add)
        nc.vector.tensor_scalar(self.items[:], self.total[:, NT - 1, :], float(SLOTS), 1.0, ALU.is_gt, ALU.add)
        nc.vector.memset(self.first[:], 0.0)
        for j in range(2, -(-N // SLOTS)):
            dve.drain()
            nc.vector.scalar_tensor_tensor(out=self.items[:], in0=self.total[:, NT - 1, :], scalar=float(SLOTS * j),
                                           in1=self.items[:], op0=ALU.is_gt, op1=ALU.add)
        for e in range(E):
            dve.drain()
            nc.vector.tensor_tensor(self.first[:, e + 1:e + 2], self.first[:, e:e + 1], self.items[:, e:e + 1], ALU.add)
        dve.drain()
        nc.vector.tensor_copy(self.first_item[:], self.first[0:1, :])
        nc.vector.tensor_scalar(self.items[:], self.first[:, 0:E], float(SLOTS), None, ALU.mult)
        for kth in range(2):
            nc.vector.scalar_tensor_tensor(out=self.pick[:, kth], in0=self.nth[:], scalar=float(kth), in1=chosen,
                                           op0=ALU.is_equal, op1=ALU.mult)
        dve.drain()
        nc.vector.tensor_tensor(self.pos[:], self.pos[:], self.items[:].unsqueeze(1).broadcast_to([P, NT, E]), ALU.add)
        dve.drain()
        for kth in range(2):
            nc.vector.tensor_tensor(scratch[:, :, kth, :], self.pick[:, kth], self.pos[:], ALU.mult)
            nc.vector.tensor_tensor(scratch[:, :, 2 + kth, :], self.pick[:, kth], share, ALU.mult)
        dve.wait_ge(self.const_ok, 1)
        dve.drain()
        for kth in range(2):
            nc.vector.tensor_reduce(self.slot_f[:, kth, :], scratch[:, :, kth, :], AX.X, ALU.add)
            nc.vector.tensor_reduce(self.pair[:, kth, :, 1], scratch[:, :, 2 + kth, :], AX.X, ALU.add)
        dve.drain()
        nc.vector.tensor_copy(self.slot_of[:], self.slot_f[:])
        dve.drain()
        dve.sem_inc(self.slots_ok, 1)

    def vector_list(self, dve):
        nc, k = self.k.nc, self.k
        dve.wait_ge(self.list_ps, 1)
        nc.vector.tensor_copy(self.nodes[:], k.bank[0:SLOTS, 0, 0:ITEMS + 2])
        nc.vector.tensor_copy(self.shares[:], k.bank[0:SLOTS, 1, 0:ITEMS + 2])
        dve.drain()
        dve.sem_inc(self.list_ok, 1)

    def range(self, eng, e):
        first = eng.value_load(self.first_item[0:1, bass.ds(e, 1)], min_val=0, max_val=ITEMS - 1)
        end = eng.value_load(self.first_item[0:1, bass.ds(e + 1, 1)], min_val=1, max_val=ITEMS)
        return first, end


def top_two_layer(k, name):
    nc, d = k.nc, k.d
    H = 1024
    FH = H // 128
    with ExitStack() as ctx:
        norm = Norm(k, name, ctx)
        router = Router(k, name, d["L3_ffn_router_w"], d["L3_ffn_router_b"], ctx)
        disp = Dispatch(k, name, ctx)
        w1 = k.sb(f"{name}_w1", [128, 2, KD, 2 * H], F32, ctx)
        w2 = k.sb(f"{name}_w2", [128, 2, FH, D], F32, ctx)
        b1 = k.sb(f"{name}_b1", [128, 2, 2 * H], F32, ctx)
        b2 = k.sb(f"{name}_b2", [E, D], F32, ctx)
        rows = k.sb(f"{name}_rows", [SLOTS, D], F32, ctx)
        rowsT = k.sb(f"{name}_rowsT", [128, KD, SLOTS], F32, ctx)
        now_in = k.sb(f"{name}_now_in", [SLOTS, 1], I32, ctx)
        now_out = k.sb(f"{name}_now_out", [SLOTS, 1], I32, ctx)
        gate = k.sb(f"{name}_gate", [SLOTS, 2, 512], F32, ctx)
        sig = k.sb(f"{name}_sig", [SLOTS, 2, 512], F32, ctx)
        hid = k.sb(f"{name}_hid", [SLOTS, 2, 512], F32, ctx)
        hT = k.sb(f"{name}_hT", [128, FH, SLOTS], F32, ctx)
        out = k.sb(f"{name}_out", [SLOTS, D], F32, ctx)
        y_out, spare_out, x_out, w_in, b_in, b2_in, out_done = (
            k.sem(f"{name}_{s}") for s in ("y_out", "spare_out", "x_out", "w_in", "b_in", "b2_in", "out_done"))
        rows_in, rows_ps, rowsT_ok, seen, items_done = (
            k.sem(f"{name}_{s}") for s in ("rows_in", "rows_ps", "rowsT_ok", "seen", "items_done"))
        gate_ps, up_ps, gate_ok, sig_ok, hid_ok, hT_ps, hT_ok = (
            k.sem(f"{name}_{s}") for s in ("gate_ps", "up_ps", "gate_ok", "sig_ok", "hid_ok", "hT_ps", "hT_ok"))
        out_ok, out_free, summed, bias_ps, bias_added = (
            k.sem(f"{name}_{s}") for s in ("out_ok", "out_free", "summed", "bias_ps", "bias_added"))
        block = ctx.enter_context(nc.Block())
        src1 = d["L3_ffn_gate_up_proj"].rearrange("e (f p) n -> p e f n", p=128)
        src2 = d["L3_ffn_down_proj"].rearrange("e (f p) n -> p e f n", p=128)
        src_b = d["L3_ffn_gate_up_proj_bias"].rearrange("(a e) n -> a e n", a=1)

        @block.sync
        def _(sp):
            router.sync(sp)
            sp.dma_start(b2[:], d["L3_ffn_down_proj_bias"]).then_inc(b2_in, 16)
            for e in range(2):
                if e:
                    sp.wait_ge(w_in, 32)
                    sp.wait_ge(b_in, 16)
                    sp.wait_ge(norm.y_ok, norm.base + NT)
                    sp.dma_start(k.y_rows[0:N].rearrange("(t p) d -> p t d", p=P), k.y[:]).then_inc(y_out, 16)
                sp.dma_start(w1[:, e], src1[:, e]).then_inc(w_in, 16)
                sp.dma_start(w2[:, e], src2[:, e]).then_inc(w_in, 16)
                sp.dma_start(b1[:, e, :], src_b[0, e].partition_broadcast(128)).then_inc(b_in, 16)
            sp.wait_ge(bias_added, NT)
            sp.dma_start(k.sums[0:N].rearrange("(t p) d -> p t d", p=P), k.x[:]).then_inc(x_out, 16)
            sp.wait_ge(disp.slots_ok, 1)
            with sp.Fori(0, E // 2 - 1) as h:
                for u in range(2):
                    e = h * 2 + u
                    end = sp.value_load(disp.first_item[0:1, bass.ds(e + 1, 1)], min_val=1, max_val=ITEMS)
                    sp.wait_ge(w_in, e * 32 + 64)
                    sp.wait_ge(b_in, e * 16 + 32)
                    sp.wait_ge(items_done, end)
                    sp.dma_start(w1[:, u:u + 1], src1[:, bass.ds(e + 2, 1)]).then_inc(w_in, 16)
                    sp.dma_start(w2[:, u:u + 1], src2[:, bass.ds(e + 2, 1)]).then_inc(w_in, 16)
                    sp.dma_start(b1[:, u:u + 1, :], src_b[:, bass.ds(e + 2, 1), :].broadcast_to([128, 1, 2 * H])).then_inc(b_in, 16)
            sp.wait_ge(out_done, 1)
            sp.dma_start(d["out"], k.sums[0:N]).then_inc(out_done, 16)
            sp.wait_ge(out_done, 17)

        @block.gpsimd
        def _(pool):
            router.gpsimd(pool)
            disp.gpsimd_constants(pool)
            nc.gpsimd.memset(out[:], 0.0)
            pool.drain()
            nc.gpsimd.dma_start(k.y_rows[N:N + SLOTS], out[:]).then_inc(spare_out, 16)
            nc.gpsimd.dma_start(k.sums[N:N + SLOTS], out[:]).then_inc(spare_out, 16)
            disp.gpsimd_list(pool)

            def gather():
                nc.gpsimd.indirect_dma_start(rows[:], None, k.y_rows,
                                             bass.IndirectOffsetOnAxis(ap=now_in[:], axis=0)).then_inc(rows_in, 16)

            pool.wait_ge(disp.list_ok, 1)
            pool.wait_ge(y_out, 16)
            pool.wait_ge(spare_out, 32)
            nc.gpsimd.tensor_copy(now_in[:], disp.nodes[:, 0:1])
            pool.drain()
            gather()
            pool.wait_ge(rows_ps, 1)
            nc.gpsimd.tensor_copy(now_in[:], disp.nodes[:, 1:2])
            pool.drain()
            gather()
            pool.wait_ge(x_out, 16)
            with pool.Fori(0, E) as e:
                first, end = disp.range(pool, e)
                with pool.Fori(first, end) as i:
                    pool.wait_ge(rows_in, i * 16 + 32)
                    pool.wait_ge(rows_ps, i + 2)
                    pool.sem_inc(seen, 1)
                    nc.gpsimd.tensor_copy(now_in[:], disp.nodes[:, bass.ds(i + 2, 1)])
                    nc.gpsimd.tensor_copy(now_out[:], disp.nodes[:, bass.ds(i, 1)])
                    pool.drain()
                    gather()
                    pool.wait_ge(out_ok, i + 2)
                    pool.sem_inc(seen, 1)
                    nc.gpsimd.indirect_dma_start(
                        k.sums, bass.IndirectOffsetOnAxis(ap=now_out[:], axis=0), out[:], None,
                        compute_op=ALU.add).then_inc(summed, 16)
                    pool.wait_ge(summed, i * 16 + 16)
                    pool.sem_inc(out_free, 1)
            items = pool.value_load(disp.first_item[0:1, E:E + 1], min_val=1, max_val=ITEMS)
            pool.wait_ge(rows_in, items * 16 + 32)
            pool.sem_inc(out_done, 1)

        @block.tensor
        def _(pe):
            norm.tensor(pe)
            router.tensor_logits(pe, norm)
            disp.tensor_counts(pe, router.chosen[:])
            router.tensor_shares(pe)
            pe.wait_ge(router.shareT_ok, router.turn + 1)
            pe.wait_ge(b2_in, 16)
            for t in range(NT):
                if t >= 2:
                    pe.wait_ge(bias_added, t - 1)
                nc.tensor.matmul(k.bank[0:P, 2 + t % 2, :], router.shareT[:, tile_cols(t)], b2[:],
                                 start=True, stop=True).then_inc(bias_ps, 1)
            disp.tensor_list(pe)

            def transpose(bank, parts):
                for f in range(KD):
                    last = nc.tensor.transpose(k.bank[:, bank, f * SLOTS:(f + 1) * SLOTS], parts[:, f * 128:(f + 1) * 128],
                                               k.ident[:])
                return last

            pe.wait_ge(rows_in, 16)
            transpose(6, rows).then_inc(rows_ps, 1)
            pe.wait_ge(bias_added, NT)

            def expert(e, u):
                first, end = disp.range(pe, e)
                pe.wait_ge(w_in, e * 32 + 32)
                pe.sem_inc(seen, 1)
                with pe.Fori(first, end) as i:
                    pe.wait_ge(rowsT_ok, i + 1)
                    for b in range(2):
                        for part, done in ((0, gate_ps), (1, up_ps)):
                            for f in range(KD):
                                last = nc.tensor.matmul(k.bank[:, 2 * b + part, :], rowsT[:, f, :],
                                                        w1[:, u, f, part * H + b * 512:part * H + (b + 1) * 512],
                                                        start=(f == 0), stop=(f == KD - 1))
                            last.then_inc(done, 1)
                    pe.wait_ge(hid_ok, i * 2 + 1)
                    transpose(4, hid[:, 0, :]).then_inc(hT_ps, 1)
                    pe.wait_ge(rows_in, i * 16 + 32)
                    transpose(6, rows).then_inc(rows_ps, 1)
                    pe.wait_ge(hT_ok, i * 2 + 1)
                    pe.wait_ge(out_ok, i + 1)
                    for f in range(KD):
                        nc.tensor.matmul(k.bank[:, 7, :], hT[:, f, :], w2[:, u, f, :], start=(f == 0), stop=False)
                        if f == KD - 2:
                            pe.wait_ge(hid_ok, i * 2 + 2)
                            transpose(5, hid[:, 1, :]).then_inc(hT_ps, 1)
                    pe.wait_ge(hT_ok, i * 2 + 2)
                    for f in range(KD, FH):
                        last = nc.tensor.matmul(k.bank[:, 7, :], hT[:, f, :], w2[:, u, f, :], start=False,
                                                stop=(f == FH - 1))
                    last.then_inc(items_done, 1)

            with pe.Fori(0, E // 2) as h:
                for u in range(2):
                    expert(h * 2 + u, u)

        @block.scalar
        def _(act):
            norm.scalar(act)
            router.scalar_exp(act)
            router.scalar_shares(act)

            def copy_T(bank, to):
                return nc.scalar.copy(to, k.bank[:, bank, :].rearrange("p (f n) -> p f n", f=KD))

            act.wait_ge(rows_ps, 1)
            copy_T(6, rowsT[:]).then_inc(rowsT_ok, 1)
            act.wait_ge(disp.slots_ok, 1)
            with act.Fori(0, E) as e:
                first, end = disp.range(act, e)
                with act.Fori(first, end) as i:
                    for b in range(2):
                        act.wait_ge(gate_ok, i * 2 + b + 1)
                        nc.scalar.activation(sig[:, b, :], gate[:, b, :], ACT.Sigmoid, scale=1.702).then_inc(sig_ok, 1)
                    act.wait_ge(hT_ps, i * 2 + 1)
                    copy_T(4, hT[:, 0:KD, :]).then_inc(hT_ok, 1)
                    act.wait_ge(rows_ps, i + 2)
                    copy_T(6, rowsT[:]).then_inc(rowsT_ok, 1)
                    act.wait_ge(hT_ps, i * 2 + 2)
                    copy_T(5, hT[:, KD:FH, :]).then_inc(hT_ok, 1)

        @block.vector
        def _(dve):
            norm.vector(dve)
            dve.wait_ge(y_out, 16)
            router.vector(dve, disp.chosen_ok)
            disp.vector_slots(dve, router.chosen[:], router.share[:], router.earlier[:], router.above)
            for t in range(NT):
                dve.wait_ge(bias_ps, t + 1)
                nc.vector.tensor_tensor(k.x[:, t, :], k.x[:, t, :], k.bank[0:P, 2 + t % 2, :], ALU.add).then_inc(bias_added, 1)
            disp.vector_list(dve)
            dve.sem_inc(out_ok, 1)
            dve.sem_inc(out_free, 1)

            def expert(e, u):
                first, end = disp.range(dve, e)
                dve.wait_ge(b_in, e * 16 + 16)
                dve.sem_inc(seen, 1)
                with dve.Fori(first, end) as i:
                    for b in range(2):
                        dve.wait_ge(gate_ps, i * 2 + b + 1)
                        nc.vector.tensor_tensor(gate[:, b, :], k.bank[:, 2 * b, :], b1[:, u, b * 512:(b + 1) * 512],
                                                ALU.add).then_inc(gate_ok, 1)
                        dve.wait_ge(sig_ok, i * 2 + b + 1)
                        nc.vector.tensor_tensor(gate[:, b, :], gate[:, b, :], sig[:, b, :], ALU.mult)
                        dve.wait_ge(up_ps, i * 2 + b + 1)
                        nc.vector.scalar_tensor_tensor(out=hid[:, b, :], in0=k.bank[:, 2 * b + 1, :], scalar=1.0,
                                                       in1=b1[:, u, H + b * 512:H + (b + 1) * 512],
                                                       op0=ALU.add, op1=ALU.add)
                        dve.drain()
                        nc.vector.tensor_tensor(hid[:, b, :], hid[:, b, :], gate[:, b, :], ALU.mult).then_inc(hid_ok, 1)
                    dve.wait_ge(items_done, i + 1)
                    dve.wait_ge(out_free, i + 1)
                    nc.vector.tensor_scalar(out[:], k.bank[:, 7, :], disp.shares[:, bass.ds(i, 1)], None,
                                            ALU.mult).then_inc(out_ok, 1)
                    dve.drain()

            with dve.Fori(0, E // 2) as h:
                for u in range(2):
                    expert(h * 2 + u, u)


def write_out(k):
    nc, d = k.nc, k.d
    out_done = k.sem("out_done")
    with ExitStack() as ctx:
        block = ctx.enter_context(nc.Block())

        @block.sync
        def _(sp):
            sp.dma_start(d["out"].rearrange("(t p) d -> p t d", p=P), k.x[:]).then_inc(out_done, 16)
            sp.wait_ge(out_done, 16)



def program(nc, dram, stop=8):
    k = Kernel(nc, dram)
    with k.ctx:
        k.x = k.sb("x", [P, NT, D])
        k.ident = k.sb("ident", [128, 128])
        k.degree = k.sb("degree", [P, NT, 2])
        k.inv_in, k.inv_out, k.has_in = (k.sb(n, [P, NT, 1]) for n in ("inv_in", "inv_out", "has_in"))
        k.adj_saved = nc.dram_tensor("adj_saved", (P, NT, N), F32, kind="Internal").ap()
        k.y_rows = nc.dram_tensor("y_rows", (N + SLOTS, D), F32, kind="Internal").ap()
        k.sums = nc.dram_tensor("sums", (N + SLOTS, D), F32, kind="Internal").ap()
        k.slot_list = nc.dram_tensor("slot_list", ((ITEMS + 2) * SLOTS, 2), F32, kind="Internal").ap()
        k.norms, k.routers = 0, 0
        k.norm_sems = [k.sem(n) for n in ("norm_var_ok", "norm_std_ok", "y_ok", "yT_ps", "yT_ok")]
        k.router_sems = [k.sem(n) for n in ("gate_in", "earlier_ok", "logit_ps", "shift_ok", "exp_ok", "share_ok",
                                            "shareT_ps", "shareT_ok")]
        k.graphs, k.graphs_own = 0, 0
        k.graph_sems = [k.sem("graph_" + n) for n in ("w_in", "adjT_ps", "adjT_ok", "z_ps", "z_ok", "own_ps", "own_ok",
                                                      "pre_ok", "sum_ps", "h_ok", "gate_ok", "done")]
        k.x_in, k.ident_ok, k.adj_in = k.sem("x_in"), k.sem("ident_ok"), k.sem("adj_in")
        k.y = k.sb("y", [P, NT, D])
        k.yT = k.sb("yT", [128, KD, N])
        adjacency = k.ctx.enter_context(ExitStack())
        k.adj = k.sb("adj", [P, NT, N], F32, adjacency)
        build_adjacency(k)
        k.bank = k.ps("bank", [128, 8, 512], k.ctx)
        layers = ExitStack()
        with layers:
            k.z = k.sb("z", [128, NT, D], F32, layers)
            k.adjT = k.sb("adjT", [P, NT, N], F32, layers)
            graph_layer(k, "l0_gnn", "sage")
            if stop > 1:
                routed_layer(k, "l0_ffn", "relu")
            if stop > 2:
                graph_layer(k, "l1_gnn", "residual")
        if stop > 3:
            balanced_layer(k, "l1_ffn")
        if stop > 4:
            attention_layer(k, "l2_gnn")
        if stop > 5:
            merged_layer(k, "l2_ffn")
        if stop > 6:
            with ExitStack() as sums:
                k.z = k.sb("z3", [128, NT, D], F32, sums)
                graph_layer(k, "l3_gnn", "sum")
        adjacency.close()
        if stop > 7:
            top_two_layer(k, "l3_ffn")
        else:
            write_out(k)


INPUTS = ['x', 'src', 'dst', 'L0_gnn_W_l', 'L0_gnn_W_r', 'L0_gnn_b', 'L0_ffn_Wg', 'L0_ffn_bg', 'L0_ffn_W1', 'L0_ffn_W2',
          'L0_ffn_b2', 'L0_ffn_Ws1', 'L0_ffn_Ws2', 'L0_ffn_bs2', 'L1_gnn_alpha', 'L1_gnn_b', 'L1_ffn_gate_w',
          'L1_ffn_experts', 'L2_gnn_b_qkv', 'L2_gnn_b_ff', 'L2_ffn_gfc2_b', 'L2_ffn_b2', 'L2_ffn_ln_g', 'L2_ffn_ln_b', 'L2_ffn_tv_b2',
          'L2_ffn_tv_ln_g', 'L2_ffn_tv_ln_b', 'L3_gnn_wc', 'L3_gnn_wn', 'L3_gnn_bias', 'L3_ffn_router_w',
          'L3_ffn_router_b', 'L3_ffn_gate_up_proj', 'L3_ffn_gate_up_proj_bias', 'L3_ffn_down_proj', 'L3_ffn_down_proj_bias']


def laid_out(inputs):
    a = {n: np.ascontiguousarray(inputs[n]) for n in INPUTS}
    for n in ('L1_gnn_W', 'L2_gnn_W_qkv', 'L2_gnn_W_ff', 'L2_ffn_gfc1_w', 'L2_ffn_gfc2_w', 'L2_ffn_W1', 'L2_ffn_W2'):
        a[n + "_T"] = np.ascontiguousarray(np.asarray(inputs[n]).T)
    for n in ('L2_ffn_tv_W1', 'L2_ffn_tv_W2'):
        a[n + "_T"] = np.ascontiguousarray(np.asarray(inputs[n]).transpose(0, 2, 1))
    for n in ('L0_ffn_b1', 'L0_ffn_bs1', 'L2_gnn_b_qkv', 'L2_ffn_gfc1_b', 'L2_ffn_b1', 'L2_ffn_tv_b1'):
        b = np.asarray(inputs[n])
        rows = b.reshape(-1, b.shape[-1] // 128, 128)
        a[n + "_P"] = np.ascontiguousarray(rows.transpose(2, 0, 1))
    return {n: v.reshape(1) if v.ndim == 0 else v for n, v in a.items()}


def kernel(**inputs):
    import concourse.bacc as bacc
    from concourse.bass_utils import run_bass_kernel_spmd

    nc = bacc.Bacc("TRN2", target_bir_lowering=False, num_devices=1)
    arrays = laid_out(inputs)
    dram = {n: nc.dram_tensor(f"in_{n}", v.shape, mybir.dt.from_np(v.dtype), kind="ExternalInput").ap()
            for n, v in arrays.items()}
    dram["out"] = nc.dram_tensor("result", (N, D), F32, kind="ExternalOutput").ap()
    program(nc, dram)
    r = run_bass_kernel_spmd(nc, [{f"in_{n}": v for n, v in arrays.items()}], core_ids=[0])
    return r.results[0]["result"]
```

```python
import numpy as np
import concourse.bass as bass
from concourse import mybir
from concourse.alu_op_type import AluOpType as ALU
from contextlib import ExitStack

F32, F16, I32 = mybir.dt.float32, mybir.dt.float16, mybir.dt.int32
ACT = mybir.ActivationFunctionType
AX = mybir.AxisListType

N, D, E = 1250, 512, 8
P, NT = 125, 10
KD = D // 128
EDGES = 40000
G, J = 40, 8
CHUNKS = [(0, 512), (512, 512), (1024, N - 1024)]
BIG = 1.0e30


class Kernel:

    def __init__(self, nc, dram):
        self.nc, self.d, self.ctx = nc, dram, ExitStack()
        self.layer_sems = None

    def sb(self, name, shape, dt=F32, ctx=None):
        return (ctx or self.ctx).enter_context(self.nc.sbuf_tensor(name, shape, dt))

    def ps(self, name, shape, ctx):
        return ctx.enter_context(self.nc.psum_tensor(name, shape, F32))

    def sem(self, name):
        if self.layer_sems is None:
            return self.ctx.enter_context(self.nc.semaphore(name))
        self.layer_sems.append(self.nc.alloc_semaphore(name))
        return self.layer_sems[-1]

    def layer(self, build, *args):
        self.layer_sems = []
        build(self, *args)
        self.nc.all_engine_barrier()
        self.nc.clear_and_free_semaphores(self.layer_sems)
        self.nc.all_engine_barrier()
        self.layer_sems = None


def build_adjacency(k):
    nc, d = k.nc, k.d
    with ExitStack() as ctx:
        edges_i = k.sb("edges_i", [G, 2, P * J], I32, ctx)
        edges_f = k.sb("edges_f", [G, 2, P * J], F32, ctx)
        ends = k.sb("ends", [G, 2], F32, ctx)
        tiles = k.sb("tiles", [G, 2], F32, ctx)
        group_no = k.sb("group_no", [1, NT, G], F32, ctx)
        tile_no = k.sb("tile_no", [1, NT, G], F32, ctx)
        touch = k.sb("touch", [1, 2, NT, G], F32, ctx)
        spans_f = k.sb("spans_f", [1, 2, NT], F32, ctx)
        spans = k.sb("spans", [1, 2, NT], I32, ctx)
        zeros = k.sb("adj_zeros", [P, P], F16, ctx)
        node = k.sb("node", [P, 2, J, G], F32, ctx)
        iota = k.sb("iota", [P, N], F16, ctx)
        hot_src = k.sb("hot_src", [P, 2, J, N], F16, ctx)
        hot_dst = k.sb("hot_dst", [P, 4, J, P], F16, ctx)
        off_dst = k.sb("off_dst", [P, 4, J, P], F16, ctx)
        far_dst = k.sb("far_dst", [P, J, P], F16, ctx)
        one = k.sb("one", [P, 1], F32, ctx)
        dst_off, seen = k.sem("dst_off"), k.sem("adj_seen")
        ps_node = k.ps("ps_node", [P, 2, 512], ctx)
        acc = k.ps("acc", [P, 2, 3 * 512], ctx)
        edges_in, x_in, ident_ok, iota_ok = k.sem("edges_in"), k.x_in, k.ident_ok, k.sem("iota_ok")
        edges_ok, node_ps, node_ok, tiles_ok = k.sem("edges_ok"), k.sem("node_ps"), k.sem("node_ok"), k.sem("tiles_ok")
        bounds_ps, spans_ok = k.sem("bounds_ps"), k.sem("spans_ok")
        src_hot, dst_hot, item_done = k.sem("src_hot"), k.sem("dst_hot"), k.sem("item_done")
        acc_free, tile_done = k.sem("acc_free"), k.sem("tile_done")

        def span(eng, t):
            return (eng.value_load(spans[0:1, 0, bass.ds(t, 1)], min_val=0, max_val=G - 2),
                    eng.value_load(spans[0:1, 1, bass.ds(t, 1)], min_val=2, max_val=G))

        block = ctx.enter_context(nc.Block())

        @block.sync
        def _(sp):
            sp.dma_start(edges_i[:, 0, :], d["dst"].rearrange("(g e) -> g e", g=G)).then_inc(edges_in, 16)
            sp.dma_start(edges_i[:, 1, :], d["src"].rearrange("(g e) -> g e", g=G)).then_inc(edges_in, 16)
            sp.dma_start(k.x[:], d["x"].rearrange("(t p) d -> p t d", p=P)).then_inc(x_in, 16)

        @block.gpsimd
        def _(pool):
            nc.gpsimd.memset(k.ident[:], 0.0)
            pool.drain()
            nc.gpsimd.affine_select(out=k.ident[:], in_=k.ident[:], compare_op=ALU.not_equal, fill=1.0, base=0,
                                    pattern=[[-1, 128]], channel_multiplier=1).then_inc(ident_ok, 1)
            nc.gpsimd.memset(one[:], 1.0).then_inc(iota_ok, 1)
            nc.gpsimd.iota(iota[:], pattern=[[1, N]], base=0, channel_multiplier=0,
                           allow_small_or_imprecise_dtypes=True).then_inc(iota_ok, 1)
            nc.gpsimd.memset(zeros[:], 0.0)
            nc.gpsimd.iota(group_no[:], pattern=[[0, NT], [1, G]], base=0, channel_multiplier=0,
                           allow_small_or_imprecise_dtypes=True)
            nc.gpsimd.iota(tile_no[:], pattern=[[1, NT], [0, G]], base=0, channel_multiplier=0,
                           allow_small_or_imprecise_dtypes=True).then_inc(iota_ok, 1)
            pool.wait_ge(node_ok, 1)
            pool.wait_ge(spans_ok, 1)
            pool.drain()
            item = pool.alloc_register("item_pool")
            pool.reg_mov(item, 0)
            with pool.Fori(0, NT) as t:
                first, end = span(pool, t)
                with pool.Fori(first, end) as g:
                    i = pool.snap(item, min_val=0, max_val=G * NT)
                    slot = pool.snap(i % 4)
                    pool.wait_ge(item_done, i + 1)
                    nc.gpsimd.tensor_tensor(off_dst[:, bass.ds(slot, 1), :, :].rearrange("p a j n -> p (a j) n"),
                                            iota[:, bass.ds(t * P, P)].unsqueeze(1).broadcast_to([P, J, P]),
                                            node[:, 0, :, bass.ds(g, 1)].broadcast_to([P, J, P]),
                                            ALU.subtract).then_inc(dst_off, 1)
                    pool.reg_add(item, item, 1)

        @block.scalar
        def _(act):
            act.wait_ge(iota_ok, 3)
            act.wait_ge(spans_ok, 1)
            item = act.alloc_register("item_act")
            act.reg_mov(item, 0)
            with act.Fori(0, NT) as t:
                first, end = span(act, t)
                with act.Fori(first, end) as g:
                    i = act.snap(item, min_val=0, max_val=G * NT)
                    slot = act.snap(i % 4)
                    act.drain()
                    act.wait_ge(dst_off, i + 1)
                    act.reg_add(item, item, 1)
                    nc.scalar.activation(far_dst[:], off_dst[:, bass.ds(slot, 1), :, :], ACT.Abs)
                    act.drain()
                    nc.scalar.activation(hot_dst[:, bass.ds(slot, 1), :, :], far_dst[:], ACT.Relu,
                                         scale=-1.0, bias=one[:]).then_inc(dst_hot, 1)

        @block.tensor
        def _(pe):
            pe.wait_ge(ident_ok, 1)
            pe.wait_ge(edges_ok, 1)
            for w in range(2):
                v = edges_f[:, w, :].rearrange("g (p j) -> g j p", j=J)
                for j in range(J):
                    last = nc.tensor.transpose(ps_node[:, w, j * G:(j + 1) * G], v[:, j, :], k.ident[0:G, 0:G])
            last.then_inc(node_ps, 1)
            pe.wait_ge(tiles_ok, 1)
            pe.wait_ge(node_ok, 1)
            for w in range(2):
                last = nc.tensor.transpose(ps_node[0:1, w, 0:G], tiles[:, w:w + 1], k.ident[0:G, 0:G])
            last.then_inc(bounds_ps, 1)
            pe.wait_ge(spans_ok, 1)
            item = pe.alloc_register("item_pe")
            pe.reg_mov(item, 0)
            with pe.Fori(0, NT // 2) as tt:
                for u in range(2):
                    t = tt * 2 + u
                    first, end = span(pe, t)
                    pe.wait_ge(acc_free, t + 1)
                    for c0, cn in CHUNKS:
                        nc.tensor.matmul(acc[:, u, c0:c0 + cn], zeros[:], iota[:, c0:c0 + cn], start=True, stop=False)
                    with pe.Fori(first, end) as g:
                        i = pe.snap(item, min_val=0, max_val=G * NT)
                        half = pe.snap(i % 2)
                        slot = pe.snap(i % 4)
                        pe.wait_ge(src_hot, i + 1)
                        pe.wait_ge(dst_hot, i + 1)
                        pe.reg_add(item, item, 1)
                        for j in range(J):
                            for c0, cn in CHUNKS:
                                last = nc.tensor.matmul(acc[:, u, c0:c0 + cn], hot_dst[:, bass.ds(slot, 1), j, :],
                                                        hot_src[:, bass.ds(half, 1), j, c0:c0 + cn],
                                                        start=False, stop=False)
                        last.then_inc(item_done, 1)
                    for c0, cn in CHUNKS:
                        nc.tensor.matmul(acc[:, u, c0:c0 + cn], zeros[:], iota[:, c0:c0 + cn], start=False, stop=True)
                    pe.drain().then_inc(tile_done, 1)

        @block.vector
        def _(dve):
            dve.wait_ge(edges_in, 32)
            nc.vector.tensor_copy(edges_f[:], edges_i[:]).then_inc(edges_ok, 1)
            dve.drain()
            nc.vector.tensor_reduce(ends[:, 0:1], edges_f[:, 0, :], AX.X, ALU.min)
            nc.vector.tensor_reduce(ends[:, 1:2], edges_f[:, 0, :], AX.X, ALU.max)
            dve.drain()
            nc.vector.tensor_scalar(tiles[:, 0:1], ends[:, 0:1], float(P), None, ALU.is_ge)
            nc.vector.tensor_scalar(tiles[:, 1:2], ends[:, 1:2], float(P), 1.0, ALU.is_ge, ALU.add)
            for t in range(2, NT):
                dve.drain()
                last = nc.vector.scalar_tensor_tensor(out=tiles[:], in0=ends[:], scalar=float(P * t), in1=tiles[:],
                                                      op0=ALU.is_ge, op1=ALU.add)
            last.then_inc(tiles_ok, 1)
            dve.wait_ge(node_ps, 1)
            nc.vector.tensor_copy(node[:, :, :, 0:G],
                                  ps_node[:, :, 0:J * G].rearrange("p w (j g) -> p w j g", j=J)).then_inc(node_ok, 1)
            dve.wait_ge(bounds_ps, 1)
            dve.wait_ge(iota_ok, 3)
            wide = [1, NT, G]
            nc.vector.tensor_tensor(touch[:, 0], ps_node[0:1, 0, 0:G].unsqueeze(1).broadcast_to(wide), tile_no[:], ALU.is_le)
            nc.vector.tensor_tensor(touch[:, 1], ps_node[0:1, 1, 0:G].unsqueeze(1).broadcast_to(wide), tile_no[:], ALU.is_gt)
            dve.drain()
            nc.vector.tensor_tensor(touch[:, 1], touch[:, 0], touch[:, 1], ALU.mult)
            nc.vector.tensor_scalar(tile_no[:], group_no[:], -1.0, float(G - 1), ALU.mult, ALU.add)
            nc.vector.tensor_scalar(group_no[:], group_no[:], 1.0, None, ALU.add)
            dve.drain()
            nc.vector.tensor_tensor(touch[:, 0], touch[:, 1], tile_no[:], ALU.mult)
            nc.vector.tensor_tensor(touch[:, 1], touch[:, 1], group_no[:], ALU.mult)
            dve.drain()
            nc.vector.tensor_reduce(spans_f[:], touch[:], AX.X, ALU.max)
            dve.drain()
            nc.vector.tensor_scalar(spans_f[:, 0], spans_f[:, 0], -1.0, float(G - 1), ALU.mult, ALU.add)
            dve.drain()
            nc.vector.tensor_scalar(spans_f[:, 0], spans_f[:, 0], float(G - 2), None, ALU.min)
            dve.drain()
            nc.vector.scalar_tensor_tensor(out=spans_f[:, 1], in0=spans_f[:, 0], scalar=2.0, in1=spans_f[:, 1],
                                           op0=ALU.add, op1=ALU.max)
            dve.drain()
            nc.vector.tensor_copy(spans[:], spans_f[:])
            dve.drain()
            dve.sem_inc(spans_ok, 1)
            dve.sem_inc(acc_free, 2)
            dve.sem_inc(item_done, 4)
            item = dve.alloc_register("item_dve")
            dve.reg_mov(item, 0)

            def one_hots(g):
                i = dve.snap(item, min_val=0, max_val=G * NT)
                half = dve.snap(i % 2)
                dve.wait_ge(item_done, i + 3)
                dve.reg_add(item, item, 1)
                for j in range(J):
                    last = nc.vector.tensor_scalar(hot_src[:, bass.ds(half, 1), j, :], iota[:], node[:, 1, j, bass.ds(g, 1)],
                                                   None, ALU.is_equal)
                last.then_inc(src_hot, 1)

            def copy_out(t, half):
                nc.vector.tensor_copy(k.adj[:, bass.ds(t, 1), :], acc[:, half, 0:N]).then_inc(acc_free, 1)

            def others(first, end):
                with dve.Fori(first + 1, end) as g:
                    one_hots(g)

            first, end = span(dve, 0)
            one_hots(first)
            others(first, end)
            first, end = span(dve, 1)
            one_hots(first)
            dve.wait_ge(tile_done, 1)
            copy_out(0, 0)
            others(first, end)
            with dve.Fori(1, NT // 2) as tt:
                for u in range(2):
                    t = tt * 2 + u
                    first, end = span(dve, t)
                    one_hots(first)
                    dve.wait_ge(tile_done, t)
                    dve.sem_inc(seen, 1)
                    copy_out(t - 1, 1 - u)
                    others(first, end)
            dve.wait_ge(tile_done, NT)
            copy_out(NT - 1, 1)
            dve.drain()


def tile_cols(t):
    return slice(t * P, (t + 1) * P)


class Norm:

    def __init__(self, k, name, ctx, have_stats=False):
        self.k = k
        self.have_stats = have_stats
        self.mean_var = k.sb(f"{name}_mean_var", [P, NT, 2], F32, ctx)
        self.var = k.sb(f"{name}_var", [P, NT, 1], F32, ctx)
        self.std = k.sb(f"{name}_std", [P, NT, 1], F32, ctx)
        self.rstd = k.sb(f"{name}_rstd", [P, NT, 1], F32, ctx)
        self.var_ok, self.std_ok, self.y_ok, self.yT_ps, self.yT_ok = k.norm_sems
        self.layer, self.base = k.norms, k.norms * NT
        k.norms += 1

    def vector(self, dve):
        nc, k = self.k.nc, self.k
        if not self.have_stats:
            for t in range(NT):
                nc.vector.bn_stats(k.stats[:, t, :], k.x[:, t, :])
            dve.drain()
        for t in range(NT):
            nc.vector.bn_aggr(self.mean_var[:, t, :], k.stats[:, t, :])
        dve.drain()
        nc.vector.tensor_scalar(self.var[:], self.mean_var[:, :, 1:2], 1e-5, None, ALU.add).then_inc(self.var_ok, 1)
        dve.wait_ge(self.std_ok, self.layer + 1)
        nc.vector.reciprocal(self.rstd[:], self.std[:])
        dve.drain()
        for t in range(NT):
            nc.vector.tensor_scalar(k.y[:, t, :], k.x[:, t, :], self.mean_var[:, t, 0:1], self.rstd[:, t, :],
                                    ALU.subtract, ALU.mult).then_inc(self.y_ok, 1)
        dve.drain()

    def scalar(self, act, after_tile=None):
        nc, k = self.k.nc, self.k
        act.wait_ge(self.var_ok, self.layer + 1)
        nc.scalar.activation(self.std[:], self.var[:], ACT.Sqrt).then_inc(self.std_ok, 1)
        for t in range(NT):
            act.wait_ge(self.yT_ps, self.base + t + 1)
            nc.scalar.copy(k.yT[:, :, tile_cols(t)],
                           k.bank[:, 6 + t % 2, 0:KD * P].rearrange("p (f n) -> p f n", f=KD)).then_inc(self.yT_ok, 1)
            if after_tile:
                after_tile(t)

    def tensor(self, pe, after_tile=None):
        nc, k = self.k.nc, self.k
        for t in range(NT):
            pe.wait_ge(self.y_ok, self.base + t + 1)
            if t >= 2:
                pe.wait_ge(self.yT_ok, self.base + t - 1)
            for f in range(KD):
                last = nc.tensor.transpose(k.bank[:, 6 + t % 2, f * P:(f + 1) * P],
                                           k.y[:, t, f * 128:(f + 1) * 128], k.ident[0:P, 0:P])
            last.then_inc(self.yT_ps, 1)
            if after_tile and t:
                after_tile(t - 1)
        if after_tile:
            after_tile(NT - 1)


def graph_layer(k, name, kind):
    nc, d = k.nc, k.d
    first = kind == "sage"
    with ExitStack() as ctx:
        norm = Norm(k, name, ctx, have_stats=not first)
        w_agg = k.sb(f"{name}_w_agg", [128, KD, D], F32, ctx)
        w_self = k.sb(f"{name}_w_self", [128, KD, D], F32, ctx) if kind != "residual" else None
        bias = k.sb(f"{name}_bias", [P, D], F32, ctx)
        alpha = k.sb(f"{name}_alpha", [P, 1], F32, ctx)
        h = k.sb(f"{name}_h", [P, D], F32, ctx)
        gate = k.sb(f"{name}_gate", [P, 2, D], F32, ctx)
        own = k.sb(f"{name}_own", [P, 2, D], F32, ctx)
        w_in, adjT_ps, adjT_ok, z_ps, z_ok, own_ps, own_ok, pre_ok, sum_ps, h_ok, gate_ok, done = k.graph_sems
        base, own_base, w_base = k.graphs * NT, k.graphs_own * NT, k.graphs * 48
        k.graphs += 1
        k.graphs_own += kind != "residual"
        weights = {"sage": ("L0_gnn_W_l", "L0_gnn_W_r", "L0_gnn_b"), "residual": ("L1_gnn_W_T", None, "L1_gnn_b"),
                   "sum": ("L3_gnn_wn", "L3_gnn_wc", "L3_gnn_bias")}[kind]
        by_edge = k.adj if kind == "sum" else k.adjT
        scale = k.inv_out if kind == "sum" else k.inv_in
        block = ctx.enter_context(nc.Block())

        @block.sync
        def _(sp):
            sp.dma_start(w_agg[:], d[weights[0]].rearrange("(f p) n -> p f n", p=128)).then_inc(w_in, 16)
            if w_self is not None:
                sp.dma_start(w_self[:], d[weights[1]].rearrange("(f p) n -> p f n", p=128)).then_inc(w_in, 16)
            else:
                sp.dma_start(alpha[:], d["L1_gnn_alpha"].partition_broadcast(P)).then_inc(w_in, 16)
            sp.dma_start(bias[:], d[weights[2]].partition_broadcast(P)).then_inc(w_in, 16)

        @block.tensor
        def _(pe):
            if first:
                for s in range(NT):
                    if s >= 2:
                        pe.wait_ge(adjT_ok, s - 1)
                    for t in range(NT):
                        last = nc.tensor.transpose(
                            k.bank[0:P, 3 * (s % 2) + t // 4, (t % 4) * P:(t % 4 + 1) * P],
                            k.adj[:, t, tile_cols(s)], k.ident[0:P, 0:P])
                    last.then_inc(adjT_ps, 1)

            def neighbours(t):
                if t == 0:
                    pe.wait_ge(w_in, w_base + 48)
                pe.wait_ge(norm.yT_ok, norm.base + t + 1)
                if t >= 2:
                    pe.wait_ge(z_ok, base + t - 1)
                for f in range(KD):
                    last = nc.tensor.matmul(k.bank[0:P, t % 2, :], k.yT[:, f, tile_cols(t)], w_agg[:, f, :],
                                            start=(f == 0), stop=(f == KD - 1))
                last.then_inc(z_ps, 1)

            norm.tensor(pe, neighbours)
            for t in range(NT):
                if w_self is not None:
                    if t >= 2:
                        pe.wait_ge(own_ok, own_base + t - 1)
                    for f in range(KD):
                        last = nc.tensor.matmul(k.bank[0:P, 4 + t % 2, :], k.yT[:, f, tile_cols(t)], w_self[:, f, :],
                                                start=(f == 0), stop=(f == KD - 1))
                    last.then_inc(own_ps, 1)
                pe.wait_ge(z_ok, base + NT)
                if kind == "sum" and t == 0:
                    pe.wait_ge(k.adj_in, 16)
                if t >= 2:
                    pe.wait_ge(h_ok, base + t - 1)
                for s in range(NT):
                    last = nc.tensor.matmul(k.bank[0:P, 2 + t % 2, :], by_edge[:, s, tile_cols(t)], k.z[0:P, s, :],
                                            start=(s == 0), stop=(s == NT - 1))
                last.then_inc(sum_ps, 1)

        @block.scalar
        def _(act):
            if first:
                for s in range(NT):
                    act.wait_ge(adjT_ps, s + 1)
                    b = 3 * (s % 2)
                    nc.scalar.copy(k.adjT[:, s, 0:8 * P].rearrange("p (b n) -> p b n", b=2),
                                   k.bank[0:P, b:b + 2, 0:4 * P])
                    nc.scalar.copy(k.adjT[:, s, 8 * P:N], k.bank[0:P, b + 2, 0:2 * P]).then_inc(adjT_ok, 1)

            def neighbours(t):
                act.wait_ge(z_ps, base + t + 1)
                nc.scalar.copy(k.z[0:P, t, :], k.bank[0:P, t % 2, :]).then_inc(z_ok, 1)

            norm.scalar(act, lambda t: neighbours(t - 1) if t else None)
            neighbours(NT - 1)
            for t in range(NT):
                if w_self is not None:
                    act.wait_ge(own_ps, own_base + t + 1)
                    if t >= 2:
                        act.wait_ge(pre_ok, own_base + t - 1)
                    nc.scalar.copy(own[:, t % 2, :], k.bank[0:P, 4 + t % 2, :]).then_inc(own_ok, 1)
                if kind == "sage":
                    act.wait_ge(pre_ok, own_base + t + 1)
                    nc.scalar.activation(gate[:, t % 2, :], h[:], ACT.Sigmoid).then_inc(gate_ok, 1)

        @block.vector
        def _(dve):
            if first:
                dve.wait_ge(k.x_in, 16)
            norm.vector(dve)
            dve.wait_ge(w_in, w_base + 48)
            if first:
                nc.vector.tensor_reduce(k.degree[:, :, 0], k.adj[:], AX.X, ALU.add)
                dve.wait_ge(adjT_ok, NT)
                nc.vector.tensor_reduce(k.degree[:, :, 1], k.adjT[:], AX.X, ALU.add)
                dve.drain()
                nc.vector.tensor_scalar(k.inv_in[:], k.degree[:, :, 0:1], 1.0, None, ALU.max)
                nc.vector.reciprocal(k.inv_out[:], k.degree[:, :, 1:2])
                nc.vector.tensor_scalar(k.has_in[:], k.degree[:, :, 0:1], 0.0, None, ALU.is_gt)
                dve.drain()
                nc.vector.reciprocal(k.inv_in[:], k.inv_in[:])
                dve.drain()
            for t in range(NT):
                dve.wait_ge(sum_ps, base + t + 1)
                if w_self is not None:
                    dve.wait_ge(own_ok, own_base + t + 1)
                    nc.vector.scalar_tensor_tensor(out=h[:], in0=k.bank[0:P, 2 + t % 2, :], scalar=scale[:, t, :],
                                                   in1=own[:, t % 2, :], op0=ALU.mult, op1=ALU.add).then_inc(h_ok, 1)
                    dve.wait_ge(h_ok, base + t + 1)
                    nc.vector.tensor_tensor(h[:], h[:], bias[:], ALU.add).then_inc(pre_ok, 1)
                    dve.wait_ge(pre_ok, own_base + t + 1)
                    if kind == "sage":
                        dve.wait_ge(gate_ok, t + 1)
                        nc.vector.tensor_tensor(h[:], h[:], gate[:, t % 2, :], ALU.mult)
                        dve.drain()
                else:
                    nc.vector.scalar_tensor_tensor(out=h[:], in0=k.bank[0:P, 2 + t % 2, :], scalar=scale[:, t, :],
                                                   in1=bias[:], op0=ALU.mult, op1=ALU.add).then_inc(h_ok, 1)
                    dve.wait_ge(h_ok, base + t + 1)
                    nc.vector.scalar_tensor_tensor(out=h[:], in0=h[:], scalar=alpha[:], in1=k.y[:, t, :],
                                                   op0=ALU.mult, op1=ALU.add)
                    dve.drain()
                nc.vector.tensor_tensor(k.x[:, t, :], k.x[:, t, :], h[:], ALU.add).then_inc(done, 1)
                dve.wait_ge(done, base + t + 1)
                nc.vector.bn_stats(k.stats[:, t, :], k.x[:, t, :])
            dve.drain()


class Router:

    def __init__(self, k, name, w_gate, b_gate, ctx, extra=0):
        self.k, self.extra, self.w_gate, self.b_gate = k, extra, w_gate, b_gate
        self.w = k.sb(f"{name}_gate_w", [128, KD, E], F32, ctx)
        self.b = k.sb(f"{name}_gate_b", [P, E], F32, ctx)
        self.logit = k.sb(f"{name}_logit", [P, NT, E], F32, ctx)
        self.best = k.sb(f"{name}_best", [P, NT], F32, ctx)
        self.rank = k.sb(f"{name}_rank", [P, NT, E], F32, ctx)
        self.share = k.sb(f"{name}_share", [P, NT, E + extra], F32, ctx)
        spare = k.y[:].rearrange("p t d -> p (t d)")
        table = NT * E * E
        self.spare, self.spare_used = spare, 2 * table + N
        self.shareT = spare[0:E + extra, 2 * table:2 * table + N]
        self.above, self.equal = (spare[:, i * table:(i + 1) * table].rearrange("p (t e o) -> p t e o", t=NT, e=E)
                                  for i in range(2))
        self.earlier = k.sb(f"{name}_earlier", [P, E, E], F32, ctx)
        self.chosen = k.sb(f"{name}_chosen", [P, NT, E], F32, ctx)
        (self.gate_in, self.earlier_ok, self.logit_ps, self.shift_ok, self.exp_ok, self.share_ok, self.shareT_ps,
         self.shareT_ok) = k.router_sems
        self.turn = k.routers
        k.routers += 1

    def sync(self, sp):
        sp.dma_start(self.w[:], self.w_gate.rearrange("(f p) e -> p f e", p=128)).then_inc(self.gate_in, 16)
        sp.dma_start(self.b[:], self.b_gate.partition_broadcast(P)).then_inc(self.gate_in, 16)

    def gpsimd(self, pool):
        nc = self.k.nc
        nc.gpsimd.memset(self.earlier[:], 1.0)
        pool.drain()
        nc.gpsimd.affine_select(out=self.earlier[:], in_=self.earlier[:], compare_op=ALU.is_gt, fill=0.0, base=0,
                                pattern=[[1, E], [-1, E]], channel_multiplier=0).then_inc(self.earlier_ok, 1)

    def tensor_logits(self, pe, norm, t):
        nc, k = self.k.nc, self.k
        if t == 0:
            pe.wait_ge(self.gate_in, 32 * self.turn + 32)
        pe.wait_ge(norm.yT_ok, norm.base + t + 1)
        for f in range(KD):
            last = nc.tensor.matmul(k.bank[0:P, 5, t * E:(t + 1) * E], k.yT[:, f, tile_cols(t)], self.w[:, f, :],
                                    start=(f == 0), stop=(f == KD - 1))
        if t == NT - 1:
            last.then_inc(self.logit_ps, 1)

    def scalar_exp(self, act):
        act.wait_ge(self.shift_ok, self.turn + 1)
        self.k.nc.scalar.activation(self.logit[:], self.logit[:], ACT.Exp).then_inc(self.exp_ok, 1)

    def vector(self, dve, chosen_ok=None):
        nc, k, wide = self.k.nc, self.k, [P, NT, E, E]
        dve.wait_ge(self.logit_ps, self.turn + 1)
        dve.wait_ge(self.gate_in, 32 * self.turn + 32)
        dve.wait_ge(self.earlier_ok, self.turn + 1)
        nc.vector.tensor_tensor(self.logit[:], k.bank[0:P, 5, 0:NT * E].rearrange("p (t e) -> p t e", t=NT),
                                self.b[:].unsqueeze(1).broadcast_to([P, NT, E]), ALU.add)
        dve.drain()
        mine = self.logit[:].unsqueeze(3).broadcast_to(wide)
        other = self.logit[:].unsqueeze(2).broadcast_to(wide)
        nc.vector.tensor_tensor(self.above, other, mine, ALU.is_gt)
        nc.vector.tensor_tensor(self.equal, other, mine, ALU.is_equal)
        nc.vector.tensor_reduce(self.best[:], self.logit[:], AX.X, ALU.max)
        dve.drain()
        nc.vector.tensor_tensor(self.equal, self.equal, self.earlier[:].unsqueeze(1).broadcast_to(wide), ALU.mult)
        nc.vector.tensor_tensor(self.logit[:], self.logit[:], self.best[:].unsqueeze(2).broadcast_to([P, NT, E]),
                                ALU.subtract).then_inc(self.shift_ok, 1)
        dve.drain()
        nc.vector.tensor_tensor(self.above, self.above, self.equal, ALU.add)
        dve.drain()
        nc.vector.tensor_reduce(self.rank[:], self.above, AX.X, ALU.add)
        dve.drain()
        if chosen_ok is not None:
            nc.vector.tensor_scalar(self.chosen[:], self.rank[:], 1.5, None, ALU.is_lt).then_inc(chosen_ok, 1)
        dve.wait_ge(self.exp_ok, self.turn + 1)
        nc.vector.scalar_tensor_tensor(out=self.rank[:], in0=self.rank[:], scalar=1.5, in1=self.logit[:],
                                       op0=ALU.is_lt, op1=ALU.mult)
        dve.drain()
        nc.vector.tensor_reduce(self.best[:], self.rank[:], AX.X, ALU.add)
        dve.drain()
        nc.vector.reciprocal(self.best[:], self.best[:])
        if self.extra:
            nc.vector.memset(self.share[:, :, E:E + 1], 0.5)
        dve.drain()
        nc.vector.tensor_tensor(self.share[:, :, 0:E], self.rank[:], self.best[:].unsqueeze(2).broadcast_to([P, NT, E]),
                                ALU.mult)
        dve.drain()
        dve.sem_inc(self.share_ok, 1)

    def tensor_shares(self, pe):
        nc, k = self.k.nc, self.k
        pe.wait_ge(self.share_ok, self.turn + 1)
        for t in range(NT):
            last = nc.tensor.transpose(k.bank[0:E + self.extra, 4 + t // 4, (t % 4) * P:(t % 4 + 1) * P],
                                       self.share[:, t, :], k.ident[0:P, 0:P])
        last.then_inc(self.shareT_ps, 1)

    def scalar_shares(self, act):
        nc, k = self.k.nc, self.k
        act.wait_ge(self.shareT_ps, self.turn + 1)
        nc.scalar.copy(self.shareT[:, 0:8 * P].rearrange("p (b n) -> p b n", b=2), k.bank[0:E + self.extra, 4:6, 0:4 * P])
        nc.scalar.copy(self.shareT[:, 8 * P:N], k.bank[0:E + self.extra, 6, 0:2 * P]).then_inc(self.shareT_ok, 1)


TOKENS = [(0, 417), (417, 417), (834, N - 834)]


SLOTS = 128
ITEMS = (2 * N + E * (SLOTS - 1)) // SLOTS
LISTS = ITEMS + 2


class Dispatch:

    def __init__(self, k, name, ctx, hot, values, rows, out):
        self.k, self.hot, self.values, self.rows, self.out = k, hot, values, rows, out
        wide = [P, NT, E]
        self.before = k.sb(f"{name}_before", [P, P], F32, ctx)
        self.ones = k.sb(f"{name}_ones", [P, P], F32, ctx)
        self.total = k.sb(f"{name}_total", wide, F32, ctx)
        self.pos = k.sb(f"{name}_pos", wide, F32, ctx)
        self.items = k.sb(f"{name}_items", [P, E], F32, ctx)
        self.first = k.sb(f"{name}_first", [P, E + 1], F32, ctx)
        self.nth = k.sb(f"{name}_nth", wide, F32, ctx)
        self.pick = k.sb(f"{name}_pick", [P, 2, NT, E], F32, ctx)
        self.slot = k.sb(f"{name}_slot", [P, 2 * NT], F32, ctx)
        self.item = k.sb(f"{name}_item", [P, 2 * NT], F32, ctx)
        self.share = k.sb(f"{name}_share_of", [P, 2 * NT], F32, ctx)
        self.node = k.sb(f"{name}_node", [P, 2 * NT], F32, ctx)
        self.slot_no = k.sb(f"{name}_slot_no", [P, SLOTS], F32, ctx)
        self.start_no = k.sb(f"{name}_start_no", [P, LISTS + 1], F32, ctx)
        self.spare = k.sb(f"{name}_spare", [SLOTS, 2], F32, ctx)
        self.first_item = k.sb(f"{name}_first_item", [1, E + 1], I32, ctx)
        self.unused = k.sb(f"{name}_unused", [SLOTS, LISTS], F32, ctx)
        self.nodes = k.sb(f"{name}_nodes", [SLOTS, LISTS], I32, ctx)
        self.shares = k.sb(f"{name}_shares", [SLOTS, LISTS], F32, ctx)
        self.now_in = k.sb(f"{name}_now_in", [SLOTS, 1], I32, ctx)
        self.now_out = k.sb(f"{name}_now_out", [SLOTS, 1], I32, ctx)
        (self.const_ok, self.chosen_ok, self.count_ps, self.slots_ok, self.values_ok, self.list_ps, self.list_ok,
         self.spare_out, self.y_out, self.x_out, self.rows_in, self.rows_ps, self.out_ok, self.summed, self.seen,
         self.all_in, self.copied) = (
            k.sem(f"{name}_{s}") for s in ("const_ok", "chosen_ok", "count_ps", "slots_ok", "values_ok", "list_ps",
                                           "list_ok", "spare_out", "y_out", "x_out", "rows_in", "rows_ps", "out_ok",
                                           "summed", "seen", "all_in", "copied"))

    def sync_y(self, sp, norm):
        k = self.k
        sp.wait_ge(norm.y_ok, norm.base + NT)
        sp.dma_start(k.y_rows[0:N].rearrange("(t p) d -> p t d", p=P), k.y[:]).then_inc(self.y_out, 16)

    def sync_x(self, sp, added):
        k = self.k
        sp.wait_ge(added, NT)
        sp.dma_start(k.sums[0:N].rearrange("(t p) d -> p t d", p=P), k.x[:]).then_inc(self.x_out, 16)

    def gpsimd_constants(self, pool):
        nc, k = self.k.nc, self.k
        inexact = dict(allow_small_or_imprecise_dtypes=True)
        nc.gpsimd.memset(self.out, 0.0)
        nc.gpsimd.memset(self.before[:], 1.0)
        nc.gpsimd.memset(self.ones[:], 1.0)
        pool.drain()
        nc.gpsimd.dma_start(k.y_rows[N:N + SLOTS], self.out).then_inc(self.spare_out, 16)
        nc.gpsimd.dma_start(k.sums[N:N + SLOTS], self.out).then_inc(self.spare_out, 16)
        nc.gpsimd.affine_select(out=self.before[:], in_=self.before[:], compare_op=ALU.is_gt, fill=0.0, base=0,
                                pattern=[[1, P]], channel_multiplier=-1)
        nc.gpsimd.iota(self.node[:], pattern=[[0, 2], [P, NT]], base=0, channel_multiplier=1, **inexact)
        nc.gpsimd.iota(self.slot_no[:], pattern=[[1, SLOTS]], base=0, channel_multiplier=0, **inexact)
        nc.gpsimd.iota(self.start_no[:], pattern=[[SLOTS, LISTS + 1]], base=0, channel_multiplier=0, **inexact)
        nc.gpsimd.iota(self.spare[:, 0:1], pattern=[[0, 1]], base=N, channel_multiplier=1, **inexact)
        nc.gpsimd.iota(self.spare[:, 1:2], pattern=[[0, 1]], base=-N, channel_multiplier=-1, **inexact)
        pool.drain()
        pool.sem_inc(self.const_ok, 1)

    def gpsimd_items(self, pool):
        nc, k = self.k.nc, self.k

        def gather(i, copies):
            nc.gpsimd.tensor_copy(self.now_in[:], self.nodes[:, i]).then_inc(self.copied, 1)
            pool.wait_ge(self.copied, copies)
            pool.sem_inc(self.seen, 1)
            nc.gpsimd.indirect_dma_start(self.rows, None, k.y_rows, bass.IndirectOffsetOnAxis(ap=self.now_in[:], axis=0)
                                         ).then_inc(self.rows_in, 16)

        def scatter(i, copies):
            nc.gpsimd.tensor_copy(self.now_out[:], self.nodes[:, i]).then_inc(self.copied, 1)
            pool.wait_ge(self.copied, copies)
            pool.sem_inc(self.seen, 1)
            nc.gpsimd.indirect_dma_start(k.sums, bass.IndirectOffsetOnAxis(ap=self.now_out[:], axis=0), self.out, None,
                                         compute_op=ALU.add).then_inc(self.summed, 16)

        pool.wait_ge(self.list_ok, 1)
        pool.wait_ge(self.y_out, 16)
        pool.wait_ge(self.spare_out, 32)
        gather(slice(0, 1), 1)
        pool.wait_ge(self.rows_ps, 1)
        gather(slice(1, 2), 2)
        nc.gpsimd.memset(self.out, 0.0)
        pool.wait_ge(self.x_out, 16)
        scatter(slice(ITEMS, ITEMS + 1), 3)
        pool.wait_ge(self.summed, 16)
        pool.sem_inc(self.seen, 1)
        with pool.Fori(0, E) as e:
            first, end = self.range(pool, e)
            with pool.Fori(first, end) as i:
                pool.wait_ge(self.rows_in, i * 16 + 32)
                pool.wait_ge(self.rows_ps, i + 2)
                pool.sem_inc(self.seen, 1)
                gather(bass.ds(i + 2, 1), i * 2 + 4)
                pool.wait_ge(self.out_ok, i + 2)
                pool.sem_inc(self.seen, 1)
                scatter(bass.ds(i, 1), i * 2 + 5)
        items = pool.value_load(self.first_item[0:1, E:E + 1], min_val=1, max_val=ITEMS)
        pool.wait_ge(self.rows_in, items * 16 + 32)
        pool.wait_ge(self.summed, items * 16 + 16)
        pool.sem_inc(self.all_in, 1)

    def tensor_counts(self, pe, chosen):
        nc, k = self.k.nc, self.k
        pe.wait_ge(self.const_ok, 1)
        pe.wait_ge(self.chosen_ok, 1)
        flat = chosen.rearrange("p t e -> p (t e)")
        nc.tensor.matmul(k.bank[0:P, 5, 0:NT * E], self.before[:], flat, start=True, stop=True)
        nc.tensor.matmul(k.bank[0:P, 6, 0:NT * E], self.ones[:], flat, start=True, stop=True).then_inc(self.count_ps, 1)

    def tensor_list(self, pe):
        nc, k = self.k.nc, self.k
        pe.wait_ge(self.values_ok, 1)
        for n in range(2 * NT):
            last = nc.tensor.matmul(k.bank[0:SLOTS, 7, 0:3 * LISTS], self.hot[:, n, :],
                                    self.values[:, n, :, :].rearrange("p c i -> p (c i)"),
                                    start=(n == 0), stop=(n == 2 * NT - 1))
        last.then_inc(self.list_ps, 1)

    def vector_slots(self, dve, chosen, share, earlier, scratch):
        nc, k = self.k.nc, self.k
        nc.vector.tensor_tensor(scratch, chosen.unsqueeze(2).broadcast_to([P, NT, E, E]),
                                earlier.unsqueeze(1).broadcast_to([P, NT, E, E]), ALU.mult)
        dve.wait_ge(self.count_ps, 1)
        nc.vector.tensor_copy(self.pos[:], k.bank[0:P, 5, 0:NT * E].rearrange("p (t e) -> p t e", t=NT))
        nc.vector.tensor_copy(self.total[:], k.bank[0:P, 6, 0:NT * E].rearrange("p (t e) -> p t e", t=NT))
        dve.drain()
        dve.sem_inc(self.slots_ok, 1)
        nc.vector.tensor_reduce(self.nth[:], scratch, AX.X, ALU.add)
        for t in range(1, NT):
            nc.vector.tensor_tensor(self.total[:, t, :], self.total[:, t, :], self.total[:, t - 1, :], ALU.add)
            dve.drain()
        nc.vector.tensor_tensor(self.pos[:, 1:NT, :], self.pos[:, 1:NT, :], self.total[:, 0:NT - 1, :], ALU.add)
        nc.vector.tensor_scalar(self.items[:], self.total[:, NT - 1, :], float(SLOTS), 1.0, ALU.is_gt, ALU.add)
        nc.vector.memset(self.first[:], 0.0)
        for j in range(2, -(-N // SLOTS)):
            dve.drain()
            nc.vector.scalar_tensor_tensor(out=self.items[:], in0=self.total[:, NT - 1, :], scalar=float(SLOTS * j),
                                           in1=self.items[:], op0=ALU.is_gt, op1=ALU.add)
        for e in range(E):
            dve.drain()
            nc.vector.tensor_tensor(self.first[:, e + 1:e + 2], self.first[:, e:e + 1], self.items[:, e:e + 1], ALU.add)
        dve.drain()
        nc.vector.tensor_copy(self.first_item[:], self.first[0:1, :])
        nc.vector.tensor_scalar(self.items[:], self.first[:, 0:E], float(SLOTS), None, ALU.mult)
        for kth in range(2):
            nc.vector.scalar_tensor_tensor(out=self.pick[:, kth], in0=self.nth[:], scalar=float(kth), in1=chosen,
                                           op0=ALU.is_equal, op1=ALU.mult)
        dve.drain()
        nc.vector.tensor_tensor(self.pos[:], self.pos[:], self.items[:].unsqueeze(1).broadcast_to([P, NT, E]), ALU.add)
        dve.drain()
        for kth in range(2):
            nc.vector.tensor_tensor(scratch[:, :, kth, :], self.pick[:, kth], self.pos[:], ALU.mult)
            nc.vector.tensor_tensor(scratch[:, :, 2 + kth, :], self.pick[:, kth], share, ALU.mult)
        dve.drain()
        for kth in range(2):
            own = slice(kth * NT, (kth + 1) * NT)
            nc.vector.tensor_reduce(self.slot[:, own], scratch[:, :, kth, :], AX.X, ALU.add)
            nc.vector.tensor_reduce(self.share[:, own], scratch[:, :, 2 + kth, :], AX.X, ALU.add)
        dve.wait_ge(self.const_ok, 1)
        dve.wait_ge(self.spare_out, 32)
        dve.drain()
        reached = scratch.rearrange("p t e o -> p (t e o)")[:, 0:2 * NT * (LISTS + 1)].rearrange("p (n i) -> p n i", n=2 * NT)
        nc.vector.tensor_tensor(reached, self.slot[:].unsqueeze(2).broadcast_to([P, 2 * NT, LISTS + 1]),
                                self.start_no[:].unsqueeze(1).broadcast_to([P, 2 * NT, LISTS + 1]), ALU.is_ge)
        dve.drain()
        nc.vector.tensor_reduce(self.item[:], reached, AX.X, ALU.add)
        nc.vector.tensor_tensor(self.values[:, :, 2, :], reached[:, :, 0:LISTS], reached[:, :, 1:LISTS + 1], ALU.subtract)
        dve.drain()
        nc.vector.scalar_tensor_tensor(out=self.slot[:], in0=self.item[:], scalar=float(-SLOTS), in1=self.slot[:],
                                       op0=ALU.mult, op1=ALU.add)
        for c, value in enumerate((self.node, self.share)):
            nc.vector.tensor_tensor(self.values[:, :, c, :], self.values[:, :, 2, :],
                                    value[:].unsqueeze(2).broadcast_to([P, 2 * NT, LISTS]), ALU.mult)
        dve.drain()
        nc.vector.tensor_scalar(self.slot[:], self.slot[:], float(SLOTS), None, ALU.add)
        dve.drain()
        nc.vector.tensor_tensor(self.hot, self.slot[:].unsqueeze(2).broadcast_to([P, 2 * NT, SLOTS]),
                                self.slot_no[:].unsqueeze(1).broadcast_to([P, 2 * NT, SLOTS]), ALU.is_equal)
        dve.drain()
        dve.sem_inc(self.values_ok, 1)

    def vector_list(self, dve):
        nc, k = self.k.nc, self.k
        dve.wait_ge(self.list_ps, 1)
        parts = k.bank[0:SLOTS, 7, 0:3 * LISTS].rearrange("s (c i) -> s c i", c=3)
        nc.vector.tensor_scalar(self.unused[:], parts[:, 2, :], self.spare[:, 1:2], self.spare[:, 0:1], ALU.mult, ALU.add)
        nc.vector.tensor_copy(self.shares[:], parts[:, 1, :])
        dve.drain()
        nc.vector.tensor_tensor(self.nodes[:], parts[:, 0, :], self.unused[:], ALU.add)
        dve.drain()
        dve.sem_inc(self.list_ok, 1)
        dve.sem_inc(self.out_ok, 1)

    def vector_result(self, dve, i, done):
        nc, k = self.k.nc, self.k
        dve.wait_ge(done, i + 1)
        dve.wait_ge(self.summed, i * 16 + 16)
        nc.vector.tensor_scalar(self.out, k.bank[:, 7, :], self.shares[:, bass.ds(i, 1)], None,
                                ALU.mult).then_inc(self.out_ok, 1)

    def range(self, eng, e):
        first = eng.value_load(self.first_item[0:1, bass.ds(e, 1)], min_val=0, max_val=ITEMS - 1)
        end = eng.value_load(self.first_item[0:1, bass.ds(e + 1, 1)], min_val=1, max_val=ITEMS)
        return first, end


def tensor_transposed(k, bank, rows):
    for f in range(KD):
        last = k.nc.tensor.transpose(k.bank[:, bank, f * SLOTS:(f + 1) * SLOTS], rows[:, f * 128:(f + 1) * 128], k.ident[:])
    return last


def scalar_untransposed(k, bank, to):
    return k.nc.scalar.copy(to, k.bank[:, bank, :].rearrange("p (f n) -> p f n", f=KD))


def sync_back(k, sp, x_back):
    rows = k.sums[0:N].rearrange("(t p) d -> p t d", p=P)
    for i in range(NT // 2):
        sp.dma_start(k.x[:, 2 * i:2 * i + 2, :], rows[:, 2 * i:2 * i + 2, :]).then_inc(x_back[i], 16)


def vector_back(k, dve, x_back):
    for t in range(NT):
        dve.wait_ge(x_back[t // 2], 16)
        k.nc.vector.bn_stats(k.stats[:, t, :], k.x[:, t, :])
    dve.drain()


def relu_layer(k, name):
    nc, d = k.nc, k.d
    H = 256
    FH = H // 128
    with ExitStack() as ctx:
        norm = Norm(k, name, ctx, have_stats=True)
        router = Router(k, name, d["L0_ffn_Wg"], d["L0_ffn_bg"], ctx, 1)
        w1 = k.sb(f"{name}_w1", [128, 2, KD, H], F32, ctx)
        w2 = k.sb(f"{name}_w2", [128, 2, FH, D], F32, ctx)
        b1 = k.sb(f"{name}_b1", [128, E + 1, FH], F32, ctx)
        b1_now = k.sb(f"{name}_b1_now", [128, FH], F32, ctx)
        b2 = k.sb(f"{name}_b2", [E + 1, D], F32, ctx)
        z = k.z[:].rearrange("p t d -> p (t d)")
        sharedT = z[:, 0:FH * N].rearrange("p (f n) -> p f n", f=FH)
        z = z[:, FH * N:]
        rows, rowsT, out = z[:, 0:D], z[:, D:2 * D].rearrange("p (f n) -> p f n", f=KD), z[:, 2 * D:3 * D]
        hT = z[:, 3 * D:3 * D + FH * SLOTS].rearrange("p (f n) -> p f n", f=FH)
        values = z[0:P, 0:2 * NT * 3 * LISTS].rearrange("p (n c i) -> p n c i", n=2 * NT, c=3)
        hot = router.spare[:, router.spare_used:router.spare_used + 2 * NT * SLOTS].rearrange("p (n s) -> p n s", n=2 * NT)
        disp = Dispatch(k, name, ctx, hot, values, rows, out)
        w_in, shared_in, b_in, half_ok = (k.sem(f"{name}_{s}") for s in ("w_in", "shared_in", "b_in", "half_ok"))
        x_back = [k.sem(f"{name}_x_back{i}") for i in range(NT // 2)]
        shared_ps, shared_ok, shared_done, sum_ps, added = (
            k.sem(f"{name}_{s}") for s in ("shared_ps", "shared_ok", "shared_done", "sum_ps", "added"))
        rowsT_ok, hid_ps, hid_ok, out_ps = (k.sem(f"{name}_{s}") for s in ("rowsT_ok", "hid_ps", "hid_ok", "out_ps"))
        block = ctx.enter_context(nc.Block())
        src1 = d["L0_ffn_W1"].rearrange("e (f p) n -> p e f n", p=128)
        src2 = d["L0_ffn_W2"].rearrange("e (f p) n -> p e f n", p=128)
        STEPS = FH * 3

        @block.sync
        def _(sp):
            router.sync(sp)
            sp.dma_start(w1[:, 1], d["L0_ffn_Ws1"].rearrange("(f p) n -> p f n", p=128)).then_inc(shared_in, 16)
            sp.dma_start(w2[:, 1], d["L0_ffn_Ws2"].rearrange("(f p) n -> p f n", p=128)).then_inc(shared_in, 16)
            sp.dma_start(b1[:, 0:E], d["L0_ffn_b1_P"]).then_inc(b_in, 16)
            sp.dma_start(b1[:, E:E + 1], d["L0_ffn_bs1_P"]).then_inc(b_in, 16)
            sp.dma_start(b2[0:E], d["L0_ffn_b2"]).then_inc(b_in, 16)
            sp.dma_start(b2[E:E + 1], d["L0_ffn_bs2"].unsqueeze(0)).then_inc(b_in, 16)
            sp.dma_start(w1[:, 0], src1[:, 0]).then_inc(w_in, 16)
            sp.dma_start(w2[:, 0], src2[:, 0]).then_inc(w_in, 16)
            disp.sync_y(sp, norm)
            sp.wait_ge(w_in, 32)
            sp.wait_ge(shared_done, 1)
            sp.dma_start(w1[:, 1], src1[:, 1]).then_inc(w_in, 16)
            sp.dma_start(w2[:, 1], src2[:, 1]).then_inc(w_in, 16)
            disp.sync_x(sp, added)
            with sp.Fori(0, E // 2 - 1) as h:
                for u in range(2):
                    e = h * 2 + u
                    end = sp.value_load(disp.first_item[0:1, bass.ds(e + 1, 1)], min_val=1, max_val=ITEMS)
                    sp.wait_ge(w_in, e * 32 + 64)
                    sp.wait_ge(out_ps, end)
                    sp.dma_start(w1[:, u:u + 1], src1[:, bass.ds(e + 2, 1)]).then_inc(w_in, 16)
                    sp.dma_start(w2[:, u:u + 1], src2[:, bass.ds(e + 2, 1)]).then_inc(w_in, 16)
            sp.wait_ge(disp.all_in, 1)
            sync_back(k, sp, x_back)

        @block.gpsimd
        def _(pool):
            router.gpsimd(pool)
            disp.gpsimd_constants(pool)
            disp.gpsimd_items(pool)

        @block.tensor
        def _(pe):
            norm.tensor(pe, lambda t: router.tensor_logits(pe, norm, t))
            pe.wait_ge(shared_in, 32)
            for n in range(STEPS):
                f, (c0, cn) = n // 3, TOKENS[n % 3]
                if n >= 3:
                    pe.wait_ge(shared_ok, n - 2)
                for kk in range(KD):
                    last = nc.tensor.matmul(k.bank[:, n % 3, 0:cn], w1[:, 1, kk, f * 128:(f + 1) * 128],
                                            k.yT[:, kk, c0:c0 + cn], start=(kk == 0), stop=(kk == KD - 1))
                last.then_inc(shared_ps, 1)
            disp.tensor_counts(pe, router.chosen[:])
            pe.wait_ge(disp.slots_ok, 1)
            router.tensor_shares(pe)
            pe.wait_ge(router.shareT_ok, router.turn + 1)
            pe.wait_ge(b_in, 64)
            pe.wait_ge(shared_ok, STEPS)
            for t in range(NT):
                if t == 4:
                    disp.tensor_list(pe)
                    pe.wait_ge(disp.rows_in, 16)
                    tensor_transposed(k, 6, rows).then_inc(disp.rows_ps, 1)
                if t >= 4:
                    pe.wait_ge(added, t - 3)
                for f in range(FH):
                    nc.tensor.matmul(k.bank[0:P, t % 4, :], sharedT[:, f, tile_cols(t)], w2[:, 1, f, :],
                                     start=(f == 0), stop=False)
                nc.tensor.matmul(k.bank[0:P, t % 4, :], router.shareT[:, tile_cols(t)], b2[:],
                                 start=False, stop=True).then_inc(sum_ps, 1)
            pe.drain()
            pe.sem_inc(shared_done, 1)
            pe.wait_ge(added, NT)

            def expert(e, u):
                first, end = disp.range(pe, e)
                pe.wait_ge(w_in, e * 32 + 32)
                pe.sem_inc(disp.seen, 1)
                with pe.Fori(first, end) as i:
                    pe.wait_ge(rowsT_ok, i + 1)
                    for f in range(FH):
                        for kk in range(KD):
                            last = nc.tensor.matmul(k.bank[:, f, 0:SLOTS], w1[:, u, kk, f * 128:(f + 1) * 128],
                                                    rowsT[:, kk, :], start=(kk == 0), stop=(kk == KD - 1))
                        last.then_inc(hid_ps, 1)
                    pe.wait_ge(disp.rows_in, i * 16 + 32)
                    tensor_transposed(k, 6, rows).then_inc(disp.rows_ps, 1)
                    pe.wait_ge(hid_ok, i * 2 + 2)
                    pe.wait_ge(disp.out_ok, i + 1)
                    for f in range(FH):
                        last = nc.tensor.matmul(k.bank[:, 7, :], hT[:, f, :], w2[:, u, f, :], start=(f == 0),
                                                stop=(f == FH - 1))
                    last.then_inc(out_ps, 1)

            with pe.Fori(0, E // 2) as h:
                for u in range(2):
                    expert(h * 2 + u, u)

        @block.scalar
        def _(act):
            norm.scalar(act)
            router.scalar_exp(act)
            act.wait_ge(half_ok, 1)
            for n in range(STEPS):
                f, (c0, cn) = n // 3, TOKENS[n % 3]
                act.wait_ge(shared_ps, n + 1)
                nc.scalar.activation(sharedT[:, f, c0:c0 + cn], k.bank[:, n % 3, 0:cn], ACT.Relu,
                                     bias=b1[:, E, f:f + 1], scale=0.5).then_inc(shared_ok, 1)
            router.scalar_shares(act)
            act.wait_ge(disp.rows_ps, 1)
            scalar_untransposed(k, 6, rowsT).then_inc(rowsT_ok, 1)
            with act.Fori(0, E) as e:
                first, end = disp.range(act, e)
                nc.scalar.copy(b1_now[:], b1[:, bass.ds(e, 1), :])
                act.drain()
                with act.Fori(first, end) as i:
                    for f in range(FH):
                        act.wait_ge(hid_ps, i * 2 + f + 1)
                        nc.scalar.activation(hT[:, f, :], k.bank[:, f, 0:SLOTS], ACT.Relu,
                                             bias=b1_now[:, f:f + 1]).then_inc(hid_ok, 1)
                    act.wait_ge(disp.rows_ps, i + 2)
                    scalar_untransposed(k, 6, rowsT).then_inc(rowsT_ok, 1)
                act.drain()

        @block.vector
        def _(dve):
            norm.vector(dve)
            dve.wait_ge(b_in, 64)
            nc.vector.tensor_scalar(b1[:, E, :], b1[:, E, :], 0.5, None, ALU.mult).then_inc(half_ok, 1)
            dve.wait_ge(disp.y_out, 16)
            router.vector(dve, disp.chosen_ok)
            disp.vector_slots(dve, router.chosen[:], router.share[:, :, 0:E], router.earlier[:], router.above)
            disp.vector_list(dve)
            for t in range(NT):
                dve.wait_ge(sum_ps, t + 1)
                nc.vector.tensor_tensor(k.x[:, t, :], k.x[:, t, :], k.bank[0:P, t % 4, :], ALU.add).then_inc(added, 1)
            with dve.Fori(0, E) as e:
                first, end = disp.range(dve, e)
                with dve.Fori(first, end) as i:
                    disp.vector_result(dve, i, out_ps)
            vector_back(k, dve, x_back)


SINKHORN, TOP = 8, N // E
HALF = TOP // 2


def balanced_layer(k, name):
    nc, d = k.nc, k.d
    with ExitStack() as ctx:
        norm = Norm(k, name, ctx, have_stats=True)
        w_gate = k.sb(f"{name}_w_gate", [128, KD, E], F32, ctx)
        ones = k.sb(f"{name}_ones", [P, P], F32, ctx)
        gate = k.sb(f"{name}_gate", [P, NT, E], F32, ctx)
        col = k.sb(f"{name}_col", [P, E], F32, ctx)
        row = k.sb(f"{name}_row", [P, NT], F32, ctx)
        top = k.sb(f"{name}_top", [E, 8], F32, ctx)
        zeros = k.sb(f"{name}_zeros", [E, N], F32, ctx)
        gateT, left, equal, count = (k.yT[0:E, i, :] for i in range(4))
        y_flat, yT_flat = k.y[:].rearrange("p t d -> p (t d)"), k.yT[:].rearrange("p f n -> p (f n)")
        hot = [(y_flat[:, e * NT * HALF:(e + 1) * NT * HALF] if e < 6 else
                yT_flat[0:P, (e - 4) * NT * HALF:(e - 3) * NT * HALF]).rearrange("p (t s) -> p t s", t=NT)
               for e in range(E)]
        rows = [k.y[0:HALF, i, :] if i < NT else yT_flat[0:HALF, (i - NT) * D:(i - NT + 1) * D] for i in range(2 * E)]
        above = k.sb(f"{name}_above", [E, 2], F32, ctx)
        taken = k.sb(f"{name}_taken", [P, NT, E], F32, ctx)
        share = k.sb(f"{name}_share", [P, NT, E], F32, ctx)
        w = k.sb(f"{name}_w", [128, E, KD, D], F32, ctx)
        iota = k.sb(f"{name}_iota", [P, HALF], F32, ctx)
        node_id = k.sb(f"{name}_node_id", [P, NT], F32, ctx)
        place = k.sb(f"{name}_place", [P, NT, E], F32, ctx)
        values = k.sb(f"{name}_values", [P, NT, E, 4], F32, ctx)
        nodes = k.sb(f"{name}_nodes", [HALF, 2 * E], I32, ctx)
        shares = k.sb(f"{name}_shares", [HALF, 2 * E], F32, ctx)
        rowsT = k.sb(f"{name}_rowsT", [128, 2, KD, HALF], F32, ctx)
        out = k.sb(f"{name}_out", [HALF, 4, D], F32, ctx)
        gate_in, gate_ps, scaled = k.sem(f"{name}_gate_in"), k.sem(f"{name}_gate_ps"), k.sem(f"{name}_scaled")
        col_ps, gateT_ps, taken_ok = k.sem(f"{name}_col_ps"), k.sem(f"{name}_gateT_ps"), k.sem(f"{name}_taken_ok")
        taken_ps, ones_ok, w_in = (k.sem(f"{name}_{s}") for s in ("taken_ps", "ones_ok", "w_in"))
        y_out, x_out, hot_ok, list_ps, list_ok = (k.sem(f"{name}_{s}") for s in ("y_out", "x_out", "hot_ok", "list_ps", "list_ok"))
        rows_in = [k.sem(f"{name}_rows_in{e}") for e in range(E)]
        rows_ps, rowsT_ok, out_ps, out_ok, summed = (
            k.sem(f"{name}_{s}") for s in ("rows_ps", "rowsT_ok", "out_ps", "out_ok", "summed"))
        x_back = [k.sem(f"{name}_x_back{i}") for i in range(NT // 2)]
        block = ctx.enter_context(nc.Block())
        src = d["L1_ffn_experts"].rearrange("e (f p) n -> p e f n", p=128)

        @block.sync
        def _(sp):
            sp.dma_start(w_gate[:], d["L1_ffn_gate_w"].rearrange("h (f p) e -> p (h f) e", p=128)).then_inc(gate_in, 16)
            sp.dma_start(w[:], src).then_inc(w_in, 16)
            sp.dma_start(k.sums[0:N].rearrange("(t p) d -> p t d", p=P), k.x[:]).then_inc(x_out, 16)
            sp.wait_ge(norm.y_ok, norm.base + NT)
            sp.dma_start(k.y_rows[0:N].rearrange("(t p) d -> p t d", p=P), k.y[:]).then_inc(y_out, 16)
            sp.wait_ge(x_out, 16)
            sp.wait_ge(summed, 2 * E * 16)
            sync_back(k, sp, x_back)

        @block.gpsimd
        def _(pool):
            nc.gpsimd.memset(ones[:], 1.0)
            nc.gpsimd.iota(iota[:], pattern=[[1, HALF]], base=1, channel_multiplier=0,
                           allow_small_or_imprecise_dtypes=True)
            nc.gpsimd.iota(node_id[:], pattern=[[P, NT]], base=0, channel_multiplier=1,
                           allow_small_or_imprecise_dtypes=True)
            nc.gpsimd.memset(zeros[:], 0.0).then_inc(ones_ok, 1)
            pool.wait_ge(y_out, 16)
            pool.wait_ge(list_ok, 1)
            for i in range(2 * E):
                nc.gpsimd.indirect_dma_start(rows[i], None, k.y_rows[0:N],
                                             bass.IndirectOffsetOnAxis(ap=nodes[:, i:i + 1], axis=0)).then_inc(rows_in[i // 2], 16)
            pool.wait_ge(x_out, 16)
            for i in range(2 * E):
                if i and i % 2 == 0:
                    pool.wait_ge(summed, i * 16)
                pool.wait_ge(out_ok, i + 1)
                nc.gpsimd.indirect_dma_start(k.sums[0:N], bass.IndirectOffsetOnAxis(ap=nodes[:, i:i + 1], axis=0),
                                             out[:, i % 4, :], None, compute_op=ALU.add).then_inc(summed, 16)

        @block.scalar
        def _(act):
            norm.scalar(act)
            for i in range(2 * E):
                act.wait_ge(rows_ps, i + 1)
                if i >= 2:
                    act.wait_ge(out_ps, i - 1)
                nc.scalar.copy(rowsT[:, i % 2, :, :],
                               k.bank[:, i % 2, 0:KD * HALF].rearrange("p (f n) -> p f n", f=KD)).then_inc(rowsT_ok, 1)

        @block.tensor
        def _(pe):
            def gates(t):
                if t == 0:
                    pe.wait_ge(gate_in, 16)
                pe.wait_ge(norm.yT_ok, norm.base + t + 1)
                for f in range(KD):
                    last = nc.tensor.matmul(k.bank[0:P, 5, t * E:(t + 1) * E], k.yT[:, f, tile_cols(t)], w_gate[:, f, :],
                                            start=(f == 0), stop=(f == KD - 1))
                if t == NT - 1:
                    last.then_inc(gate_ps, 1)

            norm.tensor(pe, gates)
            pe.wait_ge(ones_ok, 1)
            with pe.Fori(0, SINKHORN) as i:
                pe.wait_ge(scaled, i + 1)
                nc.tensor.matmul(k.bank[0:P, 4, 0:NT * E], ones[:], gate[:].rearrange("p t e -> p (t e)"),
                                 start=True, stop=True).then_inc(col_ps, 1)
            pe.wait_ge(scaled, SINKHORN + 1)
            for t in range(NT):
                last = nc.tensor.transpose(k.bank[0:E, t // 4, (t % 4) * P:(t % 4 + 1) * P], gate[:, t, :],
                                           k.ident[0:P, 0:P])
            last.then_inc(gateT_ps, 1)
            pe.wait_ge(taken_ok, 1)
            for t in range(NT):
                last = nc.tensor.transpose(k.bank[0:P, 4, t * E:(t + 1) * E], gateT[:, tile_cols(t)], k.ident[0:E, 0:E])
            last.then_inc(taken_ps, 1)

            for e in range(E):
                pe.wait_ge(hot_ok, e + 1)
                for t in range(NT):
                    last = nc.tensor.matmul(k.bank[0:HALF, 5, e * 4:(e + 1) * 4], hot[e][:, t, :], values[:, t, e, :],
                                            start=(t == 0), stop=(t == NT - 1))
            last.then_inc(list_ps, 1)

            def transpose_rows(i):
                pe.wait_ge(rows_in[i // 2], 32)
                if i >= 2:
                    pe.wait_ge(rowsT_ok, i - 1)
                for f in range(KD):
                    last = nc.tensor.transpose(k.bank[:, i % 2, f * HALF:(f + 1) * HALF], rows[i][:, f * 128:(f + 1) * 128],
                                               k.ident[0:HALF, 0:HALF])
                last.then_inc(rows_ps, 1)

            transpose_rows(0)
            pe.wait_ge(w_in, 16)
            for i in range(2 * E):
                if i + 1 < 2 * E:
                    transpose_rows(i + 1)
                pe.wait_ge(rowsT_ok, i + 1)
                if i >= 2:
                    pe.wait_ge(out_ok, i - 1)
                for f in range(KD):
                    last = nc.tensor.matmul(k.bank[0:HALF, 2 + i % 2, :], rowsT[:, i % 2, f, :], w[:, i // 2, f, :],
                                            start=(f == 0), stop=(f == KD - 1))
                last.then_inc(out_ps, 1)

        @block.vector
        def _(dve):
            norm.vector(dve)
            dve.wait_ge(gate_ps, 1)
            nc.vector.tensor_scalar(gate[:], k.bank[0:P, 5, 0:NT * E].rearrange("p (t e) -> p t e", t=NT), 1e-10, None,
                                    ALU.max).then_inc(scaled, 1)
            with dve.Fori(0, SINKHORN) as i:
                dve.wait_ge(col_ps, i + 1)
                nc.vector.tensor_reduce(col[:], k.bank[0:P, 4, 0:NT * E].rearrange("p (t e) -> p e t", t=NT), AX.X, ALU.add)
                dve.drain()
                nc.vector.reciprocal(col[:], col[:])
                dve.drain()
                nc.vector.tensor_tensor(gate[:], gate[:], col[:].unsqueeze(1).broadcast_to([P, NT, E]), ALU.mult)
                dve.drain()
                nc.vector.tensor_reduce(row[:], gate[:], AX.X, ALU.add)
                dve.drain()
                nc.vector.reciprocal(row[:], row[:])
                dve.drain()
                nc.vector.tensor_tensor(gate[:], gate[:], row[:].unsqueeze(2).broadcast_to([P, NT, E]),
                                        ALU.mult).then_inc(scaled, 1)
            dve.wait_ge(gateT_ps, 1)
            for c0, b, cn in ((0, 0, 4 * P), (4 * P, 1, 4 * P), (8 * P, 2, 2 * P)):
                nc.vector.tensor_copy(gateT[:, c0:c0 + cn], k.bank[0:E, b, 0:cn])
                nc.vector.tensor_copy(left[:, c0:c0 + cn], k.bank[0:E, b, 0:cn])
            dve.drain()
            def take_eight():
                nc.vector.max(top[:], left[:])
                dve.drain()
                nc.vector.match_replace(left[:], top[:], left[:], -1.0)
                dve.drain()

            rounds = (TOP - 1) // 8
            with dve.Fori(0, rounds // 6) as i:
                for _ in range(6):
                    take_eight()
            for _ in range(rounds % 6):
                take_eight()
            nc.vector.max(top[:], left[:])
            dve.drain()
            least = top[:, (TOP - 1) % 8:(TOP - 1) % 8 + 1]
            nc.vector.tensor_scalar(equal[:], gateT[:], least, None, ALU.is_equal)
            nc.vector.tensor_scalar(left[:], gateT[:], least, None, ALU.is_gt)
            dve.drain()
            nc.vector.tensor_reduce(above[:, 0:1], left[:], AX.X, ALU.add)
            dve.wait_ge(ones_ok, 1)
            nc.vector.tensor_tensor_scan(count[:], equal[:], zeros[:], 0.0, ALU.add, ALU.add)
            dve.drain()
            nc.vector.tensor_scalar(above[:, 1:2], above[:, 0:1], -1.0, float(TOP), ALU.mult, ALU.add)
            dve.drain()
            nc.vector.scalar_tensor_tensor(out=count[:], in0=count[:], scalar=above[:, 1:2], in1=equal[:],
                                           op0=ALU.is_le, op1=ALU.mult)
            dve.drain()
            nc.vector.tensor_tensor(gateT[:], count[:], left[:], ALU.add)
            dve.drain()
            nc.vector.tensor_tensor_scan(count[:], gateT[:], zeros[:], 0.0, ALU.add, ALU.add)
            dve.drain()
            nc.vector.tensor_tensor(gateT[:], gateT[:], count[:], ALU.mult).then_inc(taken_ok, 1)
            dve.wait_ge(taken_ps, 1)
            nc.vector.tensor_copy(place[:], k.bank[0:P, 4, 0:NT * E].rearrange("p (t e) -> p t e", t=NT))
            dve.drain()
            nc.vector.tensor_scalar(taken[:], place[:], 0.0, None, ALU.is_gt)
            dve.drain()
            nc.vector.tensor_reduce(row[:], taken[:], AX.X, ALU.add)
            nc.vector.tensor_scalar(share[:], gate[:], 0.5, None, ALU.is_gt)
            dve.drain()
            nc.vector.tensor_scalar(row[:], row[:], 1.0, None, ALU.add)
            nc.vector.tensor_tensor(share[:], share[:], taken[:], ALU.mult)
            dve.drain()
            nc.vector.reciprocal(row[:], row[:])
            dve.drain()
            nc.vector.tensor_tensor(share[:], share[:], row[:].unsqueeze(2).broadcast_to([P, NT, E]), ALU.mult)
            nc.vector.tensor_scalar(values[:, :, :, 1], place[:], float(HALF), None, ALU.is_gt)
            dve.drain()
            nc.vector.tensor_tensor(values[:, :, :, 0], taken[:], values[:, :, :, 1], ALU.subtract)
            nc.vector.scalar_tensor_tensor(out=place[:], in0=values[:, :, :, 1], scalar=float(-HALF), in1=place[:],
                                           op0=ALU.mult, op1=ALU.add)
            dve.wait_ge(y_out, 16)
            dve.drain()
            for half in range(2):
                nc.vector.tensor_tensor(values[:, :, :, 2 + half], values[:, :, :, half], share[:], ALU.mult)
            dve.drain()
            for half in range(2):
                nc.vector.tensor_tensor(values[:, :, :, half], values[:, :, :, half],
                                        node_id[:].unsqueeze(2).broadcast_to([P, NT, E]), ALU.mult)
            dve.drain()
            for e in range(E):
                nc.vector.tensor_tensor(hot[e], place[:, :, e:e + 1].broadcast_to([P, NT, HALF]),
                                        iota[:].unsqueeze(1).broadcast_to([P, NT, HALF]), ALU.is_equal).then_inc(hot_ok, 1)
            dve.wait_ge(list_ps, 1)
            lists = k.bank[0:HALF, 5, 0:4 * E].rearrange("s (e c h) -> s e c h", e=E, c=2)
            nc.vector.tensor_copy(nodes[:].rearrange("s (e h) -> s e h", e=E), lists[:, :, 0, :])
            nc.vector.tensor_copy(shares[:].rearrange("s (e h) -> s e h", e=E), lists[:, :, 1, :])
            dve.drain()
            dve.sem_inc(list_ok, 1)
            for i in range(2 * E):
                dve.wait_ge(out_ps, i + 1)
                if i >= 4:
                    dve.wait_ge(summed, (i // 2 - 1) * 32)
                nc.vector.tensor_scalar(out[:, i % 4, :], k.bank[0:HALF, 2 + i % 2, :], shares[:, i:i + 1], None,
                                        ALU.mult).then_inc(out_ok, 1)
            vector_back(k, dve, x_back)


HEADS, DH = 8, 64
SCORE_RING = 5
PIECES = [(0, 4), (4, 7), (7, 10)]


def attention_layer(k, name):
    nc, d = k.nc, k.d
    PAIRS, STEPS = HEADS // 2, 2 * NT
    with ExitStack() as ctx:
        norm = Norm(k, name, ctx, have_stats=True)
        qT = k.sb(f"{name}_qT", [128, PAIRS, N], F32, ctx)
        kT = k.sb(f"{name}_kT", [128, PAIRS, N], F32, ctx)
        v = k.sb(f"{name}_v", [P, NT, D], F32, ctx)
        work = k.sb(f"{name}_work", [128, KD * 3 * D], F32, ctx)
        w_qkv = work[:].rearrange("p (f n) -> p f n", f=KD)
        prob = work[0:P, 0:2 * N].rearrange("p (b n) -> p b n", b=2)
        probT = work[0:P, 2 * N:4 * N].rearrange("p (b s n) -> p b s n", b=2, s=NT)
        w_ff = qT[:].rearrange("p h n -> p (h n)")[:, 0:KD * D].rearrange("p (f n) -> p f n", f=KD)
        q_now = k.sb(f"{name}_q_now", [128, 2, N], F32, ctx)
        b_v = k.sb(f"{name}_b_v", [P, D], F32, ctx)
        b_ff = k.sb(f"{name}_b_ff", [P, D], F32, ctx)
        b_qk = k.sb(f"{name}_b_qk", [128, 12], F32, ctx)
        low = k.sb(f"{name}_low", [P, 2, 3], F32, ctx)
        den_now = k.sb(f"{name}_den_now", [P, 4, 1], F32, ctx)
        den = k.sb(f"{name}_den", [P, HEADS, NT], F32, ctx)
        msg = k.y
        spare = k.y[:].rearrange("p t d -> p (t d)")
        b_in, spilled, b_ok = (k.sem(f"{name}_{s}") for s in ("b_in", "spilled", "b_ok"))
        w_in = [k.sem(f"{name}_w_in{i}") for i in range(3)]
        floor_ok, ln_ok, mask_ok = (k.sem(f"{name}_{s}") for s in ("floor_ok", "ln_ok", "mask_ok"))
        qk_ps, qk_ok, v_ps, v_ok = (k.sem(f"{name}_{s}") for s in ("qk_ps", "qk_ok", "v_ps", "v_ok"))
        q_ok, score_ps, part_ok, prob_ok = (k.sem(f"{name}_{s}") for s in ("q_ok", "score_ps", "part_ok", "prob_ok"))
        probT_ps, probT_a, probT_v = (k.sem(f"{name}_{s}") for s in ("probT_ps", "probT_a", "probT_v"))
        pv_ps, pv_ok, msg_ok, msgT_ps, msgT_ok, ff_in, ff_ps, ff_ok = (
            k.sem(f"{name}_{s}") for s in ("pv_ps", "pv_ok", "msg_ok", "msgT_ps", "msgT_ok", "ff_in", "ff_ps", "ff_ok"))
        seen = k.sem(f"{name}_seen")
        block = ctx.enter_context(nc.Block())

        @block.sync
        def _(sp):
            sp.dma_start(b_qk[:], d["L2_gnn_b_qkv_P"].rearrange("p a f -> p (a f)")).then_inc(b_in, 16)
            sp.dma_start(b_v[:], d["L2_gnn_b_qkv"][2 * D:3 * D].partition_broadcast(P)).then_inc(b_in, 16)
            sp.dma_start(b_ff[:], d["L2_gnn_b_ff"].partition_broadcast(P)).then_inc(b_in, 16)
            src = d["L2_gnn_W_qkv_T"].rearrange("(f p) n -> p f n", p=128)
            for i in range(3):
                sp.dma_start(w_qkv[:, :, i * D:(i + 1) * D], src[:, :, i * D:(i + 1) * D]).then_inc(w_in[i], 16)
            sp.dma_start(k.adj_saved, k.adj[:]).then_inc(spilled, 16)
            sp.wait_ge(q_ok, HEADS)
            sp.dma_start(w_ff, d["L2_gnn_W_ff_T"].rearrange("(f p) n -> p f n", p=128)).then_inc(ff_in, 16)

        @block.gpsimd
        def _(pool):
            nc.gpsimd.memset(q_now[DH:128, 0, :], 0.0)
            nc.gpsimd.memset(q_now[0:DH, 1, :], 0.0)
            pool.wait_ge(qk_ok, 24)
            for u in range(2):
                rows = slice(DH * u, DH * (u + 1))
                nc.gpsimd.tensor_copy(q_now[rows, u, :], qT[rows, 0, :]).then_inc(q_ok, 1)
            with pool.Fori(1, PAIRS) as pair:
                for u in range(2):
                    rows = slice(DH * u, DH * (u + 1))
                    pool.drain()
                    pool.wait_ge(score_ps, (pair * STEPS - NT + NT * u) * 3)
                    pool.sem_inc(seen, 1)
                    nc.gpsimd.tensor_copy(q_now[rows, u, :], qT[rows, bass.ds(pair, 1), :]).then_inc(q_ok, 1)

        @block.tensor
        def _(pe):
            norm.tensor(pe)
            pe.wait_ge(norm.yT_ok, norm.base + NT)
            for n in range(24):
                if n % 12 == 0:
                    pe.wait_ge(w_in[n // 12], 16)
                c0, cn = TOKENS[n % 3]
                if n >= 3:
                    pe.wait_ge(qk_ok, n - 2)
                for f in range(KD):
                    last = nc.tensor.matmul(k.bank[:, n % 3, 0:cn], w_qkv[:, f, n // 3 * 128:(n // 3 + 1) * 128],
                                            k.yT[:, f, c0:c0 + cn], start=(f == 0), stop=(f == KD - 1))
                last.then_inc(qk_ps, 1)
            pe.wait_ge(w_in[2], 16)
            for t in range(NT):
                if t >= 2:
                    pe.wait_ge(v_ok, t - 1)
                for f in range(KD):
                    last = nc.tensor.matmul(k.bank[0:P, 3 + t % 2, :], k.yT[:, f, tile_cols(t)], w_qkv[:, f, 2 * D:3 * D],
                                            start=(f == 0), stop=(f == KD - 1))
                last.then_inc(v_ps, 1)
            pe.wait_ge(qk_ok, 24)
            pe.wait_ge(v_ok, NT)

            def scores(pair, n):
                if n % NT == 0:
                    pe.wait_ge(q_ok, pair * 2 + n // NT + 1)
                for c, (c0, cn) in enumerate(TOKENS):
                    i = 3 * n + c
                    pe.wait_ge(part_ok, pair * STEPS * 3 + i + 1)
                    nc.tensor.matmul(k.bank[0:P, i % SCORE_RING, 0:cn], q_now[:, n // NT, tile_cols(n % NT)],
                                     kT[:, bass.ds(pair, 1), c0:c0 + cn], start=True, stop=True).then_inc(score_ps, 1)

            def transposes(pair, n, piece):
                if piece == 0:
                    pe.wait_ge(prob_ok, pair * STEPS + n + 1)
                i = n * 3 + piece
                if piece == 0 and n:
                    pe.wait_ge(probT_v, pair * STEPS + n)
                if piece == 1 and n:
                    pe.wait_ge(probT_a, (pair * STEPS + n) * 2)
                if piece == 2:
                    pe.wait_ge(probT_a, (pair * STEPS + n) * 2 + 1)
                first, end = PIECES[piece]
                for s in range(first, end):
                    last = nc.tensor.transpose(k.bank[0:P, 5 + i % 2, (s - first) * P:(s - first + 1) * P],
                                               prob[:, n % 2, tile_cols(s)], k.ident[0:P, 0:P])
                last.then_inc(probT_ps, 1)

            def values(pair, n):
                pe.wait_ge(probT_a, (pair * STEPS + n) * 2 + 2)
                pe.wait_ge(probT_v, pair * STEPS + n + 1)
                pe.wait_ge(pv_ok, pair * STEPS + n + 1)
                for s in range(NT):
                    last = nc.tensor.matmul(k.bank[0:P, 7, 0:DH], probT[:, n % 2, s, :],
                                            v[:, s, bass.ds(pair * 2 * DH + n // NT * DH, DH)],
                                            start=(s == 0), stop=(s == NT - 1))
                last.then_inc(pv_ps, 1)

            with pe.Fori(0, PAIRS) as pair:
                scores(pair, 0)
                for n in range(STEPS + 1):
                    if n + 1 < STEPS:
                        scores(pair, n + 1)
                    if n < STEPS:
                        transposes(pair, n, 0)
                        transposes(pair, n, 1)
                    if n >= 1:
                        values(pair, n - 1)
                    if n < STEPS:
                        transposes(pair, n, 2)
            for t in range(NT):
                pe.wait_ge(msg_ok, t + 1)
                if t >= 2:
                    pe.wait_ge(msgT_ok, t - 1)
                for f in range(KD):
                    last = nc.tensor.transpose(k.bank[:, 6 + t % 2, f * P:(f + 1) * P], msg[:, t, f * 128:(f + 1) * 128],
                                               k.ident[0:P, 0:P])
                last.then_inc(msgT_ps, 1)
            pe.wait_ge(ff_in, 16)
            for t in range(NT):
                pe.wait_ge(msgT_ok, t + 1)
                if t >= 2:
                    pe.wait_ge(ff_ok, t - 1)
                for f in range(KD):
                    last = nc.tensor.matmul(k.bank[0:P, t % 2, :], k.yT[:, f, tile_cols(t)], w_ff[:, f, :],
                                            start=(f == 0), stop=(f == KD - 1))
                last.then_inc(ff_ps, 1)

        @block.scalar
        def _(act):
            norm.scalar(act)
            act.wait_ge(b_ok, 1)
            for n in range(24):
                f, (c0, cn) = n // 3, TOKENS[n % 3]
                act.wait_ge(qk_ps, n + 1)
                out = qT if f < PAIRS else kT
                nc.scalar.activation(out[:, f % PAIRS, c0:c0 + cn], k.bank[:, n % 3, 0:cn], ACT.Identity,
                                     bias=b_qk[:, f:f + 1], scale=-DH ** -0.5 if f < PAIRS else 1.0).then_inc(qk_ok, 1)
                t = n // 2
                if n % 2 == 0 or t >= NT:
                    continue
                act.wait_ge(floor_ok, t + 1)
                nc.scalar.activation(spare[:, t % 4 * N:(t % 4 + 1) * N], spare[:, t % 4 * N:(t % 4 + 1) * N],
                                     ACT.Ln).then_inc(ln_ok, 1)

            def exponentials(pair, n):
                act.wait_ge(part_ok, pair * STEPS * 3 + 3 * n + 3 + SCORE_RING)
                nc.scalar.activation(prob[:, n % 2, :], prob[:, n % 2, :], ACT.Exp, bias=low[:, n % 2, 2:3], scale=-1.0,
                                     accum_out=den_now[:, n % 4, :]).then_inc(prob_ok, 1)

            with act.Fori(0, PAIRS) as pair:
                exponentials(pair, 0)
                for n in range(STEPS):
                    for piece in (0, 2):
                        if piece == 2 and n + 1 < STEPS:
                            exponentials(pair, n + 1)
                        act.wait_ge(probT_ps, (pair * STEPS + n) * 3 + piece + 1)
                        first, end = PIECES[piece]
                        nc.scalar.copy(probT[:, n % 2, first:end, :].rearrange("p s n -> p (s n)"),
                                       k.bank[0:P, 5 + (n * 3 + piece) % 2, 0:(end - first) * P]).then_inc(probT_a, 1)
            for t in range(NT):
                act.wait_ge(msgT_ps, t + 1)
                nc.scalar.copy(k.yT[:, :, tile_cols(t)],
                               k.bank[:, 6 + t % 2, 0:KD * P].rearrange("p (f n) -> p f n", f=KD)).then_inc(msgT_ok, 1)

        @block.vector
        def _(dve):
            norm.vector(dve)
            dve.wait_ge(b_in, 48)
            nc.vector.tensor_scalar(b_qk[:, 0:PAIRS], b_qk[:, 0:PAIRS], -DH ** -0.5, None, ALU.mult).then_inc(b_ok, 1)
            dve.wait_ge(norm.yT_ps, norm.base + NT)

            def floor(t):
                nc.vector.tensor_scalar(spare[:, t % 4 * N:(t % 4 + 1) * N], k.adj[:, t, :], 1.0, None,
                                        ALU.max).then_inc(floor_ok, 1)

            def values(t):
                dve.wait_ge(v_ps, t + 1)
                nc.vector.tensor_tensor(v[:, t, :], k.bank[0:P, 3 + t % 2, :], b_v[:], ALU.add).then_inc(v_ok, 1)

            for t in range(4):
                floor(t)
            dve.wait_ge(spilled, 16)
            for t in range(NT):
                dve.wait_ge(ln_ok, t + 1)
                nc.vector.tensor_scalar(k.adj[:, t, :], k.adj[:, t, :], 0.0, BIG, ALU.is_equal, ALU.mult)
                dve.drain()
                nc.vector.tensor_tensor(k.adj[:, t, :], k.adj[:, t, :], spare[:, t % 4 * N:(t % 4 + 1) * N],
                                        ALU.subtract)
                dve.drain()
                if t + 4 < NT:
                    floor(t + 4)
            for t in range(NT):
                values(t)
            dve.drain()
            dve.sem_inc(part_ok, SCORE_RING)
            dve.sem_inc(pv_ok, 1)

            def minima(pair, n):
                for c, (c0, cn) in enumerate(TOKENS):
                    i = 3 * n + c
                    dve.wait_ge(score_ps, pair * STEPS * 3 + i + 1)
                    dve.sem_inc(seen, 1)
                    nc.vector.tensor_tensor_reduce(out=prob[:, n % 2, c0:c0 + cn], in0=k.bank[0:P, i % SCORE_RING, 0:cn],
                                                   in1=k.adj[:, n % NT, c0:c0 + cn], scale=1.0,
                                                   scalar=low[:, n % 2, c - 1:c] if c else 3.0 * BIG,
                                                   op0=ALU.add, op1=ALU.min, accum_out=low[:, n % 2, c:c + 1])
                    dve.drain()
                    dve.sem_inc(part_ok, 1)

            def piece(pair, n):
                dve.wait_ge(probT_ps, (pair * STEPS + n) * 3 + 2)
                first, end = PIECES[1]
                nc.vector.tensor_copy(probT[:, n % 2, first:end, :].rearrange("p s n -> p (s n)"),
                                      k.bank[0:P, 5 + (n * 3 + 1) % 2, 0:(end - first) * P]).then_inc(probT_v, 1)

            def sums(pair, n):
                dve.wait_ge(pv_ps, pair * STEPS + n + 1)
                nc.vector.tensor_copy(msg[:, n % NT, bass.ds(pair * 2 * DH + n // NT * DH, DH)],
                                      k.bank[0:P, 7, 0:DH]).then_inc(pv_ok, 1)
                nc.vector.tensor_copy(den[:, bass.ds(pair * 2 + n // NT, 1), n % NT:n % NT + 1], den_now[:, n % 4, :])

            with dve.Fori(0, PAIRS) as pair:
                for n in range(STEPS + 2):
                    if n < STEPS:
                        minima(pair, n)
                    if 1 <= n <= STEPS:
                        piece(pair, n - 1)
                    if n >= 2:
                        sums(pair, n - 2)
                dve.drain()
            nc.vector.reciprocal(den[:], den[:])
            dve.drain()
            nc.vector.tensor_tensor(den[:], den[:], k.has_in[:, :, 0].unsqueeze(1).broadcast_to([P, HEADS, NT]), ALU.mult)
            dve.drain()
            for t in range(NT):
                row = msg[:, t, :].rearrange("p (h c) -> p h c", h=HEADS)
                nc.vector.tensor_tensor(row, row, den[:, :, t:t + 1].broadcast_to([P, HEADS, DH]),
                                        ALU.mult).then_inc(msg_ok, 1)
            for t in range(NT):
                nc.vector.tensor_tensor(k.x[:, t, :], k.x[:, t, :], b_ff[:], ALU.add)
            for t in range(NT):
                dve.drain() if t == 0 else None
                dve.wait_ge(ff_ps, t + 1)
                nc.vector.tensor_tensor(k.x[:, t, :], k.x[:, t, :], k.bank[0:P, t % 2, :], ALU.add).then_inc(ff_ok, 1)
                dve.wait_ge(ff_ok, t + 1)
                nc.vector.bn_stats(k.stats[:, t, :], k.x[:, t, :])
            dve.drain()


F2 = 256
GROUPS = [(0, 3), (3, 6), (6, 8), (8, 10)]


def merged_layer(k, name):
    nc, d = k.nc, k.d
    TABLE = KD * F2
    RING = 8
    with ExitStack() as ctx:
        norm = Norm(k, name, ctx, have_stats=True)
        w_g1 = k.sb(f"{name}_w_g1", [128, KD, D], F32, ctx)
        b_g1 = k.sb(f"{name}_b_g1", [128, KD], F32, ctx)
        w_g2 = k.sb(f"{name}_w_g2", [128, KD, E], F32, ctx)
        b_g2 = k.sb(f"{name}_b_g2", [128, E], F32, ctx)
        b_g2_col = k.sb(f"{name}_b_g2_col", [E, 1], F32, ctx)
        tables = k.sb(f"{name}_tables", [128, RING, TABLE], F32, ctx)
        w1 = k.sb(f"{name}_w1", [128, KD, F2], F32, ctx)
        w2 = k.sb(f"{name}_w2", [128, F2 // 128, D], F32, ctx)
        b1 = k.sb(f"{name}_b1", [128, 2], F32, ctx)
        tv_b1 = k.sb(f"{name}_tv_b1", [128, E, 2], F32, ctx)
        rows = k.sb(f"{name}_rows", [E + 1, 3, D], F32, ctx)
        coef = k.sb(f"{name}_coef", [E + 1, 2, P], F32, ctx)
        hidden = k.sb(f"{name}_hidden", [128, 2, 417], F32, ctx)
        part = k.sb(f"{name}_part", [128, KD, 3], F32, ctx)
        mean_h = k.sb(f"{name}_mean_h", [128, KD], F32, ctx)
        mean_wide = k.sb(f"{name}_mean_wide", [128, KD, 128], F32, ctx)
        g = k.sb(f"{name}_g", [128, E], F32, ctx)
        norm_g = k.sb(f"{name}_norm_g", [P, 2, D], F32, ctx)
        hT = k.sb(f"{name}_hT", [128, 2, N], F32, ctx)
        res = k.sb(f"{name}_res", [P, NT, D], F32, ctx)
        stats = k.sb(f"{name}_stats2", [P, NT, 6], F32, ctx)
        mv = k.sb(f"{name}_mv2", [P, NT, 2], F32, ctx)
        rstd = k.sb(f"{name}_rstd2", [P, NT, 1], F32, ctx)
        w_in, small_in, tv_in = k.sem(f"{name}_w_in"), k.sem(f"{name}_small_in"), [k.sem(f"{name}_tv_in{n}") for n in range(2 * E)]
        coef_ok, gate_ps, gate_ok, mean_ok, g_ps, g_ok = (
            k.sem(f"{name}_{s}") for s in ("coef_ok", "gate_ps", "gate_ok", "mean_ok", "g_ps", "g_ok"))
        merged, coef8_ok, w1_ok, w2_ok, norm_ps = (
            k.sem(f"{name}_{s}") for s in ("merged", "coef8_ok", "w1_ok", "w2_ok", "norm_ps"))
        h_ps, h_ok, out_ps, out_used, var_ok, std_ok = (
            k.sem(f"{name}_{s}") for s in ("h_ps", "h_ok", "out_ps", "out_used", "res_var_ok", "res_std_ok"))
        block = ctx.enter_context(nc.Block())
        src1 = d["L2_ffn_tv_W1_T"].rearrange("e (f p) n -> p e f n", p=128)
        src2 = d["L2_ffn_tv_W2_T"].rearrange("e (f p) n -> p e f n", p=128)

        @block.sync
        def _(sp):
            sp.dma_start(b_g1[:], d["L2_ffn_gfc1_b_P"].rearrange("p a f -> p (a f)")).then_inc(small_in, 16)
            sp.dma_start(b_g2[:], d["L2_ffn_gfc2_b"].partition_broadcast(128)).then_inc(small_in, 16)
            sp.dma_start(b_g2_col[:], d["L2_ffn_gfc2_b"].unsqueeze(1)).then_inc(small_in, 16)
            sp.dma_start(b1[:], d["L2_ffn_b1_P"].rearrange("p a f -> p (a f)")).then_inc(small_in, 16)
            sp.dma_start(tv_b1[:], d["L2_ffn_tv_b1_P"]).then_inc(small_in, 16)
            for i, (table, shared) in enumerate((("tv_b2", "b2"), ("tv_ln_g", "ln_g"), ("tv_ln_b", "ln_b"))):
                sp.dma_start(rows[0:E, i, :], d[f"L2_ffn_{table}"]).then_inc(small_in, 16)
                sp.dma_start(rows[E:E + 1, i, :], d[f"L2_ffn_{shared}"].unsqueeze(0)).then_inc(small_in, 16)
            sp.dma_start(w_g1[:], d["L2_ffn_gfc1_w_T"].rearrange("(f p) n -> p f n", p=128)).then_inc(w_in, 16)
            sp.dma_start(w_g2[:], d["L2_ffn_gfc2_w_T"].rearrange("(f p) n -> p f n", p=128)).then_inc(w_in, 16)
            sp.dma_start(w1[:], d["L2_ffn_W1_T"].rearrange("(f p) n -> p f n", p=128)).then_inc(w_in, 16)
            sp.dma_start(w2[:], d["L2_ffn_W2_T"].rearrange("(f p) n -> p f n", p=128)).then_inc(w_in, 16)
            for n in range(2 * E):
                if n >= RING:
                    sp.wait_ge(merged, n - RING + 1)
                if n < E:
                    sp.dma_start(tables[:, n % RING, :].rearrange("p (f n) -> p f n", f=KD), src1[:, n]).then_inc(tv_in[n], 16)
                else:
                    sp.dma_start(tables[:, n % RING, :].rearrange("p (f n) -> p f n", n=D), src2[:, n - E]).then_inc(tv_in[n], 16)
            sp.dma_start(k.adj[:], k.adj_saved).then_inc(k.adj_in, 16)

        @block.gpsimd
        def _(pool):
            nc.gpsimd.memset(coef[:, 0, :], 1.0)
            nc.gpsimd.memset(coef[:, 1, :], 1.0 - E * 0.03)
            pool.drain()
            nc.gpsimd.memset(coef[0:E, 1, :], 0.03).then_inc(coef_ok, 1)

        @block.tensor
        def _(pe):
            norm.tensor(pe)
            pe.wait_ge(coef_ok, 1)
            pe.wait_ge(small_in, 16 * 11)
            for i in range(2):
                last = nc.tensor.matmul(k.bank[0:P, 3 + i, :], coef[:, 1, :], rows[:, 1 + i, :], start=True, stop=True)
            last.then_inc(norm_ps, 1)
            pe.wait_ge(w_in, 64)
            pe.wait_ge(norm.yT_ok, norm.base + NT)
            for n in range(12):
                f, (c0, cn) = n // 3, TOKENS[n % 3]
                if n >= 3:
                    pe.wait_ge(gate_ok, n - 2)
                for kk in range(KD):
                    last = nc.tensor.matmul(k.bank[:, n % 3, 0:cn], w_g1[:, kk, f * 128:(f + 1) * 128],
                                            k.yT[:, kk, c0:c0 + cn], start=(kk == 0), stop=(kk == KD - 1))
                last.then_inc(gate_ps, 1)
            pe.wait_ge(mean_ok, 1)
            for f in range(KD):
                nc.tensor.matmul(k.bank[:, 0, 0:E], mean_wide[:, f, :], w_g2[:, f, :], start=(f == 0), stop=(f == KD - 1))
            for f in range(KD):
                last = nc.tensor.matmul(k.bank[0:E, 1, 0:P], w_g2[:, f, :], mean_wide[:, f, 0:P],
                                        start=(f == 0), stop=(f == KD - 1))
            last.then_inc(g_ps, 1)
            pe.wait_ge(w1_ok, 1)
            for n in range(6):
                f, (c0, cn) = n // 3, TOKENS[n % 3]
                if n >= 3:
                    pe.wait_ge(h_ok, n - 2)
                for kk in range(KD):
                    last = nc.tensor.matmul(k.bank[:, n % 3, 0:cn], w1[:, kk, f * 128:(f + 1) * 128],
                                            k.yT[:, kk, c0:c0 + cn], start=(kk == 0), stop=(kk == KD - 1))
                last.then_inc(h_ps, 1)
            pe.wait_ge(h_ok, 6)
            pe.wait_ge(w2_ok, 1)
            for t in range(NT):
                if t >= 4:
                    pe.wait_ge(out_used, t - 3)
                nc.tensor.matmul(k.bank[0:P, 4 + t % 4, :], coef[:, 0, :], rows[:, 0, :], start=True, stop=False)
                for f in range(2):
                    last = nc.tensor.matmul(k.bank[0:P, 4 + t % 4, :], hT[:, f, tile_cols(t)], w2[:, f, :],
                                            start=False, stop=(f == 1))
                last.then_inc(out_ps, 1)

        @block.scalar
        def _(act):
            norm.scalar(act)
            act.wait_ge(small_in, 16 * 11)
            for n in range(12):
                f, (c0, cn) = n // 3, TOKENS[n % 3]
                act.wait_ge(gate_ps, n + 1)
                if n >= 2:
                    act.wait_ge(gate_ok, n - 1)
                nc.scalar.activation(hidden[:, n % 2, 0:cn], k.bank[:, n % 3, 0:cn], ACT.Relu, bias=b_g1[:, f:f + 1],
                                     accum_out=part[:, f, n % 3:n % 3 + 1]).then_inc(gate_ok, 1)
            act.drain()
            act.sem_inc(gate_ok, 1)
            act.wait_ge(w1_ok, 1)
            for n in range(6):
                f, (c0, cn) = n // 3, TOKENS[n % 3]
                act.wait_ge(h_ps, n + 1)
                nc.scalar.activation(hT[:, f, c0:c0 + cn], k.bank[:, n % 3, 0:cn], ACT.Relu,
                                     bias=b1[:, f:f + 1]).then_inc(h_ok, 1)
            for group, (first, end) in enumerate(GROUPS):
                act.wait_ge(var_ok, group + 1)
                nc.scalar.activation(rstd[:, first:end], rstd[:, first:end], ACT.Sqrt).then_inc(std_ok, 1)

        @block.vector
        def _(dve):
            norm.vector(dve)
            dve.wait_ge(norm_ps, 1)
            nc.vector.tensor_copy(norm_g[:], k.bank[0:P, 3:5, :])
            dve.wait_ge(gate_ok, 13)
            nc.vector.tensor_reduce(mean_h[:], part[:], AX.X, ALU.add)
            dve.drain()
            nc.vector.tensor_scalar(mean_h[:], mean_h[:], 1.0 / N, None, ALU.mult)
            dve.drain()
            nc.vector.tensor_copy(mean_wide[:], mean_h[:].unsqueeze(2).broadcast_to([128, KD, 128])).then_inc(mean_ok, 1)
            dve.wait_ge(g_ps, 1)
            dve.wait_ge(small_in, 16 * 11)
            nc.vector.tensor_tensor(g[:], k.bank[:, 0, 0:E], b_g2[:], ALU.add)
            nc.vector.tensor_scalar(coef[0:E, 0, :], k.bank[0:E, 1, 0:P], b_g2_col[:], None, ALU.add)
            dve.drain()
            dve.wait_ge(w_in, 64)
            for n in range(2 * E):
                e = n % E
                into = w1[:].rearrange("p f n -> p (f n)") if n < E else w2[:].rearrange("p f n -> p (f n)")
                dve.wait_ge(tv_in[n], 16)
                nc.vector.scalar_tensor_tensor(out=into, in0=tables[:, n % RING, :], scalar=g[:, e:e + 1], in1=into,
                                               op0=ALU.mult, op1=ALU.add).then_inc(merged, 1)
                if n < E:
                    nc.vector.scalar_tensor_tensor(out=b1[:], in0=tv_b1[:, e, :], scalar=g[:, e:e + 1], in1=b1[:],
                                                   op0=ALU.mult, op1=ALU.add)
                dve.drain()
                if n == E - 1:
                    dve.sem_inc(w1_ok, 1)
            dve.sem_inc(w2_ok, 1)
            for t in range(NT):
                nc.vector.tensor_tensor(k.x[:, t, :], k.x[:, t, :], norm_g[:, 1, :], ALU.add)
            dve.drain()

            def finish(first, end, group):
                nc.vector.tensor_scalar(rstd[:, first:end], mv[:, first:end, 1:2], 1e-5, None, ALU.add).then_inc(var_ok, 1)
                for t in range(first, end):
                    nc.vector.scalar_tensor_tensor(out=res[:, t, :], in0=res[:, t, :], scalar=mv[:, t, 0:1],
                                                   in1=norm_g[:, 0, :], op0=ALU.subtract, op1=ALU.mult)
                dve.wait_ge(std_ok, group + 1)
                nc.vector.reciprocal(rstd[:, first:end], rstd[:, first:end])
                dve.drain()
                for t in range(first, end):
                    nc.vector.scalar_tensor_tensor(out=k.x[:, t, :], in0=res[:, t, :], scalar=rstd[:, t, :],
                                                   in1=k.x[:, t, :], op0=ALU.mult, op1=ALU.add)
                dve.drain()
                for t in range(first, end):
                    nc.vector.bn_stats(k.stats[:, t, :], k.x[:, t, :])

            for group, (first, end) in enumerate(GROUPS):
                for t in range(first, end):
                    dve.wait_ge(out_ps, t + 1)
                    nc.vector.tensor_tensor(res[:, t, :], k.y[:, t, :], k.bank[0:P, 4 + t % 4, :], ALU.add).then_inc(out_used, 1)
                    dve.wait_ge(out_used, t + 1)
                    nc.vector.bn_stats(stats[:, t, :], res[:, t, :])
                    dve.drain()
                    nc.vector.bn_aggr(mv[:, t, :], stats[:, t, :])
                dve.drain()
                finish(first, end, group)
            dve.drain()


def top_two_layer(k, name):
    nc, d = k.nc, k.d
    H = 1024
    FH = H // 128
    with ExitStack() as ctx:
        norm = Norm(k, name, ctx, have_stats=True)
        router = Router(k, name, d["L3_ffn_router_w"], d["L3_ffn_router_b"], ctx)
        w1 = k.sb(f"{name}_w1", [128, 2, KD, 2 * H], F32, ctx)
        w2 = k.sb(f"{name}_w2", [128, 2, FH, D], F32, ctx)
        b1 = k.sb(f"{name}_b1", [128, 2, 2 * H], F32, ctx)
        b2 = k.sb(f"{name}_b2", [E, D], F32, ctx)
        rows = k.sb(f"{name}_rows", [SLOTS, D], F32, ctx)
        rowsT = k.sb(f"{name}_rowsT", [128, KD, SLOTS], F32, ctx)
        gate = k.sb(f"{name}_gate", [SLOTS, 2, 512], F32, ctx)
        sig = k.sb(f"{name}_sig", [SLOTS, 2, 512], F32, ctx)
        hid = k.sb(f"{name}_hid", [SLOTS, 2, 512], F32, ctx)
        hT = k.sb(f"{name}_hT", [128, FH, SLOTS], F32, ctx)
        out = k.sb(f"{name}_out", [SLOTS, D], F32, ctx)
        yT_flat = k.yT[0:P].rearrange("p f n -> p (f n)")
        hot = yT_flat[:, 0:2 * NT * SLOTS].rearrange("p (n s) -> p n s", n=2 * NT)
        values = yT_flat[:, 2 * NT * SLOTS:2 * NT * (SLOTS + 3 * LISTS)].rearrange("p (n c i) -> p n c i", n=2 * NT, c=3)
        disp = Dispatch(k, name, ctx, hot, values, rows[:], out[:])
        w_in, b_in, b2_in, out_done, rowsT_ok, items_done = (
            k.sem(f"{name}_{s}") for s in ("w_in", "b_in", "b2_in", "out_done", "rowsT_ok", "items_done"))
        gate_ps, up_ps, gate_ok, sig_ok, hid_ok, hT_ps, hT_ok = (
            k.sem(f"{name}_{s}") for s in ("gate_ps", "up_ps", "gate_ok", "sig_ok", "hid_ok", "hT_ps", "hT_ok"))
        bias_ps, bias_added = k.sem(f"{name}_bias_ps"), k.sem(f"{name}_bias_added")
        block = ctx.enter_context(nc.Block())
        src1 = d["L3_ffn_gate_up_proj"].rearrange("e (f p) n -> p e f n", p=128)
        src2 = d["L3_ffn_down_proj"].rearrange("e (f p) n -> p e f n", p=128)
        src_b = d["L3_ffn_gate_up_proj_bias"].rearrange("(a e) n -> a e n", a=1)

        @block.sync
        def _(sp):
            router.sync(sp)
            sp.dma_start(b2[:], d["L3_ffn_down_proj_bias"]).then_inc(b2_in, 16)
            disp.sync_y(sp, norm)
            for e in range(2):
                if e:
                    sp.wait_ge(w_in, 32)
                    sp.wait_ge(b_in, 16)
                sp.dma_start(w1[:, e], src1[:, e]).then_inc(w_in, 16)
                sp.dma_start(w2[:, e], src2[:, e]).then_inc(w_in, 16)
                sp.dma_start(b1[:, e, :], src_b[0, e].partition_broadcast(128)).then_inc(b_in, 16)
            disp.sync_x(sp, bias_added)
            with sp.Fori(0, E // 2 - 1) as h:
                for u in range(2):
                    e = h * 2 + u
                    end = sp.value_load(disp.first_item[0:1, bass.ds(e + 1, 1)], min_val=1, max_val=ITEMS)
                    sp.wait_ge(w_in, e * 32 + 64)
                    sp.wait_ge(b_in, e * 16 + 32)
                    sp.wait_ge(items_done, end)
                    sp.dma_start(w1[:, u:u + 1], src1[:, bass.ds(e + 2, 1)]).then_inc(w_in, 16)
                    sp.dma_start(w2[:, u:u + 1], src2[:, bass.ds(e + 2, 1)]).then_inc(w_in, 16)
                    sp.dma_start(b1[:, u:u + 1, :], src_b[:, bass.ds(e + 2, 1), :].broadcast_to([128, 1, 2 * H])).then_inc(b_in, 16)
            sp.wait_ge(disp.all_in, 1)
            sp.dma_start(d["out"], k.sums[0:N]).then_inc(out_done, 16)
            sp.wait_ge(out_done, 16)

        @block.gpsimd
        def _(pool):
            router.gpsimd(pool)
            disp.gpsimd_constants(pool)
            disp.gpsimd_items(pool)

        @block.tensor
        def _(pe):
            norm.tensor(pe, lambda t: router.tensor_logits(pe, norm, t))
            disp.tensor_counts(pe, router.chosen[:])
            pe.wait_ge(disp.slots_ok, 1)
            router.tensor_shares(pe)
            pe.wait_ge(router.shareT_ok, router.turn + 1)
            pe.wait_ge(b2_in, 16)
            disp.tensor_list(pe)
            for t in range(NT):
                if t >= 2:
                    pe.wait_ge(bias_added, t - 1)
                nc.tensor.matmul(k.bank[0:P, 2 + t % 2, :], router.shareT[:, tile_cols(t)], b2[:],
                                 start=True, stop=True).then_inc(bias_ps, 1)
            pe.wait_ge(disp.rows_in, 16)
            tensor_transposed(k, 6, rows).then_inc(disp.rows_ps, 1)
            pe.wait_ge(bias_added, NT)

            def expert(e, u):
                first, end = disp.range(pe, e)
                pe.wait_ge(w_in, e * 32 + 32)
                pe.sem_inc(disp.seen, 1)
                with pe.Fori(first, end) as i:
                    pe.wait_ge(rowsT_ok, i + 1)
                    for b in range(2):
                        for part, done in ((0, gate_ps), (1, up_ps)):
                            for f in range(KD):
                                last = nc.tensor.matmul(k.bank[:, 2 * b + part, :], rowsT[:, f, :],
                                                        w1[:, u, f, part * H + b * 512:part * H + (b + 1) * 512],
                                                        start=(f == 0), stop=(f == KD - 1))
                            last.then_inc(done, 1)
                    pe.wait_ge(hid_ok, i * 2 + 1)
                    tensor_transposed(k, 4, hid[:, 0, :]).then_inc(hT_ps, 1)
                    pe.wait_ge(disp.rows_in, i * 16 + 32)
                    tensor_transposed(k, 6, rows).then_inc(disp.rows_ps, 1)
                    pe.wait_ge(hT_ok, i * 2 + 1)
                    pe.wait_ge(disp.out_ok, i + 1)
                    for f in range(KD):
                        nc.tensor.matmul(k.bank[:, 7, :], hT[:, f, :], w2[:, u, f, :], start=(f == 0), stop=False)
                        if f == KD - 2:
                            pe.wait_ge(hid_ok, i * 2 + 2)
                            tensor_transposed(k, 5, hid[:, 1, :]).then_inc(hT_ps, 1)
                    pe.wait_ge(hT_ok, i * 2 + 2)
                    for f in range(KD, FH):
                        last = nc.tensor.matmul(k.bank[:, 7, :], hT[:, f, :], w2[:, u, f, :], start=False,
                                                stop=(f == FH - 1))
                    last.then_inc(items_done, 1)

            with pe.Fori(0, E // 2) as h:
                for u in range(2):
                    expert(h * 2 + u, u)

        @block.scalar
        def _(act):
            norm.scalar(act)
            router.scalar_exp(act)
            router.scalar_shares(act)

            act.wait_ge(disp.rows_ps, 1)
            scalar_untransposed(k, 6, rowsT[:]).then_inc(rowsT_ok, 1)
            with act.Fori(0, E) as e:
                first, end = disp.range(act, e)
                with act.Fori(first, end) as i:
                    for b in range(2):
                        act.wait_ge(gate_ok, i * 2 + b + 1)
                        nc.scalar.activation(sig[:, b, :], gate[:, b, :], ACT.Sigmoid, scale=1.702).then_inc(sig_ok, 1)
                    act.wait_ge(hT_ps, i * 2 + 1)
                    scalar_untransposed(k, 4, hT[:, 0:KD, :]).then_inc(hT_ok, 1)
                    act.wait_ge(disp.rows_ps, i + 2)
                    scalar_untransposed(k, 6, rowsT[:]).then_inc(rowsT_ok, 1)
                    act.wait_ge(hT_ps, i * 2 + 2)
                    scalar_untransposed(k, 5, hT[:, KD:FH, :]).then_inc(hT_ok, 1)

        @block.vector
        def _(dve):
            norm.vector(dve)
            dve.wait_ge(disp.y_out, 16)
            router.vector(dve, disp.chosen_ok)
            disp.vector_slots(dve, router.chosen[:], router.share[:], router.earlier[:], router.above)
            disp.vector_list(dve)
            for t in range(NT):
                dve.wait_ge(bias_ps, t + 1)
                nc.vector.tensor_tensor(k.x[:, t, :], k.x[:, t, :], k.bank[0:P, 2 + t % 2, :], ALU.add).then_inc(bias_added, 1)

            def expert(e, u):
                first, end = disp.range(dve, e)
                dve.wait_ge(b_in, e * 16 + 16)
                dve.sem_inc(disp.seen, 1)
                with dve.Fori(first, end) as i:
                    for b in range(2):
                        dve.wait_ge(gate_ps, i * 2 + b + 1)
                        nc.vector.tensor_tensor(gate[:, b, :], k.bank[:, 2 * b, :], b1[:, u, b * 512:(b + 1) * 512],
                                                ALU.add).then_inc(gate_ok, 1)
                        dve.wait_ge(sig_ok, i * 2 + b + 1)
                        nc.vector.tensor_tensor(gate[:, b, :], gate[:, b, :], sig[:, b, :], ALU.mult)
                        dve.wait_ge(up_ps, i * 2 + b + 1)
                        nc.vector.scalar_tensor_tensor(out=hid[:, b, :], in0=k.bank[:, 2 * b + 1, :], scalar=1.0,
                                                       in1=b1[:, u, H + b * 512:H + (b + 1) * 512],
                                                       op0=ALU.add, op1=ALU.add)
                        dve.drain()
                        nc.vector.tensor_tensor(hid[:, b, :], hid[:, b, :], gate[:, b, :], ALU.mult).then_inc(hid_ok, 1)
                    disp.vector_result(dve, i, items_done)
                    dve.drain()

            with dve.Fori(0, E // 2) as h:
                for u in range(2):
                    expert(h * 2 + u, u)


def write_out(k):
    nc, d = k.nc, k.d
    out_done = k.sem("out_done")
    with ExitStack() as ctx:
        block = ctx.enter_context(nc.Block())

        @block.sync
        def _(sp):
            sp.dma_start(d["out"].rearrange("(t p) d -> p t d", p=P), k.x[:]).then_inc(out_done, 16)
            sp.wait_ge(out_done, 16)



def program(nc, dram, stop=8):
    k = Kernel(nc, dram)
    with k.ctx:
        k.x = k.sb("x", [P, NT, D])
        k.stats = k.sb("stats", [P, NT, 6])
        k.ident = k.sb("ident", [128, 128])
        k.degree = k.sb("degree", [P, NT, 2])
        k.inv_in, k.inv_out, k.has_in = (k.sb(n, [P, NT, 1]) for n in ("inv_in", "inv_out", "has_in"))
        k.adj_saved = nc.dram_tensor("adj_saved", (P, NT, N), F32, kind="Internal").ap()
        k.y_rows = nc.dram_tensor("y_rows", (N + SLOTS, D), F32, kind="Internal").ap()
        k.sums = nc.dram_tensor("sums", (N + SLOTS, D), F32, kind="Internal").ap()
        k.norms, k.routers = 0, 0
        k.norm_sems = [k.sem(n) for n in ("norm_var_ok", "norm_std_ok", "y_ok", "yT_ps", "yT_ok")]
        k.router_sems = [k.sem(n) for n in ("gate_in", "earlier_ok", "logit_ps", "shift_ok", "exp_ok", "share_ok",
                                            "shareT_ps", "shareT_ok")]
        k.graphs, k.graphs_own = 0, 0
        k.graph_sems = [k.sem("graph_" + n) for n in ("w_in", "adjT_ps", "adjT_ok", "z_ps", "z_ok", "own_ps", "own_ok",
                                                      "pre_ok", "sum_ps", "h_ok", "gate_ok", "done")]
        k.x_in, k.ident_ok, k.adj_in = k.sem("x_in"), k.sem("ident_ok"), k.sem("adj_in")
        k.y = k.sb("y", [P, NT, D])
        k.yT = k.sb("yT", [128, KD, N])
        adjacency = k.ctx.enter_context(ExitStack())
        k.adj = k.sb("adj", [P, NT, N], F32, adjacency)
        build_adjacency(k)
        k.bank = k.ps("bank", [128, 8, 512], k.ctx)
        layers = ExitStack()
        with layers:
            k.z = k.sb("z", [128, NT, D], F32, layers)
            k.adjT = k.sb("adjT", [P, NT, N], F32, layers)
            graph_layer(k, "l0_gnn", "sage")
            if stop > 1:
                k.layer(relu_layer, "l0_ffn")
            if stop > 2:
                graph_layer(k, "l1_gnn", "residual")
        if stop > 3:
            k.layer(balanced_layer, "l1_ffn")
        if stop > 4:
            k.layer(attention_layer, "l2_gnn")
        if stop > 5:
            k.layer(merged_layer, "l2_ffn")
        if stop > 6:
            with ExitStack() as sums:
                k.z = k.sb("z3", [128, NT, D], F32, sums)
                graph_layer(k, "l3_gnn", "sum")
        adjacency.close()
        if stop > 7:
            k.layer(top_two_layer, "l3_ffn")
        else:
            write_out(k)


INPUTS = ['x', 'src', 'dst', 'L0_gnn_W_l', 'L0_gnn_W_r', 'L0_gnn_b', 'L0_ffn_Wg', 'L0_ffn_bg', 'L0_ffn_W1', 'L0_ffn_W2',
          'L0_ffn_b2', 'L0_ffn_Ws1', 'L0_ffn_Ws2', 'L0_ffn_bs2', 'L1_gnn_alpha', 'L1_gnn_b', 'L1_ffn_gate_w',
          'L1_ffn_experts', 'L2_gnn_b_qkv', 'L2_gnn_b_ff', 'L2_ffn_gfc2_b', 'L2_ffn_b2', 'L2_ffn_ln_g', 'L2_ffn_ln_b', 'L2_ffn_tv_b2',
          'L2_ffn_tv_ln_g', 'L2_ffn_tv_ln_b', 'L3_gnn_wc', 'L3_gnn_wn', 'L3_gnn_bias', 'L3_ffn_router_w',
          'L3_ffn_router_b', 'L3_ffn_gate_up_proj', 'L3_ffn_gate_up_proj_bias', 'L3_ffn_down_proj', 'L3_ffn_down_proj_bias']


def laid_out(inputs):
    a = {n: np.ascontiguousarray(inputs[n]) for n in INPUTS}
    for n in ('L1_gnn_W', 'L2_gnn_W_qkv', 'L2_gnn_W_ff', 'L2_ffn_gfc1_w', 'L2_ffn_gfc2_w', 'L2_ffn_W1', 'L2_ffn_W2'):
        a[n + "_T"] = np.ascontiguousarray(np.asarray(inputs[n]).T)
    for n in ('L2_ffn_tv_W1', 'L2_ffn_tv_W2'):
        a[n + "_T"] = np.ascontiguousarray(np.asarray(inputs[n]).transpose(0, 2, 1))
    for n in ('L0_ffn_b1', 'L0_ffn_bs1', 'L2_gnn_b_qkv', 'L2_ffn_gfc1_b', 'L2_ffn_b1', 'L2_ffn_tv_b1'):
        b = np.asarray(inputs[n])
        rows = b.reshape(-1, b.shape[-1] // 128, 128)
        a[n + "_P"] = np.ascontiguousarray(rows.transpose(2, 0, 1))
    return {n: v.reshape(1) if v.ndim == 0 else v for n, v in a.items()}


def kernel(**inputs):
    import concourse.bacc as bacc
    from concourse.bass_utils import run_bass_kernel_spmd

    nc = bacc.Bacc("TRN2", target_bir_lowering=False, num_devices=1)
    arrays = laid_out(inputs)
    dram = {n: nc.dram_tensor(f"in_{n}", v.shape, mybir.dt.from_np(v.dtype), kind="ExternalInput").ap()
            for n, v in arrays.items()}
    dram["out"] = nc.dram_tensor("result", (N, D), F32, kind="ExternalOutput").ap()
    program(nc, dram)
    r = run_bass_kernel_spmd(nc, [{f"in_{n}": v for n, v in arrays.items()}], core_ids=[0])
    return r.results[0]["result"]
```
